# Optimizing a Trainium2 kernel written in Bass

```python
import numpy as np
import jax
import jax.numpy as jnp

def _softmax(x, axis=-1):
    return jax.nn.softmax(x, axis=axis)

def _gelu(x):
    return jax.nn.gelu(x, approximate=True)

def _silu(x):
    return jax.nn.silu(x)

def _sigmoid(x):
    return jax.nn.sigmoid(x)

def _layernorm(x, axis=-1, eps=1e-05):
    m = jnp.mean(x, axis=axis, keepdims=True)
    v = jnp.var(x, axis=axis, keepdims=True)
    return (x - m) / jnp.sqrt(v + eps)

def _scatter_add(tgt, idx, src, axis=0):
    return tgt.at[idx].add(src)

def _segment_sum(src, seg, n):
    return jax.ops.segment_sum(src, seg, n)
kernel_name = 'mk_flamingo_gated_d2_seqx_r8_4687a1'

def setup_inputs(seed: int=0):
    np.random.seed(seed)
    _w = jnp.asarray

    def _rec_inputs():
        import jax
        import jax.numpy as jnp
        _rk = jax.random.key(seed)
        x = -0.0002928 + 1 * jax.random.normal(jax.random.fold_in(_rk, 1), (4, 256, 128), jnp.float32)
        _lenS = 256 - jax.random.randint(jax.random.fold_in(_rk, 7), (4,), 0, max(1, 256 // 4) + 1, jnp.int32)
        _lenS2 = 512 - jax.random.randint(jax.random.fold_in(_rk, 8), (4,), 0, max(1, 512 // 4) + 1, jnp.int32)
        _ctx_1024P = jax.random.normal(jax.random.fold_in(_rk, 11), (4, 16, 128), jnp.float32)
        _ctx_1024c = jax.random.dirichlet(jax.random.fold_in(_rk, 511), 0.3 * jnp.ones((16,), jnp.float32), (4, 512))
        _ctx_1024t = jnp.einsum('bsk,bkd->bsd', _ctx_1024c, _ctx_1024P)
        _ctx_1024t = _ctx_1024t * jax.lax.rsqrt(jnp.mean(jnp.square(_ctx_1024t)) + 1e-12) * 0.953939
        ctx_1024 = -1.39393e-06 + 0.999914 * (_ctx_1024t + 0.3 * jax.random.normal(jax.random.fold_in(_rk, 611), (4, 512, 128), jnp.float32))
        _g = jax.random.normal(jax.random.fold_in(_rk, 9001), (2, 2), jnp.float32)
        _g = jnp.sign(_g) * jnp.maximum(jnp.abs(_g), 1.0) + (_g == 0) * 1.0
        g_xattn = _g[0]
        g_ffn = _g[1]
        return (x, ctx_1024, g_xattn, g_ffn)
    x, ctx_1024, g_xattn, g_ffn = _rec_inputs()

    def _L0_xattn_setup():
        import jax, jax.numpy as jnp
        import numpy as np
        DIM = 128
        H = 16
        D = DIM // H
        SCALE = D ** (-0.5)
        LN_EPS = 1e-05

        def _layernorm(t, gamma, beta):
            mu = jnp.mean(t, axis=-1, keepdims=True)
            var = jnp.var(t, axis=-1, keepdims=True)
            return (t - mu) * jax.lax.rsqrt(var + LN_EPS) * gamma + beta
        key = jax.random.key(seed)
        ks = jax.random.split(key, 8)
        s = DIM ** (-0.5)
        return {'x': jax.random.normal(ks[0], (2, 256, DIM), dtype=jnp.float32), 'y': jax.random.normal(ks[1], (2, 256, DIM), dtype=jnp.float32), 'Wq': jax.random.normal(ks[2], (DIM, DIM), dtype=jnp.float32) * s, 'bq': jnp.zeros((DIM,), dtype=jnp.float32), 'Wkv': jax.random.normal(ks[3], (2 * DIM, DIM), dtype=jnp.float32) * s, 'bkv': jnp.zeros((2 * DIM,), dtype=jnp.float32), 'q_gamma': jnp.ones((D,), dtype=jnp.float32), 'q_beta': jnp.zeros((D,), dtype=jnp.float32), 'k_gamma': jnp.ones((D,), dtype=jnp.float32), 'k_beta': jnp.zeros((D,), dtype=jnp.float32), 'Wproj': jax.random.normal(ks[4], (DIM, DIM), dtype=jnp.float32) * s, 'bproj': jnp.zeros((DIM,), dtype=jnp.float32)}
    _L0_xattn_all = _L0_xattn_setup()
    _L0_xattn_in = {k: v for k, v in _L0_xattn_all.items() if k in ('Wq', 'bq', 'Wkv', 'bkv', 'q_gamma', 'q_beta', 'k_gamma', 'k_beta', 'Wproj', 'bproj')}
    del _L0_xattn_all

    def _L0_ffn_setup():
        import jax, jax.numpy as jnp
        import numpy as np
        E = 8
        TOPK = 2
        SCALE = 2.0
        key = jax.random.key(seed)
        ks = jax.random.split(key, 12)
        B, S, D, F, R = (2, 64, 128, 512, 16)
        w = lambda k, shp: jax.random.normal(k, shp, dtype=jnp.float32) * 0.02
        return {'hidden_states': jax.random.normal(ks[0], (B, S, D), dtype=jnp.float32), 'gate_w': w(ks[1], (E, D)), 'w_gate': w(ks[2], (F, D)), 'w_up': w(ks[3], (F, D)), 'w_down': w(ks[4], (D, F)), 'A1': w(ks[5], (E, R, D)), 'B1': w(ks[6], (E, F, R)), 'A3': w(ks[7], (E, R, D)), 'B3': w(ks[8], (E, F, R)), 'A2': w(ks[9], (E, R, F)), 'B2': w(ks[10], (E, D, R))}
    _L0_ffn_all = _L0_ffn_setup()
    _L0_ffn_in = {k: v for k, v in _L0_ffn_all.items() if k in ('gate_w', 'w_gate', 'w_up', 'w_down', 'A1', 'B1', 'A3', 'B3', 'A2', 'B2')}
    del _L0_ffn_all

    def _L1_xattn_setup():
        import jax, jax.numpy as jnp
        import numpy as np
        EPS = 1e-05

        def layer_norm(x, g, b):
            mu = jnp.mean(x, axis=-1, keepdims=True)
            var = jnp.var(x, axis=-1, keepdims=True)
            return (x - mu) * jax.lax.rsqrt(var + EPS) * g + b
        key = jax.random.key(seed)
        ks = jax.random.split(key, 8)
        dim, heads, dim_head = (128, 16, 64)
        inner = heads * dim_head
        b, n, m = (8, 512, 64)
        s = dim ** (-0.5)
        return {'x': jax.random.normal(ks[0], (b, n, dim), jnp.float32), 'latents': jax.random.normal(ks[1], (b, m, dim), jnp.float32), 'ln_m_g': jnp.ones((dim,), jnp.float32), 'ln_m_b': jnp.zeros((dim,), jnp.float32), 'ln_l_g': jnp.ones((dim,), jnp.float32), 'ln_l_b': jnp.zeros((dim,), jnp.float32), 'Wq': jax.random.normal(ks[2], (dim, inner), jnp.float32) * s, 'Wkv': jax.random.normal(ks[3], (dim, 2 * inner), jnp.float32) * s, 'Wout': jax.random.normal(ks[4], (inner, dim), jnp.float32) * s}
    _L1_xattn_all = _L1_xattn_setup()
    _L1_xattn_in = {k: v for k, v in _L1_xattn_all.items() if k in ('ln_m_g', 'ln_m_b', 'ln_l_g', 'ln_l_b', 'Wq', 'Wkv', 'Wout')}
    del _L1_xattn_all

    def _L1_ffn_setup():
        import jax, jax.numpy as jnp
        import numpy as np
        D_MODEL, FFN, N_EXP = (128, 512, 8)
        BS, L = (4, 256)
        key = jax.random.key(seed)
        ks = jax.random.split(key, 7)
        s = 0.02
        return {'x': jax.random.normal(ks[0], (BS, L, D_MODEL), dtype=jnp.float32), 'gate_w': s * jax.random.normal(ks[1], (D_MODEL, N_EXP), dtype=jnp.float32), 'gate_b': jnp.zeros((N_EXP,), dtype=jnp.float32), 'W1': s * jax.random.normal(ks[2], (N_EXP, D_MODEL, FFN), dtype=jnp.float32), 'b1': jnp.zeros((N_EXP, FFN), dtype=jnp.float32), 'W2': s * jax.random.normal(ks[3], (N_EXP, FFN, D_MODEL), dtype=jnp.float32), 'b2': jnp.zeros((N_EXP, D_MODEL), dtype=jnp.float32)}
    _L1_ffn_all = _L1_ffn_setup()
    _L1_ffn_in = {k: v for k, v in _L1_ffn_all.items() if k in ('gate_w', 'gate_b', 'W1', 'b1', 'W2', 'b2')}
    del _L1_ffn_all
    return {'x': x, 'ctx_1024': ctx_1024, 'g_xattn': g_xattn, 'g_ffn': g_ffn, 'L0_xattn_Wq': _L0_xattn_in['Wq'], 'L0_xattn_bq': _L0_xattn_in['bq'], 'L0_xattn_Wkv': _L0_xattn_in['Wkv'], 'L0_xattn_bkv': _L0_xattn_in['bkv'], 'L0_xattn_q_gamma': _L0_xattn_in['q_gamma'], 'L0_xattn_q_beta': _L0_xattn_in['q_beta'], 'L0_xattn_k_gamma': _L0_xattn_in['k_gamma'], 'L0_xattn_k_beta': _L0_xattn_in['k_beta'], 'L0_xattn_Wproj': _L0_xattn_in['Wproj'], 'L0_xattn_bproj': _L0_xattn_in['bproj'], 'L0_ffn_gate_w': _L0_ffn_in['gate_w'], 'L0_ffn_w_gate': _L0_ffn_in['w_gate'], 'L0_ffn_w_up': _L0_ffn_in['w_up'], 'L0_ffn_w_down': _L0_ffn_in['w_down'], 'L0_ffn_A1': _L0_ffn_in['A1'], 'L0_ffn_B1': _L0_ffn_in['B1'], 'L0_ffn_A3': _L0_ffn_in['A3'], 'L0_ffn_B3': _L0_ffn_in['B3'], 'L0_ffn_A2': _L0_ffn_in['A2'], 'L0_ffn_B2': _L0_ffn_in['B2'], 'L1_xattn_ln_m_g': _L1_xattn_in['ln_m_g'], 'L1_xattn_ln_m_b': _L1_xattn_in['ln_m_b'], 'L1_xattn_ln_l_g': _L1_xattn_in['ln_l_g'], 'L1_xattn_ln_l_b': _L1_xattn_in['ln_l_b'], 'L1_xattn_Wq': _L1_xattn_in['Wq'], 'L1_xattn_Wkv': _L1_xattn_in['Wkv'], 'L1_xattn_Wout': _L1_xattn_in['Wout'], 'L1_ffn_gate_w': _L1_ffn_in['gate_w'], 'L1_ffn_gate_b': _L1_ffn_in['gate_b'], 'L1_ffn_W1': _L1_ffn_in['W1'], 'L1_ffn_b1': _L1_ffn_in['b1'], 'L1_ffn_W2': _L1_ffn_in['W2'], 'L1_ffn_b2': _L1_ffn_in['b2']}

def reference(x, ctx_1024, g_xattn, g_ffn, L0_xattn_Wq, L0_xattn_bq, L0_xattn_Wkv, L0_xattn_bkv, L0_xattn_q_gamma, L0_xattn_q_beta, L0_xattn_k_gamma, L0_xattn_k_beta, L0_xattn_Wproj, L0_xattn_bproj, L0_ffn_gate_w, L0_ffn_w_gate, L0_ffn_w_up, L0_ffn_w_down, L0_ffn_A1, L0_ffn_B1, L0_ffn_A3, L0_ffn_B3, L0_ffn_A2, L0_ffn_B2, L1_xattn_ln_m_g, L1_xattn_ln_m_b, L1_xattn_ln_l_g, L1_xattn_ln_l_b, L1_xattn_Wq, L1_xattn_Wkv, L1_xattn_Wout, L1_ffn_gate_w, L1_ffn_gate_b, L1_ffn_W1, L1_ffn_b1, L1_ffn_W2, L1_ffn_b2):
    import jax
    import jax.numpy as jnp

    def _L0_xattn_ref(x, y, Wq, bq, Wkv, bkv, q_gamma, q_beta, k_gamma, k_beta, Wproj, bproj):
        import jax, jax.numpy as jnp
        import numpy as np
        DIM = 128
        H = 16
        D = DIM // H
        SCALE = D ** (-0.5)
        LN_EPS = 1e-05

        def _layernorm(t, gamma, beta):
            mu = jnp.mean(t, axis=-1, keepdims=True)
            var = jnp.var(t, axis=-1, keepdims=True)
            return (t - mu) * jax.lax.rsqrt(var + LN_EPS) * gamma + beta
        B, N, C = x.shape
        M = y.shape[1]
        q = (x @ Wq.T + bq).reshape(B, N, H, D).transpose(0, 2, 1, 3)
        kv = (y @ Wkv.T + bkv).reshape(B, M, 2, H, D).transpose(2, 0, 3, 1, 4)
        k, v = (kv[0], kv[1])
        q = _layernorm(q, q_gamma, q_beta) * SCALE
        k = _layernorm(k, k_gamma, k_beta)
        attn = jax.nn.softmax(jnp.einsum('bhnd,bhmd->bhnm', q, k), axis=-1)
        out = jnp.einsum('bhnm,bhmd->bhnd', attn, v)
        out = out.transpose(0, 2, 1, 3).reshape(B, N, C)
        return out @ Wproj.T + bproj

    def _L0_ffn_ref(hidden_states, gate_w, w_gate, w_up, w_down, A1, B1, A3, B3, A2, B2):
        import jax, jax.numpy as jnp
        import numpy as np
        E = 8
        TOPK = 2
        SCALE = 2.0
        B, S, D = hidden_states.shape
        x = hidden_states.reshape(-1, D)
        N = x.shape[0]
        probs = jax.nn.softmax(x @ gate_w.T, axis=-1)
        vals, idx = jax.lax.top_k(probs, TOPK)
        rw = vals / jnp.sum(vals, axis=-1, keepdims=True)
        weight = jnp.zeros((N, E), x.dtype).at[jnp.arange(N)[:, None], idx].add(rw)
        common_w1 = x @ w_gate.T
        common_w3 = x @ w_up.T
        d1 = jnp.einsum('enr,efr->enf', jnp.einsum('nd,erd->enr', x, A1), B1) * SCALE
        d3 = jnp.einsum('enr,efr->enf', jnp.einsum('nd,erd->enr', x, A3), B3) * SCALE
        act = jax.nn.silu(common_w1[None] + d1) * (common_w3[None] + d3)
        out = jnp.einsum('ne,enf->nf', weight, act) @ w_down.T
        z = jnp.einsum('enf,erf->enr', act, A2)
        out = out + jnp.einsum('ne,enr,edr->nd', weight, z, B2) * SCALE
        return out.reshape(B, S, D)

    def _L1_xattn_ref(x, latents, ln_m_g, ln_m_b, ln_l_g, ln_l_b, Wq, Wkv, Wout):
        import jax, jax.numpy as jnp
        import numpy as np
        EPS = 1e-05

        def layer_norm(x, g, b):
            mu = jnp.mean(x, axis=-1, keepdims=True)
            var = jnp.var(x, axis=-1, keepdims=True)
            return (x - mu) * jax.lax.rsqrt(var + EPS) * g + b
        heads, dim_head = (16, 64)
        scale = dim_head ** (-0.5)
        x = layer_norm(x, ln_m_g, ln_m_b)
        lat = layer_norm(latents, ln_l_g, ln_l_b)
        b, m, _ = lat.shape
        q = lat @ Wq
        kv_input = jnp.concatenate([x, lat], axis=1)
        kv = kv_input @ Wkv
        k, v = jnp.split(kv, 2, axis=-1)

        def split_heads(t):
            return t.reshape(t.shape[0], t.shape[1], heads, dim_head).transpose(0, 2, 1, 3)
        q, k, v = (split_heads(q), split_heads(k), split_heads(v))
        dots = jnp.einsum('bhid,bhjd->bhij', q, k) * scale
        attn = jax.nn.softmax(dots, axis=-1)
        out = jnp.einsum('bhij,bhjd->bhid', attn, v)
        out = out.transpose(0, 2, 1, 3).reshape(b, m, heads * dim_head)
        return out @ Wout

    def _L1_ffn_ref(x, gate_w, gate_b, W1, b1, W2, b2):
        import jax, jax.numpy as jnp
        import numpy as np
        D_MODEL, FFN, N_EXP = (128, 512, 8)
        BS, L = (4, 256)
        logits = jnp.einsum('bld,de->ble', x, gate_w) + gate_b
        probs = jax.nn.softmax(logits, axis=1)
        idx = jnp.argmax(probs, axis=-1)
        out = jnp.zeros_like(x)
        for e in range(N_EXP):
            h = jax.nn.gelu(jnp.einsum('bld,df->blf', x, W1[e]) + b1[e], approximate=False)
            y = jnp.einsum('blf,fd->bld', h, W2[e]) + b2[e]
            out = out + jnp.where((idx == e)[..., None], y, jnp.float32(0.0))
        return out
    x = x + jnp.tanh(g_xattn[0]) * _L0_xattn_ref(_layernorm(x, axis=-1), ctx_1024, L0_xattn_Wq, L0_xattn_bq, L0_xattn_Wkv, L0_xattn_bkv, L0_xattn_q_gamma, L0_xattn_q_beta, L0_xattn_k_gamma, L0_xattn_k_beta, L0_xattn_Wproj, L0_xattn_bproj)
    x = x + jnp.tanh(g_ffn[0]) * _L0_ffn_ref(_layernorm(x, axis=-1), L0_ffn_gate_w, L0_ffn_w_gate, L0_ffn_w_up, L0_ffn_w_down, L0_ffn_A1, L0_ffn_B1, L0_ffn_A3, L0_ffn_B3, L0_ffn_A2, L0_ffn_B2)
    x = x + jnp.tanh(g_xattn[1]) * _L1_xattn_ref(ctx_1024, _layernorm(x, axis=-1), L1_xattn_ln_m_g, L1_xattn_ln_m_b, L1_xattn_ln_l_g, L1_xattn_ln_l_b, L1_xattn_Wq, L1_xattn_Wkv, L1_xattn_Wout)
    x = x + jnp.tanh(g_ffn[1]) * _L1_ffn_ref(_layernorm(x, axis=-1), L1_ffn_gate_w, L1_ffn_gate_b, L1_ffn_W1, L1_ffn_b1, L1_ffn_W2, L1_ffn_b2)
    return x

_drawn_inputs = setup_inputs


def setup_inputs(seed=0):
    import zlib

    import numpy as np

    out = dict(_drawn_inputs(seed))
    spreads = {'g_ffn': (-1.0, 0.6),
     'L0_xattn_bq': (0.0, 0.435),
     'L0_xattn_bkv': (0.0, 0.1),
     'L0_xattn_q_gamma': (1.0, 0.597),
     'L0_xattn_q_beta': (0.0, 0.592),
     'L0_xattn_k_gamma': (1.0, 0.6),
     'L0_xattn_k_beta': (0.0, 2.0),
     'L0_xattn_bproj': (0.0, 0.1),
     'L1_xattn_ln_m_g': (1.0, 0.6),
     'L1_xattn_ln_m_b': (0.0, 0.76),
     'L1_xattn_ln_l_g': (1.0, 0.6),
     'L1_xattn_ln_l_b': (0.0, 0.8),
     'L1_ffn_gate_b': (0.0, 0.1),
     'L1_ffn_b1': (0.0, 2.0),
     'L1_ffn_b2': (0.0, 0.8)}
    factors = {'L0_ffn_gate_w': 8.0,
     'L0_ffn_w_gate': 6.166,
     'L0_ffn_w_up': 5.91,
     'L0_ffn_w_down': 5.843,
     'L0_ffn_A1': 8.0,
     'L0_ffn_B1': 8.0,
     'L0_ffn_A3': 8.0,
     'L0_ffn_B3': 8.0,
     'L0_ffn_A2': 8.0,
     'L0_ffn_B2': 8.0,
     'L1_ffn_gate_w': 4.699,
     'L1_ffn_W1': 8.0,
     'L1_ffn_W2': 5.125}
    for name, (base, spread) in spreads.items():
        noise = np.random.default_rng([zlib.crc32(name.encode()), seed]).standard_normal(out[name].shape)
        drawn = base * np.exp(spread * noise) if base else spread * noise
        out[name] = jnp.asarray(drawn.astype(out[name].dtype))
    for name, factor in factors.items():
        out[name] = (out[name] * factor).astype(out[name].dtype)
    return out
```

```python
from contextlib import ExitStack

import concourse.bass as bass
from concourse import mybir

F32 = mybir.dt.float32
F32R = mybir.dt.float32r
BF16 = mybir.dt.bfloat16
I32 = mybir.dt.int32
U32 = mybir.dt.uint32
ALU = mybir.AluOpType
ACT = mybir.ActivationFunctionType
AX = mybir.AxisListType.X

P = 128
BANK = 512
EPS = 1e-5
RSQRT_MAGIC = 0x5F3759DF


class Signal:

    def __init__(self, sem, per_batch, before=0):
        self.sem, self.per_batch, self.before = sem, per_batch, before

    def after(self, b, k):
        return b * self.per_batch + (self.before + k)


def flamingo(nc, t_in, out):
    x_d, ctx_d = t_in["x"], t_in["ctx_1024"]
    B, NQ, D = x_d.shape
    NC_ = ctx_d.shape[1]
    TQ, TC = NQ // P, NC_ // P
    TK = TC + TQ
    NK = NC_ + NQ
    H = 16
    D0 = D // H
    D1 = t_in["L1_xattn_Wq"].shape[1] // H
    E, R = t_in["L0_ffn_A1"].shape[:2]
    F = t_in["L0_ffn_w_gate"].shape[0]
    FC = F // P
    SCALE0 = float(D0) ** -0.5
    SCALE1 = float(D1) ** -0.5
    LORA_SCALE = 2.0
    NPART = 3
    SR = NPART * NPART * D0
    SK = 96
    G0 = (TC + TQ) * H
    NPAIR = H // 2
    QUAD = 4
    NQUAD = H // QUAD
    V0W = D0 + 1
    V0C = H * V0W + 32 - V0W
    PR0, PR1 = 6, 3
    assert D == P and E * R == P and NQ == 256 and NC_ == 512 and D1 == 64 and SR <= SK

    with ExitStack() as ctx:
        def sb(name, shape, dt=F32):
            return ctx.enter_context(nc.sbuf_tensor(name, shape, dt))

        signals = {}

        def signal(name, per_batch=0, before=0):
            s = Signal(ctx.enter_context(nc.semaphore(name)), per_batch, before)
            signals[name] = s
            return s

        ident = sb("ident", [P, P])
        identb = sb("identb", [P, P], BF16)
        negidentb = sb("negidentb", [P, P], BF16)
        onesb = sb("onesb", [P, P], BF16)
        onesf = sb("onesf", [P, D1])
        iota_er = sb("iota_er", [P, E, R])
        iota_col = sb("iota_col", [P, P])
        iota_ed = sb("iota_ed", [P, E, P], BF16)
        NT = 31
        wt = sb("wt", [P, NT, P])
        W_Q0, W_K0, W_V0, W_PROJ, W_GATE, W_UP, W_B1, W_B3, W_DOWN, W_A1, W_A3, W_B2 = (
            0, 1, 2, 3, 4, 8, 12, 16, 20, 28, 29, 30)
        gate0 = sb("gate0", [P, E])
        wkv_h = sb("wkv_h", [P, 2, NPAIR, P], F32R)
        wkv_l = sb("wkv_l", [P, 2, NPAIR, P], F32R)
        wq_h = sb("wq_h", [P, H, 2, D1], F32R)
        wq_l = sb("wq_l", [P, H, 2, D1], F32R)
        wout = sb("wout", [P, NPAIR, P])
        w1 = sb("w1", [P, E, F])
        b1 = sb("b1", [P, F])
        b2 = sb("b2", [P, P])
        gate1 = sb("gate1", [P, E])
        gate1_b = sb("gate1_b", [E, 1])
        bq0 = sb("bq0", [P, P])
        bkv0 = sb("bkv0", [P, 2, P])
        bproj0 = sb("bproj0", [P, P])
        qg0, qb0, kg0, kb0 = (sb(n, [P, D0]) for n in ("qg0", "qb0", "kg0", "kb0"))
        lnm_g, lnm_b, lnl_g, lnl_b = (sb(n, [P, P]) for n in ("lnm_g", "lnm_b", "lnl_g", "lnl_b"))
        gates_raw = sb("gates_raw", [P, 4])
        gates = sb("gates", [P, 4])
        G_X0, G_X1, G_F0, G_F1 = (gates[:, i:i + 1] for i in range(4))

        x_in = sb("x_in", [P, TQ, P])
        ctx_in = sb("ctx_in", [P, TC, P])
        xr = sb("xr", [P, TQ, P])
        xn = sb("xn", [P, TQ, P])
        xT = sb("xT", [P, NQ])
        kv_h = sb("kv_h", [P, NK], F32R)
        kv_l = sb("kv_l", [P, NK], F32R)
        v0 = sb("v0", [P, TC, V0C])
        keys = sb("keys", [P, H, NK], F32R)
        q_h = sb("q_h", [P, 2, 2, NQ], F32R)
        q_l = sb("q_l", [P, 2, 2, NQ], F32R)
        area_o = sb("area_o", [P, NPAIR * NQ])
        area_v = sb("area_v", [P, TK * H * D1])
        area_p = sb("area_p", [P, 6144])
        stats = sb("stats", [P, TC, 6])
        moments = sb("moments", [P, TC, 2])
        rs_small = tuple(sb(n, [P, TC]) for n in ("rs_v", "rs_y", "rs_t"))
        rowmax = sb("rowmax", [P, 2, TQ])
        diag = sb("diag", [P, 2, TQ, P], BF16)
        rden0 = sb("rden0", [P, TQ, H])
        lg = sb("lg", [P, TQ, E])
        top = sb("top", [P, TQ, 8])
        topi = sb("topi", [P, TQ, 8], U32)
        topf = sb("topf", [P, TQ, 8])
        wsel = sb("wsel", [P, 4, TQ])
        mask = sb("mask", [P, TQ, E])
        sm = sb("sm", [E, 4])
        scratch = sb("scratch", [P, 1])

        o0 = area_o[:, 0:NQUAD * NQ].rearrange("p (g q) -> p g q", g=NQUAD)
        o0_tok = area_o[:, 1024:1280].rearrange("p (t d) -> p t d", t=TQ)
        o0_T = area_o[:, 1280:1536]
        cn = area_o[:, 1024:1536].rearrange("p (t d) -> p t d", t=TC)
        ctxT = area_o[:, 1536:2048]
        o1 = area_o[:, :].rearrange("p (h q) -> p h q", h=NPAIR)
        qk = area_v[:, 0:768].rearrange("p (g d) -> p g d", d=D0)
        qk2 = area_v[:, 768:1536].rearrange("p (g d) -> p g d", d=D0)
        parts = area_v[:, 1536:2688].bitcast(BF16).rearrange("p (g s d) -> p g s d", s=NPART, d=D0)
        rs_wide = tuple(area_v[:, n:n + G0] for n in range(2688, 2688 + 3 * G0, G0))
        hsum = area_v[:, 2688 + 3 * G0:2688 + 4 * G0]
        kq = area_v[:, :].bitcast(BF16).rearrange("p (h n) -> p h n", h=H)
        v1 = area_v[:, :].rearrange("p (t n) -> p t n", t=TK)
        w2 = area_v[:, 0:FC * E * P].rearrange("p (c n) -> p c n", c=FC)
        stack = area_p[:, 0:G0 * SK // 2].bitcast(BF16).rearrange("p (g r) -> p g r", r=SK)
        p0 = area_p[:, 0:PR0 * TC * NQ].rearrange("p (s k q) -> p s k q", s=PR0, q=NQ)
        p1 = area_p[:, 0:PR1 * TK * NQ].rearrange("p (s n) -> p s n", s=PR1)
        psum_a = area_p[:, 4608:5376]
        psum_1 = area_p[:, 5376:5888].rearrange("p (s q) -> p s q", s=2)
        exm = area_p[:, 0:512].rearrange("p (j t n) -> p j t n", j=2, t=TQ)
        exmT = area_p[:, 512:1024].rearrange("p (j q) -> p j q", j=2)
        um = area_p[:, 1024:2048].rearrange("p (u j q) -> p u j q", u=2, j=2)
        hid0 = area_p[:, 2048:4096].rearrange("p (j c q) -> p j c q", j=2, c=FC)
        sg = area_p[:, 4096:5120].rearrange("p (s n) -> p s n", s=2)
        zm = area_p[:, 5120:5632].rearrange("p (j t n) -> p j t n", j=2, t=TQ)
        zT = area_p[:, 5632:5888]
        dsum = area_p[:, 5888:6144].rearrange("p (t n) -> p t n", t=TQ)
        xm = area_p[:, 0:2048].rearrange("p (e q) -> p e q", e=E)
        hid1 = area_p[:, 2048:3072].rearrange("p (c q) -> p c q", c=FC)
        maskb = area_p[:, 3072:4096].bitcast(BF16).rearrange("p (t e d) -> p t e d", t=TQ, e=E)
        sel = area_p[:, 4096:5120].rearrange("p (e d) -> p e d", e=E)
        maskp = area_p[:, 5120:5376].rearrange("p (t n) -> p t n", t=TQ)
        maskT = area_p[:, 5376:5632]
        probT = area_p[:, 5632:5888]
        ysum = area_p[:, 5888:6144].rearrange("p (t n) -> p t n", t=TQ)
        yT = area_p[:, 0:256]
        raw = area_v[:, 0:NT * P].rearrange("p (n d) -> p n d", n=NT)
        raw_kv = area_p[:, 0:2048].rearrange("p (a n d) -> p a n d", a=2, d=P)
        gate0_raw = area_p[0:E, 3072:3072 + P]
        raw_q = area_p[:, 2048:3072].rearrange("p (h d) -> p h d", h=H)

        ps = ctx.enter_context(nc.psum_tensor("ps", [P, 8 * BANK], F32))

        def bank(i, n=1):
            return ps[:, i * BANK:(i + n) * BANK]

        s_raw = signal("s_raw")
        s_rawkv = signal("s_rawkv")
        s_small = signal("s_small")
        s_zero = signal("s_zero")
        s_const = signal("s_const")
        s_wT = signal("s_wT")
        s_wT_copied = signal("s_wT_copied")
        s_whigh = signal("s_whigh")
        s_ready = signal("s_ready")
        s_x = signal("s_x", 16)
        s_ctx = signal("s_ctx", 16)
        s_w2 = signal("s_w2", 16 * FC)
        s_out = signal("s_out", 16, before=1)
        e_xT = signal("e_xT", 4)
        e_ctxT = signal("e_ctxT", 1)
        e_cnT = signal("e_cnT", 1)
        e_qkv0 = signal("e_qkv0", 1)
        e_k = signal("e_k", NPAIR)
        e_kq = signal("e_kq", H)
        e_max0 = signal("e_max0", H)
        e_st0 = signal("e_st0", H)
        e_pv0 = signal("e_pv0", NQUAD)
        e_o0 = signal("e_o0", 3)
        e_route0 = signal("e_route0", 3)
        e_pre0 = signal("e_pre0", 4)
        e_down0 = signal("e_down0", 2)
        e_z = signal("e_z", 2)
        e_v = signal("e_v", TK)
        e_klat = signal("e_klat", 4)
        e_q = signal("e_q", NPAIR)
        e_max1 = signal("e_max1", H)
        e_st1 = signal("e_st1", H)
        e_pv1 = signal("e_pv1", NPAIR)
        e_den1 = signal("e_den1", NPAIR)
        e_y1 = signal("e_y1", 2)
        e_route1 = signal("e_route1", 5)
        e_pre1 = signal("e_pre1", 2)
        e_out1 = signal("e_out1", 2)
        a_xT = signal("a_xT", 3)
        a_ctxT = signal("a_ctxT", 1)
        a_cH = signal("a_cH", 1)
        a_kH = signal("a_kH", NPAIR)
        a_kq = signal("a_kq", H // 2)
        a_exp0 = signal("a_exp0", H)
        a_o0 = signal("a_o0", NQUAD)
        a_oT = signal("a_oT", 1)
        a_ratio = signal("a_ratio", 1)
        a_silu = signal("a_silu", 4)
        a_zT = signal("a_zT", 1)
        a_v = signal("a_v", TK)
        a_latH = signal("a_latH", 1)
        a_klat = signal("a_klat", 4)
        a_qH = signal("a_qH", NPAIR)
        a_exp1 = signal("a_exp1", H)
        a_yT = signal("a_yT", 1)
        a_sm = signal("a_sm", 1)
        a_maskT = signal("a_maskT", 1)
        a_gelu = signal("a_gelu", 2)
        d_xn = signal("d_xn", 4)
        d_cn = signal("d_cn", 1)
        d_cL = signal("d_cL", 1)
        d_qkv0 = signal("d_qkv0", 1)
        d_stack = signal("d_stack", 1)
        d_kL = signal("d_kL", NPAIR)
        d_kq = signal("d_kq", H // 2)
        d_max0 = signal("d_max0", H)
        d_diag0 = signal("d_diag0", H)
        d_o0 = signal("d_o0", 1)
        d_x = signal("d_x", 4, before=1)
        d_gap = signal("d_gap", 1)
        d_exm = signal("d_exm", 1)
        d_um = signal("d_um", 1)
        d_hid0 = signal("d_hid0", 4)
        d_zm = signal("d_zm", 1)
        d_latL = signal("d_latL", 1)
        d_klat = signal("d_klat", 4)
        d_qL = signal("d_qL", NPAIR)
        d_max1 = signal("d_max1", H)
        d_diag1 = signal("d_diag1", H)
        d_o1 = signal("d_o1", NPAIR)
        d_smax = signal("d_smax", 1)
        d_prob = signal("d_prob", 1)
        d_mask = signal("d_mask", 1)
        d_xm = signal("d_xm", 2)
        g_cn = signal("g_cn", 1)
        g_pad = signal("g_pad", 1)
        g_sum = signal("g_sum", H, before=1)
        DVE_STEPS = 225
        d_step = signal("d_step", DVE_STEPS)
        g_step = signal("g_step", 1 + 2 * H)

        x_v = x_d.rearrange("b (t p) d -> b p t d", p=P)
        ctx_v = ctx_d.rearrange("b (t p) d -> b p t d", p=P)
        out_v = out.rearrange("b (t p) d -> b p t d", p=P)

        def row(a, n):
            return a.rearrange("(o n) -> o n", o=1).to_broadcast([P, n])

        block = ctx.enter_context(nc.Block())

        @block.sync
        def _(sp):
            W = t_in
            raw_loads = [
                (raw[:, W_Q0, :], W["L0_xattn_Wq"]),
                (raw[:, W_K0:W_V0 + 1, :], W["L0_xattn_Wkv"].rearrange("(n p) d -> p n d", p=P)),
                (raw[:, W_PROJ, :], W["L0_xattn_Wproj"]),
                (raw[:, W_GATE:W_GATE + FC, :], W["L0_ffn_w_gate"].rearrange("(n p) d -> p n d", p=P)),
                (raw[:, W_UP:W_UP + FC, :], W["L0_ffn_w_up"].rearrange("(n p) d -> p n d", p=P)),
                (raw[:, W_DOWN:W_DOWN + 2 * FC, :].rearrange("p (c a) d -> p c a d", a=2)[:, :, 0, :],
                 W["L0_ffn_w_down"].rearrange("d (c f) -> d c f", f=P)),
                (raw[:, W_DOWN:W_DOWN + 2 * FC, :].rearrange("p (c a) d -> p c a d", a=2)[:, :, 1, :],
                 W["L0_ffn_A2"].rearrange("e r (c f) -> (e r) c f", f=P)),
                (raw[:, W_A1, :], W["L0_ffn_A1"].rearrange("e r d -> (e r) d")),
                (raw[:, W_A3, :], W["L0_ffn_A3"].rearrange("e r d -> (e r) d")),
                (raw[:, W_B2, :].rearrange("p (e r) -> p e r", e=E), W["L0_ffn_B2"].rearrange("e d r -> d e r")),
                (gate0_raw, W["L0_ffn_gate_w"]),
            ]
            for c in range(FC):
                for to, name in ((W_B1, "L0_ffn_B1"), (W_B3, "L0_ffn_B3")):
                    raw_loads.append((raw[:, to + c, :].rearrange("p (e r) -> p e r", e=E),
                                      W[name][:, c * P:(c + 1) * P, :].rearrange("e f r -> f e r")))
            assert len(raw_loads) == RAW_LOADS
            sp.dma_start(x_in[:, :, :], x_v[0]).then_inc(s_x.sem, 16)
            sp.dma_start(ctx_in[:, :, :], ctx_v[0]).then_inc(s_ctx.sem, 16)
            for to, of in raw_loads:
                sp.dma_start(to, of).then_inc(s_raw.sem, 16)
            sp.dma_start(raw_kv[:, :, :, :],
                         W["L1_xattn_Wkv"].rearrange("d (a n m) -> d a n m", a=2, m=P)).then_inc(s_rawkv.sem, 16)
            sp.dma_start(raw_q[:, :, :],
                         W["L1_xattn_Wq"].rearrange("d (h m) -> d h m", h=H)).then_inc(s_rawkv.sem, 16)
            sp.wait_ge(s_zero.sem, 1)
            small = [
                (bq0[:, :], row(W["L0_xattn_bq"], P)),
                (bkv0[:, :, :].rearrange("p a d -> p (a d)"), row(W["L0_xattn_bkv"], 2 * P)),
                (bproj0[:, :], row(W["L0_xattn_bproj"], P)),
                (qg0[:, :], row(W["L0_xattn_q_gamma"], D0)), (qb0[:, :], row(W["L0_xattn_q_beta"], D0)),
                (kg0[:, :], row(W["L0_xattn_k_gamma"], D0)), (kb0[:, :], row(W["L0_xattn_k_beta"], D0)),
                (lnm_g[:, :], row(W["L1_xattn_ln_m_g"], P)), (lnm_b[:, :], row(W["L1_xattn_ln_m_b"], P)),
                (lnl_g[:, :], row(W["L1_xattn_ln_l_g"], P)), (lnl_b[:, :], row(W["L1_xattn_ln_l_b"], P)),
                (gates_raw[:, 0:2], row(W["g_xattn"], 2)), (gates_raw[:, 2:4], row(W["g_ffn"], 2)),
                (gate1[:, :], W["L1_ffn_gate_w"]),
                (gate1_b[:, :], W["L1_ffn_gate_b"].rearrange("(e o) -> e o", o=1)),
                (b1[0:E, :], W["L1_ffn_b1"]), (b2[0:E, :], W["L1_ffn_b2"]),
                (wout[:, :, :], W["L1_xattn_Wout"].rearrange("(n p) d -> p n d", p=P)),
                (w1[:, :, :], W["L1_ffn_W1"].rearrange("e d f -> d e f")),
            ]
            assert len(small) == SMALL_LOADS
            for to, of in small:
                sp.dma_start(to, of).then_inc(s_small.sem, 16)
            def batch(b, last):
                if not last:
                    sp.wait_ge(d_x.sem, d_x.after(b, 1))
                    sp.dma_start(x_in[:, :, :], x_v[b + 1]).then_inc(s_x.sem, 16)
                    sp.dma_start(ctx_in[:, :, :], ctx_v[b + 1]).then_inc(s_ctx.sem, 16)
                sp.wait_ge(e_pv1.sem, e_pv1.after(b, NPAIR))
                for c in range(FC):
                    sp.dma_start(w2[:, c, :].rearrange("p (e d) -> p e d", e=E),
                                 t_in["L1_ffn_W2"][:, c * P:(c + 1) * P, :].rearrange("e f d -> f e d")
                                 ).then_inc(s_w2.sem, 16)
                sp.wait_ge(d_x.sem, d_x.after(b, 4))
                sp.dma_start(out_v[b], xr[:, :, :]).then_inc(s_out.sem, 16)

            with sp.Fori(0, B - 1) as b:
                batch(b, False)
            batch(B - 1, True)
            sp.wait_ge(s_out.sem, s_out.after(B, 0))

        @block.gpsimd
        def _(pool):
            pool.memset(b1[:, :], 0.0)
            pool.memset(b2[:, :], 0.0).then_inc(s_zero.sem, 1)
            pool.memset(ident[:, :], 0.0)
            pool.memset(onesb[:, :], 1.0)
            pool.memset(onesf[:, :], 1.0)
            pool.memset(v0[:, :, :], 1.0)
            pool.iota(iota_col[:, :], [[1, P]], base=0, channel_multiplier=0, allow_small_or_imprecise_dtypes=True)
            pool.iota(iota_er[:, :, :], [[1, E], [0, R]], base=0, channel_multiplier=0,
                      allow_small_or_imprecise_dtypes=True)
            pool.iota(iota_ed[:, :, :], [[1, E], [0, P]], base=0, channel_multiplier=0,
                      allow_small_or_imprecise_dtypes=True).then_inc(s_const.sem, 1)
            pool.wait_ge(s_const.sem, 1)
            pool.affine_select(out=ident[:, :], in_=ident[:, :], compare_op=ALU.not_equal, fill=1.0, base=0,
                               pattern=[[-1, P]], channel_multiplier=1).then_inc(s_const.sem, 1)
            pool.wait_ge(s_const.sem, 2)
            pool.tensor_copy(identb[:, :], ident[:, :])
            pool.tensor_scalar(negidentb[:, :], ident[:, :], -1.0, None, ALU.mult).then_inc(s_const.sem, 1)
            pool.memset(psum_1[:, 0, 0:1], 0.0).then_inc(g_sum.sem, 1)

            with pool.Fori(0, B) as b:
                pool.wait_ge(d_cn.sem, d_cn.after(b, 1))
                pool.tensor_tensor(cn, cn, lnm_g[:, :].rearrange("p (o d) -> p o d", o=1).to_broadcast([P, TC, P]),
                                   ALU.mult).then_inc(g_step.sem, 1)
                pool.wait_ge(g_step.sem, g_step.after(b, 1))
                pool.tensor_tensor(cn, cn, lnm_b[:, :].rearrange("p (o d) -> p o d", o=1).to_broadcast([P, TC, P]),
                                   ALU.add).then_inc(g_cn.sem, 1)
                pool.memset(stack[:, :, SR:SK], 0.0).then_inc(g_pad.sem, 1)
                for h in range(H):
                    pool.wait_ge(a_exp1.sem, a_exp1.after(b, h + 1))
                    pool.wait_ge(g_sum.sem, g_sum.after(b, h))
                    e = p1[:, h % PR1, :]
                    pool.tensor_tensor(psum_a, e[:, 0:768], e[:, 768:1536], ALU.add).then_inc(g_step.sem, 1)
                    pool.wait_ge(g_step.sem, g_step.after(b, 2 + 2 * h))
                    if h >= 2:
                        pool.wait_ge(e_den1.sem, e_den1.after(b, h // 2))
                    pool.tensor_tensor(psum_a[:, 0:256], psum_a[:, 0:256], psum_a[:, 256:512],
                                       ALU.add).then_inc(g_step.sem, 1)
                    pool.wait_ge(g_step.sem, g_step.after(b, 3 + 2 * h))
                    pool.tensor_tensor(psum_1[:, h % 2, :], psum_a[:, 0:256], psum_a[:, 512:768],
                                       ALU.add).then_inc(g_sum.sem, 1)

        @block.scalar
        def _(act):
            def copy(to, of):
                return act.activation(to, of, ACT.Copy)

            act.wait_ge(s_rawkv.sem, 32)
            copy(wkv_h[:, :, :, :], raw_kv)
            copy(wq_h[:, :, 0, :], raw_q)
            copy(wq_h[:, :, 1, :], raw_q).then_inc(s_whigh.sem, 1)
            act.wait_ge(s_small.sem, 16 * SMALL_LOADS)
            act.activation(gates[:, :], gates_raw[:, :], ACT.Tanh).then_inc(s_ready.sem, 1)

            with act.Fori(0, B) as b:
                act.wait_ge(e_xT.sem, e_xT.after(b, 1))
                copy(xT[:, :], bank(6)[:, 0:NQ]).then_inc(a_xT.sem, 1)
                act.wait_ge(e_ctxT.sem, e_ctxT.after(b, 1))
                copy(ctxT, bank(7)).then_inc(a_ctxT.sem, 1)
                act.wait_ge(e_cnT.sem, e_cnT.after(b, 1))
                copy(kv_h[:, 0:NC_], bank(5)).then_inc(a_cH.sem, 1)
                for p in range(NPAIR):
                    act.wait_ge(e_k.sem, e_k.after(b, p + 1))
                    src = bank(3 + p % 3)
                    copy(keys[0:D1, 2 * p, 0:NC_], src[0:D1, :])
                    copy(keys[D1:P, 2 * p + 1, 0:NC_], src[D1:P, :]).then_inc(a_kH.sem, 1)
                for h in range(0, H, 2):
                    act.wait_ge(e_kq.sem, e_kq.after(b, h + 1))
                    copy(kq[0:SK, h, :], bank(6)[0:SK, 0:384].bitcast(BF16)).then_inc(a_kq.sem, 1)
                for h in range(H):
                    act.wait_ge(e_st0.sem, e_st0.after(b, h + 1))
                    if h >= PR0:
                        act.wait_ge(e_pv0.sem, e_pv0.after(b, (h - PR0) // QUAD + 1))
                    act.activation(p0[:, h % PR0, :, :].rearrange("p k q -> p (k q)"), bank(2 + 2 * (h % 2), 2),
                                   ACT.Exp).then_inc(a_exp0.sem, 1)
                    if h % QUAD == 1 and h > QUAD:
                        g = h // QUAD - 1
                        act.wait_ge(e_pv0.sem, e_pv0.after(b, g + 1))
                        copy(o0[:, g, :], bank(6 + g % 2)[:, 0:NQ]).then_inc(a_o0.sem, 1)
                act.wait_ge(e_pv0.sem, e_pv0.after(b, NQUAD))
                copy(o0[:, NQUAD - 1, :], bank(6 + (NQUAD - 1) % 2)[:, 0:NQ]).then_inc(a_o0.sem, 1)
                act.wait_ge(e_o0.sem, e_o0.after(b, 2))
                copy(o0_T, bank(2)[:, 0:NQ]).then_inc(a_oT.sem, 1)
                act.wait_ge(e_xT.sem, e_xT.after(b, 2))
                copy(xT[:, :], bank(4)[:, 0:NQ]).then_inc(a_xT.sem, 1)
                act.wait_ge(d_gap.sem, d_gap.after(b, 1))
                act.activation(wsel[:, 1, :], wsel[:, 0, :], ACT.Exp).then_inc(a_ratio.sem, 1)
                for s in range(4):
                    act.wait_ge(e_pre0.sem, e_pre0.after(b, s + 1))
                    if s >= 2:
                        act.wait_ge(d_hid0.sem, d_hid0.after(b, s - 1))
                    act.activation(sg[:, s % 2, :], bank(s % 2), ACT.Silu).then_inc(a_silu.sem, 1)
                act.wait_ge(e_z.sem, e_z.after(b, 1))
                copy(zT, bank(6)[:, 0:NQ]).then_inc(a_zT.sem, 1)
                for t in range(TK):
                    if t == TC:
                        act.wait_ge(e_xT.sem, e_xT.after(b, 3))
                        copy(kv_h[:, NC_:NK], bank(0)[:, 0:NQ]).then_inc(a_latH.sem, 1)
                    act.wait_ge(e_v.sem, e_v.after(b, t + 1))
                    copy(v1[:, t, :], bank(2 + 2 * (t % 2), 2)).then_inc(a_v.sem, 1)
                for r in range(4):
                    act.wait_ge(e_klat.sem, e_klat.after(b, r + 1))
                    src = bank(r % 2).rearrange("p (n q) -> p n q", n=2)
                    copy(keys[0:D1, 4 * r:4 * r + 4:2, NC_:NK], src[0:D1, :, :])
                    copy(keys[D1:P, 4 * r + 1:4 * r + 4:2, NC_:NK], src[D1:P, :, :]).then_inc(a_klat.sem, 1)

                def q_high(m):
                    act.wait_ge(e_q.sem, e_q.after(b, m + 1))
                    if m >= 2:
                        act.wait_ge(e_st1.sem, e_st1.after(b, 2 * m - 2))
                    copy(q_h[:, m % 2, :, :].rearrange("p h q -> p (h q)"), bank(6 + m % 2)).then_inc(a_qH.sem, 1)

                q_high(0)
                q_high(1)
                for i in range(1, H + 1):
                    h = i - 1
                    act.wait_ge(e_st1.sem, e_st1.after(b, h + 1))
                    if h >= PR1:
                        act.wait_ge(e_pv1.sem, e_pv1.after(b, (h - PR1) // 2 + 1))
                        act.wait_ge(g_sum.sem, g_sum.after(b, h - PR1 + 1))
                    act.activation(p1[:, h % PR1, :], bank(3, 3), ACT.Exp, scale=SCALE1).then_inc(a_exp1.sem, 1)
                    if i % 2 == 0 and (i - 2) // 2 + 2 < NPAIR:
                        q_high((i - 2) // 2 + 2)
                act.wait_ge(e_y1.sem, e_y1.after(b, 1))
                copy(yT, bank(0)[:, 0:NQ]).then_inc(a_yT.sem, 1)
                act.wait_ge(e_xT.sem, e_xT.after(b, 4))
                copy(xT[:, :], bank(2)[:, 0:NQ]).then_inc(a_xT.sem, 1)
                act.wait_ge(d_smax.sem, d_smax.after(b, 1))
                act.activation(probT[0:E, :], probT[0:E, :], ACT.Exp, bias=sm[:, 1:2],
                               accum_out=sm[:, 2:3]).then_inc(a_sm.sem, 1)
                act.wait_ge(e_route1.sem, e_route1.after(b, 3))
                copy(maskT, bank(5)[:, 0:NQ]).then_inc(a_maskT.sem, 1)
                for n in range(2):
                    act.wait_ge(e_pre1.sem, e_pre1.after(b, n + 1))
                    act.activation(hid1[:, 2 * n:2 * n + 2, :].rearrange("p c q -> p (c q)"), bank(2 + n),
                                   ACT.Gelu).then_inc(a_gelu.sem, 1)

        @block.vector
        def _(dve):
            dve.wait_ge(s_whigh.sem, 1)
            dve.tensor_tensor(wkv_l[:, :, :, :], raw_kv, wkv_h[:, :, :, :], ALU.subtract)
            for n in range(2):
                dve.tensor_tensor(wq_l[:, :, n, :], raw_q, wq_h[:, :, n, :], ALU.subtract)
            dve.wait_ge(s_small.sem, 16 * SMALL_LOADS)
            dve.tensor_scalar(qg0[:, :], qg0[:, :], SCALE0, None, ALU.mult)
            dve.tensor_scalar(qb0[:, :], qb0[:, :], SCALE0, None, ALU.mult).then_inc(s_ready.sem, 1)
            for n in range(8):
                dve.wait_ge(s_wT.sem, n + 1)
                k = min(4, NT - 4 * n)
                dve.tensor_copy(wt[:, 4 * n:4 * n + k, :].rearrange("p n d -> p (n d)"),
                                bank(n)[:, 0:k * P]).then_inc(s_wT_copied.sem, 1)
            dve.wait_ge(s_wT.sem, 9)
            dve.tensor_copy(gate0[:, :], bank(0)[:, 0:E]).then_inc(s_wT_copied.sem, 1)
            dve.wait_ge(s_wT_copied.sem, 9)
            dve.wait_ge(s_ready.sem, 2)
            dve.memset(scratch[:, :], 0.0).then_inc(d_x.sem, 1)
            dve.memset(wsel[:, 0, 0:1], 0.0).then_inc(s_out.sem, 1)
            dve.wait_ge(d_x.sem, 1)

            with dve.Fori(0, B) as b:
                steps = [0]

                def step(ins):
                    steps[0] += 1
                    ins.then_inc(d_step.sem, 1)

                def own():
                    dve.wait_ge(d_step.sem, d_step.after(b, steps[0]))

                def own_first():
                    own()
                    step(dve.memset(scratch[:, :], 0.0))

                def then(ins):
                    step(ins)
                    own()

                def rsqrt(v, y, t):
                    then(dve.tensor_scalar(t.bitcast(I32), v.bitcast(I32), 1, None, ALU.arith_shift_right))
                    then(dve.tensor_scalar(y.bitcast(I32), t.bitcast(I32), -1.0, float(RSQRT_MAGIC),
                                           ALU.mult, ALU.add))
                    for _ in range(3):
                        then(dve.scalar_tensor_tensor(out=t, in0=y, scalar=-0.5, in1=y, op0=ALU.mult, op1=ALU.mult))
                        then(dve.tensor_tensor(t, t, v, ALU.mult))
                        then(dve.scalar_tensor_tensor(out=y, in0=t, scalar=1.5, in1=y, op0=ALU.add, op1=ALU.mult))

                def layernorm(to, of, tiles):
                    for t in range(tiles):
                        step(dve.bn_stats(stats[:, t, :], of[:, t, :]))
                    own_first()
                    for t in range(tiles):
                        step(dve.bn_aggr(moments[:, t, :], stats[:, t, :]))
                    own()
                    v, y, tmp = (a[:, 0:tiles] for a in rs_small)
                    then(dve.tensor_scalar(v, moments[:, 0:tiles, 1], EPS, None, ALU.add))
                    rsqrt(v, y, tmp)
                    for t in range(tiles):
                        ins = dve.tensor_scalar(to[:, t, :], of[:, t, :], moments[:, t, 0:1], y[:, t:t + 1],
                                                ALU.subtract, ALU.mult)
                        if t < tiles - 1:
                            step(ins)
                    return ins

                dve.wait_ge(s_x.sem, s_x.after(b, 16))
                layernorm(xn, x_in, TQ).then_inc(d_xn.sem, 1)
                dve.wait_ge(s_ctx.sem, s_ctx.after(b, 16))
                layernorm(cn, ctx_in, TC).then_inc(d_cn.sem, 1)

                dve.wait_ge(e_qkv0.sem, e_qkv0.after(b, 1))
                k_tiles = qk[:, 0:TC * H, :].rearrange("p (t h) d -> p t (h d)", t=TC)
                q_tiles = qk[:, TC * H:G0, :].rearrange("p (t h) d -> p t (h d)", t=TQ)
                kv_ps = bank(1, 2).rearrange("p (t a d) -> p t a d", t=TC, a=2)

                def wide(a, n, m):
                    return a.rearrange("p (o d) -> p o d", o=1).to_broadcast([P, n, m])

                step(dve.tensor_tensor(q_tiles, bank(0)[:, 0:NQ].rearrange("p (t d) -> p t d", t=TQ),
                                       wide(bq0[:, :], TQ, P), ALU.add))
                step(dve.tensor_tensor(k_tiles, kv_ps[:, :, 0, :], wide(bkv0[:, 0, :], TC, P), ALU.add))
                for t in range(TC):
                    ins = dve.tensor_tensor(
                        v0[:, t, 0:H * V0W].rearrange("p (h d) -> p h d", h=H)[:, :, 0:D0],
                        kv_ps[:, t, 1, :].rearrange("p (h d) -> p h d", h=H),
                        bkv0[:, 1, :].rearrange("p (h d) -> p h d", h=H), ALU.add)
                    if t < TC - 1:
                        step(ins)
                ins.then_inc(d_qkv0.sem, 1)
                own()

                def groups(a):
                    return a.rearrange("p (g o) -> p g o", o=1).to_broadcast([P, G0, D0])

                then(dve.tensor_reduce(hsum, qk, AX, ALU.add))
                then(dve.tensor_scalar(hsum, hsum, 1.0 / D0, None, ALU.mult))
                then(dve.tensor_tensor(qk, qk, groups(hsum), ALU.subtract))
                then(dve.tensor_tensor(qk2, qk, qk, ALU.mult))
                then(dve.tensor_reduce(hsum, qk2, AX, ALU.add))
                then(dve.tensor_scalar(rs_wide[0], hsum, 1.0 / D0, EPS, ALU.mult, ALU.add))
                rsqrt(*rs_wide)
                then(dve.tensor_tensor(qk, qk, groups(rs_wide[1]), ALU.mult))
                for lo, hi, g, be in ((0, TC * H, kg0, kb0), (TC * H, G0, qg0, qb0)):
                    then(dve.tensor_tensor(qk[:, lo:hi, :], qk[:, lo:hi, :], wide(g[:, :], hi - lo, D0), ALU.mult))
                    then(dve.tensor_tensor(qk[:, lo:hi, :], qk[:, lo:hi, :], wide(be[:, :], hi - lo, D0), ALU.add))
                then(dve.tensor_copy(parts[:, :, 0, :], qk))
                then(dve.tensor_tensor(qk2, qk, parts[:, :, 0, :], ALU.subtract))
                then(dve.tensor_copy(parts[:, :, 1, :], qk2))
                then(dve.tensor_tensor(qk, qk2, parts[:, :, 1, :], ALU.subtract))
                then(dve.tensor_copy(parts[:, :, 2, :], qk))
                PW = NPART * D0
                for n in range(NPART):
                    step(dve.tensor_copy(stack[:, 0:TC * H, n * PW:(n + 1) * PW],
                                         parts[:, 0:TC * H, :, :].rearrange("p g s d -> p g (s d)")))
                for n in range(NPART):
                    ins = dve.tensor_copy(
                        stack[:, TC * H:G0, n * PW:(n + 1) * PW].rearrange("p g (s d) -> p g s d", s=NPART),
                        parts[:, TC * H:G0, n:n + 1, :].to_broadcast([P, TQ * H, NPART, D0]))
                    if n < NPART - 1:
                        step(ins)
                ins.then_inc(d_stack.sem, 1)

                dve.wait_ge(a_cH.sem, a_cH.after(b, 1))
                dve.tensor_tensor(kv_l[:, 0:NC_], bank(5), kv_h[:, 0:NC_], ALU.subtract).then_inc(d_cL.sem, 1)
                for p in range(NPAIR):
                    dve.wait_ge(a_kH.sem, a_kH.after(b, p + 1))
                    src = bank(3 + p % 3)
                    step(dve.tensor_tensor(keys[D1:P, 2 * p, 0:NC_], src[0:D1, :], keys[0:D1, 2 * p, 0:NC_],
                                           ALU.subtract))
                    dve.tensor_tensor(keys[0:D1, 2 * p + 1, 0:NC_], src[D1:P, :], keys[D1:P, 2 * p + 1, 0:NC_],
                                      ALU.subtract).then_inc(d_kL.sem, 1)

                for h in range(1, H, 2):
                    dve.wait_ge(e_kq.sem, e_kq.after(b, h + 1))
                    dve.tensor_copy(kq[0:SK, h, :], bank(7)[0:SK, 0:384].bitcast(BF16)).then_inc(d_kq.sem, 1)

                def row_max(h, src, e_max, d_max, e_st, d_diag):
                    dve.wait_ge(e_max.sem, e_max.after(b, h + 1))
                    dve.tensor_reduce(rowmax[:, h % 2, :], src, AX, ALU.max).then_inc(d_max.sem, 1)
                    dve.wait_ge(d_max.sem, d_max.after(b, h + 1))
                    if h >= 2:
                        dve.wait_ge(e_st.sem, e_st.after(b, h - 1))
                    dve.tensor_tensor(
                        diag[:, h % 2, :, :],
                        negidentb[:, :].rearrange("p (o q) -> p o q", o=1).to_broadcast([P, TQ, P]),
                        rowmax[:, h % 2, :].rearrange("p (t o) -> p t o", o=1).to_broadcast([P, TQ, P]),
                        ALU.mult).then_inc(d_diag.sem, 1)

                for h in range(H):
                    row_max(h, bank(0, 2).rearrange("p (t k) -> p t k", t=TQ), e_max0, d_max0, e_st0, d_diag0)

                dve.wait_ge(e_o0.sem, e_o0.after(b, 1))
                o_ps = bank(0, 2).rearrange("p (t h c) -> p t h c", t=TQ, h=H)
                then(dve.reciprocal(rden0[:, :, :], o_ps[:, :, :, D0]))
                for t in range(TQ):
                    ins = dve.tensor_tensor(o0_tok[:, t, :].rearrange("p (h d) -> p h d", h=H), o_ps[:, t, :, 0:D0],
                                            rden0[:, t, :].rearrange("p (h o) -> p h o", o=1)
                                            .to_broadcast([P, H, D0]), ALU.mult)
                    if t < TQ - 1:
                        step(ins)
                ins.then_inc(d_o0.sem, 1)
                dve.wait_ge(e_o0.sem, e_o0.after(b, 3))
                dve.wait_ge(s_out.sem, s_out.after(b, 0))
                then(dve.tensor_tensor(xr[:, :, :], bank(3)[:, 0:NQ].rearrange("p (t d) -> p t d", t=TQ),
                                       wide(bproj0[:, :], TQ, P), ALU.add))
                dve.scalar_tensor_tensor(out=xr[:, :, :], in0=xr[:, :, :], scalar=G_X0, in1=x_in[:, :, :],
                                         op0=ALU.mult, op1=ALU.add).then_inc(d_x.sem, 1)

                dve.wait_ge(d_x.sem, d_x.after(b, 1))
                layernorm(xn, xr, TQ).then_inc(d_xn.sem, 1)
                dve.wait_ge(e_route0.sem, e_route0.after(b, 1))
                step(dve.tensor_copy(lg[:, :, :].rearrange("p t e -> p (t e)"), bank(5)[:, 0:TQ * E]))

                def top8(of):
                    own_first()
                    for t in range(TQ):
                        step(dve.max(top[:, t, :], of[:, t, :]))
                    own_first()
                    for t in range(TQ):
                        step(dve.max_index(topi[:, t, :], top[:, t, :], of[:, t, :]))
                    own()
                    then(dve.tensor_copy(topf[:, :, :], topi[:, :, :]))

                top8(lg)
                dve.tensor_tensor(wsel[:, 0, :], top[:, :, 1], top[:, :, 0], ALU.subtract).then_inc(d_gap.sem, 1)
                for j in range(2):
                    for t in range(TQ):
                        ins = dve.tensor_scalar(exm[:, j, t, :], iota_er[:, :, :].rearrange("p e r -> p (e r)"),
                                                topf[:, t, j:j + 1], None, ALU.is_equal)
                        if (j, t) != (1, TQ - 1):
                            step(ins)
                ins.then_inc(d_exm.sem, 1)
                dve.wait_ge(a_ratio.sem, a_ratio.after(b, 1))
                then(dve.tensor_scalar(wsel[:, 2, :], wsel[:, 1, :], 1.0, None, ALU.add))
                then(dve.reciprocal(wsel[:, 2, :], wsel[:, 2, :]))
                then(dve.tensor_tensor(wsel[:, 3, :], wsel[:, 2, :], wsel[:, 1, :], ALU.mult))
                dve.wait_ge(e_route0.sem, e_route0.after(b, 3))
                then(dve.tensor_scalar(exmT.rearrange("p j q -> p (j q)"), bank(7), LORA_SCALE, None, ALU.mult))
                for u in range(2):
                    ins = dve.tensor_tensor(
                        um[:, u, :, :],
                        bank(6)[:, u * NQ:(u + 1) * NQ].rearrange("p (o q) -> p o q", o=1).to_broadcast([P, 2, NQ]),
                        exmT, ALU.mult)
                    if u == 0:
                        step(ins)
                ins.then_inc(d_um.sem, 1)
                for s in range(4):
                    dve.wait_ge(a_silu.sem, a_silu.after(b, s + 1))
                    dve.tensor_tensor(hid0[:, s // 2, 2 * (s % 2):2 * (s % 2) + 2, :].rearrange("p c q -> p (c q)"),
                                      bank(2 + s % 2), sg[:, s % 2, :], ALU.mult).then_inc(d_hid0.sem, 1)
                for j in range(2):
                    for t in range(TQ):
                        step(dve.tensor_scalar(exm[:, j, t, :], exm[:, j, t, :], wsel[:, 2 + j, t:t + 1], LORA_SCALE,
                                               ALU.mult, ALU.mult))
                own()
                for j in range(2):
                    dve.wait_ge(e_down0.sem, e_down0.after(b, j + 1))
                    dn = bank(4 + j).rearrange("p (t a d) -> p t a d", t=TQ, a=2)
                    step(dve.tensor_tensor(zm[:, j, :, :], dn[:, :, 1, :], exm[:, j, :, :], ALU.mult))
                    for t in range(TQ):
                        if j == 0:
                            step(dve.tensor_scalar(dsum[:, t, :], dn[:, t, 0, :], wsel[:, 2, t:t + 1], None,
                                                   ALU.mult))
                        else:
                            step(dve.scalar_tensor_tensor(out=dsum[:, t, :], in0=dn[:, t, 0, :],
                                                          scalar=wsel[:, 3, t:t + 1], in1=dsum[:, t, :],
                                                          op0=ALU.mult, op1=ALU.add))
                    own()
                dve.tensor_tensor(zm[:, 0, :, :], zm[:, 0, :, :], zm[:, 1, :, :], ALU.add).then_inc(d_zm.sem, 1)
                dve.wait_ge(e_z.sem, e_z.after(b, 2))
                then(dve.tensor_tensor(dsum, bank(7)[:, 0:NQ].rearrange("p (t d) -> p t d", t=TQ), dsum, ALU.add))
                dve.scalar_tensor_tensor(out=xr[:, :, :], in0=dsum, scalar=G_F0, in1=xr[:, :, :],
                                         op0=ALU.mult, op1=ALU.add).then_inc(d_x.sem, 1)

                dve.wait_ge(d_x.sem, d_x.after(b, 2))
                then(layernorm(xn, xr, TQ))
                then(layernorm(xn, xn, TQ))
                then(dve.tensor_tensor(xn[:, :, :], xn[:, :, :], wide(lnl_g[:, :], TQ, P), ALU.mult))
                dve.tensor_tensor(xn[:, :, :], xn[:, :, :], wide(lnl_b[:, :], TQ, P), ALU.add).then_inc(d_xn.sem, 1)
                dve.wait_ge(a_latH.sem, a_latH.after(b, 1))
                dve.tensor_tensor(kv_l[:, NC_:NK], bank(0)[:, 0:NQ], kv_h[:, NC_:NK],
                                  ALU.subtract).then_inc(d_latL.sem, 1)
                for r in range(4):
                    dve.wait_ge(a_klat.sem, a_klat.after(b, r + 1))
                    src = bank(r % 2).rearrange("p (n q) -> p n q", n=2)
                    ev, od = slice(4 * r, 4 * r + 4, 2), slice(4 * r + 1, 4 * r + 4, 2)
                    step(dve.tensor_tensor(keys[D1:P, ev, NC_:NK], src[0:D1, :, :], keys[0:D1, ev, NC_:NK],
                                           ALU.subtract))
                    dve.tensor_tensor(keys[0:D1, od, NC_:NK], src[D1:P, :, :], keys[D1:P, od, NC_:NK],
                                      ALU.subtract).then_inc(d_klat.sem, 1)

                def q_low(m):
                    dve.wait_ge(a_qH.sem, a_qH.after(b, m + 1))
                    dve.tensor_tensor(q_l[:, m % 2, :, :].rearrange("p h q -> p (h q)"), bank(6 + m % 2),
                                      q_h[:, m % 2, :, :].rearrange("p h q -> p (h q)"),
                                      ALU.subtract).then_inc(d_qL.sem, 1)

                def divide(p):
                    dve.wait_ge(e_den1.sem, e_den1.after(b, p + 1))
                    o = bank(6 + p % 2)
                    then(dve.reciprocal(o1[:, p, :], o[:, NQ:2 * NQ]))
                    dve.tensor_tensor(o1[:, p, :], o[:, 0:NQ], o1[:, p, :], ALU.mult).then_inc(d_o1.sem, 1)

                q_low(0)
                q_low(1)
                for i in range(H + 2):
                    if i < H:
                        row_max(i, bank(0, 3).rearrange("p (t k) -> p t k", t=TQ), e_max1, d_max1, e_st1, d_diag1)
                    if i % 2 == 1 and i >= 5:
                        divide((i - 3) // 2 - 1)
                    if i % 2 == 0 and i >= 2 and (i - 2) // 2 + 2 < NPAIR:
                        q_low((i - 2) // 2 + 2)
                divide(NPAIR - 1)
                dve.wait_ge(e_y1.sem, e_y1.after(b, 2))
                dve.scalar_tensor_tensor(out=xr[:, :, :], in0=bank(1)[:, 0:NQ].rearrange("p (t d) -> p t d", t=TQ),
                                         scalar=G_X1, in1=xr[:, :, :], op0=ALU.mult,
                                         op1=ALU.add).then_inc(d_x.sem, 1)

                dve.wait_ge(d_x.sem, d_x.after(b, 3))
                layernorm(xn, xr, TQ).then_inc(d_xn.sem, 1)
                then(dve.memset(probT, 0.0))
                dve.wait_ge(e_route1.sem, e_route1.after(b, 1))
                then(dve.tensor_scalar(probT[0:E, :], bank(3)[0:E, 0:NQ], gate1_b[:, :], None, ALU.add))
                then(dve.tensor_reduce(sm[:, 0:1], probT[0:E, :], AX, ALU.max))
                dve.tensor_scalar(sm[:, 1:2], sm[:, 0:1], -1.0, None, ALU.mult).then_inc(d_smax.sem, 1)
                dve.wait_ge(a_sm.sem, a_sm.after(b, 1))
                then(dve.reciprocal(sm[:, 3:4], sm[:, 2:3]))
                dve.tensor_scalar(probT[0:E, :], probT[0:E, :], sm[:, 3:4], None, ALU.mult).then_inc(d_prob.sem, 1)
                dve.wait_ge(e_route1.sem, e_route1.after(b, 2))
                step(dve.tensor_copy(lg[:, :, :], bank(4)[:, 0:NQ].rearrange("p (t n) -> p t n", t=TQ)[:, :, 0:E]))
                top8(lg)
                for t in range(TQ):
                    step(dve.tensor_scalar(maskb[:, t, :, :].rearrange("p e d -> p (e d)"),
                                           iota_ed[:, :, :].rearrange("p e d -> p (e d)"), topf[:, t, 0:1], None,
                                           ALU.is_equal))
                for t in range(TQ):
                    ins = dve.tensor_scalar(maskp[:, t, :], iota_col[:, :], topf[:, t, 0:1], None, ALU.is_equal)
                    if t < TQ - 1:
                        step(ins)
                ins.then_inc(d_mask.sem, 1)
                for n in range(2):
                    dve.wait_ge(e_route1.sem, e_route1.after(b, 4 + n))
                    dve.tensor_tensor(xm[:, 4 * n:4 * n + 4, :],
                                      bank((0, 6)[n], 2).rearrange("p (e q) -> p e q", e=4),
                                      xT[:, :].rearrange("p (o q) -> p o q", o=1).to_broadcast([P, 4, NQ]),
                                      ALU.mult).then_inc(d_xm.sem, 1)
                for t in range(TQ):
                    dve.wait_ge(e_out1.sem, e_out1.after(b, t + 1))
                    then(dve.tensor_tensor(sel, bank((0, 6)[t], 2).rearrange("p (e d) -> p e d", e=E),
                                           maskp[:, t, 0:E].rearrange("p (e o) -> p e o", o=1)
                                           .to_broadcast([P, E, P]), ALU.mult))
                    then(dve.tensor_reduce(ysum[:, t, :], sel.rearrange("p e d -> p d e"), AX, ALU.add))
                    then(dve.tensor_tensor(ysum[:, t, :], bank(4 + t)[:, 0:P], ysum[:, t, :], ALU.add))
                dve.scalar_tensor_tensor(out=xr[:, :, :], in0=ysum, scalar=G_F1, in1=xr[:, :, :],
                                         op0=ALU.mult, op1=ALU.add).then_inc(d_x.sem, 1)
                assert steps[0] == DVE_STEPS, steps[0]

        @block.tensor
        def _(pe):
            def mm(o, lhsT, rhs, start=True, stop=True):
                return pe.matmul(o, lhsT, rhs, start=start, stop=stop)

            def mm_split(o, lhs_hl, rhs_hl, start=True, stop=True):
                (lh, ll), (rh, rl) = lhs_hl, rhs_hl
                mm(o, lh, rh, start, False)
                mm(o, lh, rl, False, False)
                return mm(o, ll, rh, False, stop)

            pe.wait_ge(s_const.sem, 3)
            pe.wait_ge(s_raw.sem, 16 * RAW_LOADS)
            for n in range(NT):
                ins = pe.transpose(bank(n // 4)[:, (n % 4) * P:(n % 4 + 1) * P], raw[:, n, :], ident[:, :])
                if n % 4 == 3 or n == NT - 1:
                    ins.then_inc(s_wT.sem, 1)
            pe.wait_ge(s_wT_copied.sem, 1)
            pe.transpose(bank(0)[:, 0:E], gate0_raw, ident[0:E, 0:E]).then_inc(s_wT.sem, 1)
            pe.wait_ge(s_wT_copied.sem, 9)
            pe.wait_ge(s_small.sem, 16 * SMALL_LOADS)
            pe.wait_ge(s_ready.sem, 2)

            def tok(a, t):
                return a[:, t * P:(t + 1) * P]

            with pe.Fori(0, B) as b:
                def transpose_tiles(o, of, tiles):
                    for t in range(tiles):
                        ins = pe.transpose(tok(o, t), of[:, t, :], ident[:, :])
                    return ins

                pe.wait_ge(d_x.sem, d_x.after(b, 0))
                pe.wait_ge(d_xn.sem, d_xn.after(b, 1))
                transpose_tiles(bank(6), xn, TQ).then_inc(e_xT.sem, 1)
                pe.wait_ge(s_ctx.sem, s_ctx.after(b, 16))
                transpose_tiles(bank(7), ctx_in, TC).then_inc(e_ctxT.sem, 1)
                pe.wait_ge(g_cn.sem, g_cn.after(b, 1))
                transpose_tiles(bank(5), cn, TC).then_inc(e_cnT.sem, 1)
                pe.wait_ge(a_xT.sem, a_xT.after(b, 1))
                for t in range(TQ):
                    mm(tok(bank(0), t), tok(xT, t), wt[:, W_Q0, :])
                pe.wait_ge(a_ctxT.sem, a_ctxT.after(b, 1))
                for t in range(TC):
                    ins = mm(bank(1, 2)[:, t * 2 * P:(t + 1) * 2 * P], tok(ctxT, t),
                             wt[:, W_K0:W_V0 + 1, :].rearrange("p n d -> p (n d)"))
                ins.then_inc(e_qkv0.sem, 1)
                pe.wait_ge(d_cL.sem, d_cL.after(b, 1))
                for p in range(NPAIR):
                    if p >= 3:
                        pe.wait_ge(d_kL.sem, d_kL.after(b, p - 2))
                    mm_split(bank(3 + p % 3), (wkv_h[:, 0, p, :], wkv_l[:, 0, p, :]),
                             (kv_h[:, 0:NC_], kv_l[:, 0:NC_])).then_inc(e_k.sem, 1)
                pe.wait_ge(d_stack.sem, d_stack.after(b, 1))
                pe.wait_ge(g_pad.sem, g_pad.after(b, 1))
                for h in range(H):
                    if h >= 2:
                        done = a_kq if h % 2 == 0 else d_kq
                        pe.wait_ge(done.sem, done.after(b, h // 2))
                    o = bank(6 + h % 2)[:, 0:384].bitcast(BF16)
                    for t in range(TK):
                        ins = pe.transpose(o[0:SK, t * P:(t + 1) * P], stack[:, t * H + h, :], identb[:, :])
                    ins.then_inc(e_kq.sem, 1)
                pe.wait_ge(a_kq.sem, a_kq.after(b, H // 2))
                pe.wait_ge(d_kq.sem, d_kq.after(b, H // 2))
                pe.wait_ge(d_kL.sem, d_kL.after(b, NPAIR))

                def max0(h):
                    if h >= 1:
                        pe.wait_ge(d_max0.sem, d_max0.after(b, h))
                    for t in range(TQ):
                        ins = mm(bank(t), kq[0:SK, h, NC_ + t * P:NC_ + (t + 1) * P], kq[0:SK, h, 0:NC_])
                    ins.then_inc(e_max0.sem, 1)

                def scores0(h):
                    pe.wait_ge(d_diag0.sem, d_diag0.after(b, h + 1))
                    if h >= 2:
                        pe.wait_ge(a_exp0.sem, a_exp0.after(b, h - 1))
                    for k in range(TC):
                        o = bank(2 + 2 * (h % 2), 2)[:, k * NQ:(k + 1) * NQ]
                        mm(o, kq[0:SK, h, k * P:(k + 1) * P], kq[0:SK, h, NC_:NK], True, False)
                        ins = mm(o, onesb[:, :], diag[:, h % 2, :, :].rearrange("p t q -> p (t q)"), False, True)
                    ins.then_inc(e_st0.sem, 1)

                def values0(g):
                    pe.wait_ge(a_exp0.sem, a_exp0.after(b, QUAD * (g + 1)))
                    if g >= 2:
                        pe.wait_ge(a_o0.sem, a_o0.after(b, g - 1))
                    for k in range(TC):
                        for j in range(QUAD):
                            h = QUAD * g + j
                            ins = mm(bank(6 + g % 2)[32 * j:32 * j + 32, 0:NQ], v0[:, k, h * V0W:h * V0W + 32],
                                     p0[:, h % PR0, k, :], k == 0, k == TC - 1)
                    ins.then_inc(e_pv0.sem, 1)

                for i in range(H + 1):
                    if i < H:
                        max0(i)
                    if i >= 1:
                        scores0(i - 1)
                    if i >= 5 and i % 4 == 1:
                        if i < H + 1 or True:
                            if i - 1 < H:
                                values0((i - 5) // 4)
                values0(NQUAD - 1)
                pe.wait_ge(a_o0.sem, a_o0.after(b, NQUAD))
                pe.wait_ge(d_max0.sem, d_max0.after(b, H))
                for t in range(TQ):
                    for g in range(NQUAD):
                        ins = pe.transpose(bank(t)[:, g * P:(g + 1) * P], o0[:, g, t * P:(t + 1) * P], ident[:, :])
                ins.then_inc(e_o0.sem, 1)
                pe.wait_ge(d_o0.sem, d_o0.after(b, 1))
                transpose_tiles(bank(2), o0_tok, TQ).then_inc(e_o0.sem, 1)
                pe.wait_ge(a_oT.sem, a_oT.after(b, 1))
                for t in range(TQ):
                    ins = mm(tok(bank(3), t), tok(o0_T, t), wt[:, W_PROJ, :])
                ins.then_inc(e_o0.sem, 1)

                pe.wait_ge(d_xn.sem, d_xn.after(b, 2))
                transpose_tiles(bank(4), xn, TQ).then_inc(e_xT.sem, 1)
                pe.wait_ge(a_xT.sem, a_xT.after(b, 2))
                for t in range(TQ):
                    ins = mm(bank(5)[:, t * E:(t + 1) * E], tok(xT, t), gate0[:, :])
                ins.then_inc(e_route0.sem, 1)
                for u, w in enumerate((W_A1, W_A3)):
                    ins = mm(bank(6)[:, u * NQ:(u + 1) * NQ], wt[:, w, :], xT[:, :])
                ins.then_inc(e_route0.sem, 1)
                pe.wait_ge(d_exm.sem, d_exm.after(b, 1))
                for j in range(2):
                    for t in range(TQ):
                        ins = pe.transpose(bank(7)[:, (j * TQ + t) * P:(j * TQ + t + 1) * P], exm[:, j, t, :],
                                           ident[:, :])
                ins.then_inc(e_route0.sem, 1)
                pe.wait_ge(d_um.sem, d_um.after(b, 1))
                for s in range(4):
                    j = s // 2
                    if s >= 2:
                        pe.wait_ge(d_hid0.sem, d_hid0.after(b, s - 1))
                    for u, (wx, wb) in enumerate(((W_GATE, W_B1), (W_UP, W_B3))):
                        for c in (2 * (s % 2), 2 * (s % 2) + 1):
                            o = bank(2 * u + s % 2)[:, (c % 2) * NQ:(c % 2 + 1) * NQ]
                            mm(o, wt[:, wx + c, :], xT[:, :], True, False)
                            ins = mm(o, wt[:, wb + c, :], um[:, u, j, :], False, True)
                    ins.then_inc(e_pre0.sem, 1)
                for j in range(2):
                    pe.wait_ge(d_hid0.sem, d_hid0.after(b, 2 * j + 2))
                    for t in range(TQ):
                        for c in range(FC):
                            ins = mm(bank(4 + j)[:, t * 2 * P:(t + 1) * 2 * P], hid0[:, j, c, t * P:(t + 1) * P],
                                     wt[:, W_DOWN + 2 * c:W_DOWN + 2 * c + 2, :].rearrange("p n d -> p (n d)"),
                                     c == 0, c == FC - 1)
                    ins.then_inc(e_down0.sem, 1)
                pe.wait_ge(d_zm.sem, d_zm.after(b, 1))
                transpose_tiles(bank(6), zm[:, 0, :, :], TQ).then_inc(e_z.sem, 1)
                pe.wait_ge(a_zT.sem, a_zT.after(b, 1))
                for t in range(TQ):
                    ins = mm(tok(bank(7), t), tok(zT, t), wt[:, W_B2, :])
                ins.then_inc(e_z.sem, 1)

                for t in range(TK):
                    if t == TC:
                        pe.wait_ge(d_xn.sem, d_xn.after(b, 3))
                        transpose_tiles(bank(0), xn, TQ).then_inc(e_xT.sem, 1)
                        pe.wait_ge(d_latL.sem, d_latL.after(b, 1))
                    if t >= 2:
                        pe.wait_ge(a_v.sem, a_v.after(b, t - 1))
                    for n in range(2):
                        ins = mm_split(bank(2 + 2 * (t % 2) + n), (tok(kv_h, t), tok(kv_l, t)),
                                       tuple(w[:, 1, 4 * n:4 * n + 4, :].rearrange("p n d -> p (n d)")
                                             for w in (wkv_h, wkv_l)))
                    ins.then_inc(e_v.sem, 1)
                lat = (kv_h[:, NC_:NK], kv_l[:, NC_:NK])
                for r in range(4):
                    if r >= 2:
                        pe.wait_ge(d_klat.sem, d_klat.after(b, r - 1))
                    for n in range(2):
                        ins = mm_split(bank(r % 2)[:, n * NQ:(n + 1) * NQ],
                                       (wkv_h[:, 0, 2 * r + n, :], wkv_l[:, 0, 2 * r + n, :]), lat)
                    ins.then_inc(e_klat.sem, 1)

                def project_q(m):
                    if m >= 4:
                        pe.wait_ge(d_o1.sem, d_o1.after(b, m - 3))
                    for n in range(2):
                        h = 2 * m + n
                        w = tuple(x[:, h, :, :].rearrange("p n d -> p (n d)") for x in (wq_h, wq_l))
                        ins = mm_split(bank(6 + m % 2)[:, n * NQ:(n + 1) * NQ], w, lat)
                    ins.then_inc(e_q.sem, 1)

                project_q(0)
                project_q(1)
                pe.wait_ge(a_v.sem, a_v.after(b, TK))
                pe.wait_ge(d_klat.sem, d_klat.after(b, 4))

                def max1(h):
                    pe.wait_ge(d_qL.sem, d_qL.after(b, h // 2 + 1))
                    if h >= 1:
                        pe.wait_ge(d_max1.sem, d_max1.after(b, h))
                    cuts = sorted({0, BANK, 2 * BANK, 3 * BANK, NK})
                    for lo, hi in zip(cuts, cuts[1:]):
                        t, k = lo // NK, lo % NK
                        ins = mm(bank(0, 3)[:, lo:hi], q_h[:, (h // 2) % 2, h % 2, t * P:(t + 1) * P],
                                 keys[:, h, k:k + hi - lo])
                    ins.then_inc(e_max1.sem, 1)

                def scores1(h):
                    pe.wait_ge(d_diag1.sem, d_diag1.after(b, h + 1))
                    if h >= 1:
                        pe.wait_ge(a_exp1.sem, a_exp1.after(b, h))
                    for k in range(TK):
                        o = bank(3, 3)[:, k * NQ:(k + 1) * NQ]
                        mm(o, keys[:, h, k * P:(k + 1) * P], q_h[:, (h // 2) % 2, h % 2, :], True, False)
                        mm(o, keys[:, h, k * P:(k + 1) * P], q_l[:, (h // 2) % 2, h % 2, :], False, False)
                        ins = mm(o, onesb[:, :], diag[:, h % 2, :, :].rearrange("p t q -> p (t q)"), False, True)
                    ins.then_inc(e_st1.sem, 1)

                def values1(p):
                    pe.wait_ge(a_exp1.sem, a_exp1.after(b, 2 * p + 2))
                    pe.wait_ge(d_qL.sem, d_qL.after(b, min(p + 3, NPAIR)))
                    if p >= 2:
                        pe.wait_ge(d_o1.sem, d_o1.after(b, p - 1))
                    for k in range(TK):
                        for j in range(2):
                            h = 2 * p + j
                            ins = mm(bank(6 + p % 2)[j * D1:(j + 1) * D1, 0:NQ], v1[:, k, h * D1:(h + 1) * D1],
                                     p1[:, h % PR1, k * NQ:(k + 1) * NQ], k == 0, k == TK - 1)
                    ins.then_inc(e_pv1.sem, 1)

                def sums1(p):
                    pe.wait_ge(g_sum.sem, g_sum.after(b, 2 * p + 2))
                    for j in range(2):
                        ins = mm(bank(6 + p % 2)[j * D1:(j + 1) * D1, NQ:2 * NQ], onesf[:, :], psum_1[:, j, :])
                    ins.then_inc(e_den1.sem, 1)

                for i in range(H + 2):
                    if i < H:
                        max1(i)
                    if 1 <= i <= H:
                        scores1(i - 1)
                    if i % 2 == 1 and i >= 3:
                        p = (i - 3) // 2
                        values1(p)
                        if p >= 1:
                            sums1(p - 1)
                    if i % 2 == 0 and i >= 2 and (i - 2) // 2 + 2 < NPAIR:
                        project_q((i - 2) // 2 + 2)
                sums1(NPAIR - 1)
                pe.wait_ge(d_max1.sem, d_max1.after(b, H))
                pe.wait_ge(d_o1.sem, d_o1.after(b, NPAIR))
                for p in range(NPAIR):
                    ins = mm(bank(0)[:, 0:NQ], wout[:, p, :], o1[:, p, :], p == 0, p == NPAIR - 1)
                ins.then_inc(e_y1.sem, 1)
                pe.wait_ge(a_yT.sem, a_yT.after(b, 1))
                transpose_tiles(bank(1), yT.rearrange("p (t d) -> p t d", t=TQ), TQ).then_inc(e_y1.sem, 1)

                pe.wait_ge(d_xn.sem, d_xn.after(b, 4))
                transpose_tiles(bank(2), xn, TQ).then_inc(e_xT.sem, 1)
                pe.wait_ge(a_xT.sem, a_xT.after(b, 3))
                mm(bank(3)[0:E, 0:NQ], gate1[:, :], xT[:, :]).then_inc(e_route1.sem, 1)
                pe.wait_ge(d_prob.sem, d_prob.after(b, 1))
                transpose_tiles(bank(4), probT.rearrange("p (t d) -> p t d", t=TQ), TQ).then_inc(e_route1.sem, 1)
                pe.wait_ge(d_mask.sem, d_mask.after(b, 1))
                transpose_tiles(bank(5), maskp, TQ).then_inc(e_route1.sem, 1)
                for n in range(2):
                    for e in range(4):
                        for t in range(TQ):
                            ins = mm(bank((0, 6)[n], 2)[:, e * NQ + t * P:e * NQ + (t + 1) * P],
                                     maskb[:, t, 4 * n + e, :], identb[:, :])
                    ins.then_inc(e_route1.sem, 1)
                pe.wait_ge(a_maskT.sem, a_maskT.after(b, 1))
                pe.wait_ge(d_xm.sem, d_xm.after(b, 2))
                for c in range(FC):
                    o = bank(2 + c // 2)[:, (c % 2) * NQ:(c % 2 + 1) * NQ]
                    for e in range(E):
                        mm(o, w1[:, e, c * P:(c + 1) * P], xm[:, e, :], e == 0, False)
                    ins = mm(o, b1[:, c * P:(c + 1) * P], maskT, False, True)
                    if c % 2 == 1:
                        ins.then_inc(e_pre1.sem, 1)
                for t in range(TQ):
                    mm(bank(4 + t)[:, 0:P], maskT[:, t * P:(t + 1) * P], b2[:, :])
                pe.wait_ge(s_w2.sem, s_w2.after(b, 16 * FC))
                pe.wait_ge(a_gelu.sem, a_gelu.after(b, 2))
                for t in range(TQ):
                    for n in range(2):
                        for c in range(FC):
                            ins = mm(bank((0, 6)[t] + n), hid1[:, c, t * P:(t + 1) * P],
                                     w2[:, c, n * BANK:(n + 1) * BANK], c == 0, c == FC - 1)
                    ins.then_inc(e_out1.sem, 1)


RAW_LOADS = 19
SMALL_LOADS = 19

_INS = ['x', 'ctx_1024', 'g_xattn', 'g_ffn', 'L0_xattn_Wq', 'L0_xattn_bq', 'L0_xattn_Wkv', 'L0_xattn_bkv',
        'L0_xattn_q_gamma', 'L0_xattn_q_beta', 'L0_xattn_k_gamma', 'L0_xattn_k_beta', 'L0_xattn_Wproj',
        'L0_xattn_bproj', 'L0_ffn_gate_w', 'L0_ffn_w_gate', 'L0_ffn_w_up', 'L0_ffn_w_down', 'L0_ffn_A1',
        'L0_ffn_B1', 'L0_ffn_A3', 'L0_ffn_B3', 'L0_ffn_A2', 'L0_ffn_B2', 'L1_xattn_ln_m_g', 'L1_xattn_ln_m_b',
        'L1_xattn_ln_l_g', 'L1_xattn_ln_l_b', 'L1_xattn_Wq', 'L1_xattn_Wkv', 'L1_xattn_Wout', 'L1_ffn_gate_w',
        'L1_ffn_gate_b', 'L1_ffn_W1', 'L1_ffn_b1', 'L1_ffn_W2', 'L1_ffn_b2']
_OUT = ((4, 256, 128), 'float32')


def kernel(**inputs):
    import numpy as _np
    import concourse.bacc as _bacc
    from concourse import mybir as _mybir
    from concourse.bass_utils import run_bass_kernel_spmd as _run

    nc = _bacc.Bacc("TRN2", target_bir_lowering=False, num_devices=1)
    arrays, args = {}, {}
    for name in _INS:
        a = _np.ascontiguousarray(inputs[name])
        arrays[f"in_{name}_dram"] = a
        args[name] = nc.dram_tensor(f"in_{name}_dram", a.shape, _mybir.dt.from_np(a.dtype), kind="ExternalInput").ap()
    out = nc.dram_tensor("out_0_dram", _OUT[0], _mybir.dt.from_np(_np.dtype(_OUT[1])), kind="ExternalOutput").ap()
    flamingo(nc, args, out)
    r = _run(nc, [arrays], core_ids=[0])
    return r.results[0]["out_0_dram"]
```

```python
from contextlib import ExitStack

import concourse.bass as bass
from concourse import mybir

F32 = mybir.dt.float32
F32R = mybir.dt.float32r
BF16 = mybir.dt.bfloat16
I32 = mybir.dt.int32
U32 = mybir.dt.uint32
ALU = mybir.AluOpType
ACT = mybir.ActivationFunctionType
AX = mybir.AxisListType.X

P = 128
BANK = 512
SBUF_END = 229368
EPS = 1e-5
RSQRT_MAGIC = 0x5F3759DF


class Signal:

    def __init__(self, sem, per_batch, before=0):
        self.sem, self.per_batch, self.before = sem, per_batch, before

    def after(self, b, k):
        return b * self.per_batch + (self.before + k)


def flamingo(nc, t_in, out):
    x_d, ctx_d = t_in["x"], t_in["ctx_1024"]
    B, NQ, D = x_d.shape
    NC_ = ctx_d.shape[1]
    TQ, TC = NQ // P, NC_ // P
    TK = TC + TQ
    NK = NC_ + NQ
    H = 16
    D0 = D // H
    D1 = t_in["L1_xattn_Wq"].shape[1] // H
    E, R = t_in["L0_ffn_A1"].shape[:2]
    F = t_in["L0_ffn_w_gate"].shape[0]
    FC = F // P
    SCALE0 = float(D0) ** -0.5
    SCALE1 = float(D1) ** -0.5
    LORA_SCALE = 2.0
    NPART = 3
    SR = NPART * NPART * D0
    SK = 96
    G0 = (TC + TQ) * H
    NPAIR = H // 2
    QUAD = 4
    NQUAD = H // QUAD
    V0W = D0 + 1
    V0C = H * V0W + 32 - V0W
    PR0, PR1 = 6, 3
    RM0, DG0 = 4, 3
    KEYS_AT = (SBUF_END - 4 * H * NK) // 32 * 32
    assert D == P and E * R == P and NQ == 256 and NC_ == 512 and D1 == 64 and SR <= SK

    with ExitStack() as ctx:
        def sb(name, shape, dt=F32):
            return ctx.enter_context(nc.sbuf_tensor(name, shape, dt))

        signals = {}

        def signal(name, per_batch=0, before=0):
            s = Signal(ctx.enter_context(nc.semaphore(name)), per_batch, before)
            signals[name] = s
            return s

        ident = sb("ident", [P, P])
        identb = sb("identb", [P, P], BF16)
        negidentb = sb("negidentb", [P, P], BF16)
        onesb = sb("onesb", [P, P], BF16)
        onesf = sb("onesf", [P, D1])
        iota_er = sb("iota_er", [P, E, R])
        iota_col = sb("iota_col", [P, P])
        iota_ed = sb("iota_ed", [P, E, P], BF16)
        NT = 31
        wt = sb("wt", [P, NT, P])
        W_Q0, W_K0, W_V0, W_PROJ, W_GATE, W_UP, W_B1, W_B3, W_DOWN, W_A1, W_A3, W_B2 = (
            0, 1, 2, 3, 4, 8, 12, 16, 20, 28, 29, 30)
        gate0 = sb("gate0", [P, E])
        wkv_h = sb("wkv_h", [P, 2, NPAIR, P], F32R)
        wkv_l = sb("wkv_l", [P, 2, NPAIR, P], F32R)
        wq_h = sb("wq_h", [P, NPAIR, P], F32R)
        wq_l = sb("wq_l", [P, NPAIR, P], F32R)
        wout = sb("wout", [P, NPAIR, P])
        w1 = sb("w1", [P, E, F])
        b1 = sb("b1", [P, F])
        b2 = sb("b2", [P, P])
        gate1 = sb("gate1", [P, E])
        gate1_b = sb("gate1_b", [E, 1])
        bq0 = sb("bq0", [P, P])
        bkv0 = sb("bkv0", [P, 2, P])
        bproj0 = sb("bproj0", [P, P])
        qg0, qb0, kg0, kb0 = (sb(n, [P, D0]) for n in ("qg0", "qb0", "kg0", "kb0"))
        lnm_g, lnm_b = (sb(n, [P, P]) for n in ("lnm_g", "lnm_b"))
        lnl_g, lnl_b = (sb(n, [P, 1]) for n in ("lnl_g", "lnl_b"))
        gates_raw = sb("gates_raw", [P, 4])
        gates = sb("gates", [P, 4])
        G_X0, G_X1, G_F0, G_F1 = (gates[:, i:i + 1] for i in range(4))

        x_in = sb("x_in", [P, TQ, P])
        ctx_in = sb("ctx_in", [P, TC, P])
        xr = sb("xr", [P, TQ, P])
        xn = sb("xn", [P, TQ, P])
        xT = sb("xT", [P, NQ])
        xn0 = sb("xn0", [P, TQ, P])
        cn = sb("cn", [P, TC, P])
        xT0 = sb("xT0", [P, NQ])
        ctxT = sb("ctxT", [P, NC_])
        stats0 = sb("stats0", [P, TK, 6])
        moments0 = sb("moments0", [P, TK, 2])
        rs0 = tuple(sb(n, [P, TK]) for n in ("rs0_v", "rs0_y", "rs0_t"))
        kv_h = sb("kv_h", [P, NK], F32R)
        kv_l = sb("kv_l", [P, NK], F32R)
        v0 = sb("v0", [P, TC, V0C])
        area_k = nc.alloc_sbuf_tensor_at("area_k", [P, H * NK], F32, offset=KEYS_AT)
        keys = nc.alloc_sbuf_tensor_at("keys", [P, H, NK], F32R, offset=KEYS_AT)
        q_h = sb("q_h", [P, 2, 2, NQ], F32R)
        q_l = sb("q_l", [P, 2, 2, NQ], F32R)
        area_o = sb("area_o", [P, NPAIR * NQ])
        area_v = sb("area_v", [P, TK * H * D1])
        area_p = sb("area_p", [P, 6144])
        stats = sb("stats", [P, TQ, 6])
        moments = sb("moments", [P, TQ, 2])
        rs_small = tuple(sb(n, [P, TQ]) for n in ("rs_v", "rs_y", "rs_t"))
        rowmax = sb("rowmax", [P, RM0, TQ])
        diag = sb("diag", [P, DG0, TQ, P], BF16)
        rden0 = sb("rden0", [P, TQ, H])
        lg = sb("lg", [P, TQ, E])
        top = sb("top", [P, TQ, 8])
        topi = sb("topi", [P, TQ, 8], U32)
        topf = sb("topf", [P, TQ, 8])
        wsel = sb("wsel", [P, 4, TQ])
        mask = sb("mask", [P, TQ, E])
        sm = sb("sm", [E, 4])
        scratch = sb("scratch", [P, 2])
        scratch_g = sb("scratch_g", [P, 1])
        assert nc.sbuf_base <= KEYS_AT, nc.sbuf_base

        o0 = area_o[:, 0:NQUAD * NQ].rearrange("p (g q) -> p g q", g=NQUAD)
        o0_tok = area_o[:, 1024:1280].rearrange("p (t d) -> p t d", t=TQ)
        o0_T = area_o[:, 1280:1536]
        o1 = area_o[:, :].rearrange("p (h q) -> p h q", h=NPAIR)
        qk = area_k[:, 4608:5376].rearrange("p (g d) -> p g d", d=D0)
        qk2 = area_k[:, 5376:6144].rearrange("p (g d) -> p g d", d=D0)
        parts = area_k[:, 6144:7296].bitcast(BF16).rearrange("p (g s d) -> p g s d", s=NPART, d=D0)
        rs_wide = tuple(area_k[:, n:n + G0] for n in range(7296, 7296 + 3 * G0, G0))
        hsum = area_k[:, 7296 + 3 * G0:7296 + 4 * G0]
        stack = area_k[:, 7680:7680 + G0 * SK // 2].bitcast(BF16).rearrange("p (g r) -> p g r", r=SK)
        kq = area_v[:, :].bitcast(BF16).rearrange("p (h n) -> p h n", h=H)
        v1 = area_v[:, :].rearrange("p (t n) -> p t n", t=TK)
        w2 = area_v[:, 0:FC * E * P].rearrange("p (c n) -> p c n", c=FC)
        p0 = area_p[:, 0:PR0 * TC * NQ].rearrange("p (s k q) -> p s k q", s=PR0, q=NQ)
        p1 = area_p[:, 0:PR1 * TK * NQ].rearrange("p (s n) -> p s n", s=PR1)
        psum_a = area_p[:, 4608:5376]
        psum_1 = area_p[:, 5376:5888].rearrange("p (s q) -> p s q", s=2)
        exm = area_p[:, 0:512].rearrange("p (j t n) -> p j t n", j=2, t=TQ)
        exmT = area_p[:, 512:1024].rearrange("p (j q) -> p j q", j=2)
        um = area_p[:, 1024:2048].rearrange("p (u j q) -> p u j q", u=2, j=2)
        hid0 = area_p[:, 2048:4096].rearrange("p (j c q) -> p j c q", j=2, c=FC)
        sg = area_p[:, 4096:5120].rearrange("p (s n) -> p s n", s=2)
        zm = area_p[:, 5120:5632].rearrange("p (j t n) -> p j t n", j=2, t=TQ)
        zT = area_p[:, 5632:5888]
        dsum = area_p[:, 5888:6144].rearrange("p (t n) -> p t n", t=TQ)
        xm = area_p[:, 0:2048].rearrange("p (e q) -> p e q", e=E)
        hid1 = area_p[:, 2048:3072].rearrange("p (c q) -> p c q", c=FC)
        maskb = area_p[:, 3072:4096].bitcast(BF16).rearrange("p (t e d) -> p t e d", t=TQ, e=E)
        sel = area_p[:, 4096:5120].rearrange("p (e d) -> p e d", e=E)
        maskp = area_p[:, 5120:5376].rearrange("p (t n) -> p t n", t=TQ)
        maskT = area_p[:, 5376:5632]
        probT = area_p[:, 5632:5888]
        ysum = area_p[:, 5888:6144].rearrange("p (t n) -> p t n", t=TQ)
        yT = area_p[:, 0:256]
        latT = area_p[:, 5888:6144]
        raw = area_v[:, 0:NT * P].rearrange("p (n d) -> p n d", n=NT)
        raw_kv = area_p[:, 0:2048].rearrange("p (a n d) -> p a n d", a=2, d=P)
        gate0_raw = area_p[0:E, 3072:3072 + P]
        raw_q = area_p[:, 2048:3072].rearrange("p (n d) -> p n d", d=P)

        ps = ctx.enter_context(nc.psum_tensor("ps", [P, 8 * BANK], F32))

        def bank(i, n=1):
            return ps[:, i * BANK:(i + n) * BANK]

        def q_bank(m):
            return bank(6 + m)[:, 0:NQ] if m < 2 else bank(6 + (m - 1) % 2)[:, NQ:2 * NQ]

        STACK_PAIR = 7680 // (2 * NK)
        KEY_ORDER = [("stack", 0), ("stack", 1), ("keys", 0), ("keys", 1), ("stack", 2), ("stack", 3)]
        for n in range(2, STACK_PAIR):
            KEY_ORDER += [("keys", n), ("stack", 2 * n), ("stack", 2 * n + 1)]
        KEY_ORDER += [("stack", h) for h in range(2 * STACK_PAIR, H)]

        CN_HEAD = H - 5
        STACK_BANK = (2, 3, 6, 7)
        KEY_BANK = (0, 1, 4, 5, 0, 6, 7, 6)
        V_BANK = (4, 6, 0, 2, 3, 4)
        KLAT_BANK = (3, 4, 5, 6)

        s_first = signal("s_first")
        s_bias = signal("s_bias")
        s_raw = signal("s_raw")
        s_rawkv = signal("s_rawkv")
        s_small = signal("s_small")
        s_zero = signal("s_zero")
        s_const = signal("s_const")
        s_wT = signal("s_wT")
        s_wT_copied = signal("s_wT_copied")
        s_whigh = signal("s_whigh")
        s_wlow = signal("s_wlow")
        s_scaled = signal("s_scaled")
        s_tanh = signal("s_tanh")
        s_x = signal("s_x", 16)
        s_ctx = signal("s_ctx", 16)
        s_w2 = signal("s_w2", 16 * FC)
        s_out = signal("s_out", 16, before=1)
        e_xT0 = signal("e_xT0", 1)
        e_xT = signal("e_xT", 3)
        e_ctxT = signal("e_ctxT", 1)
        e_cnT = signal("e_cnT", 1)
        e_qkv0 = signal("e_qkv0", 1)
        e_k = signal("e_k", NPAIR)
        e_kq = signal("e_kq", H)
        e_max0 = signal("e_max0", H)
        e_st0 = signal("e_st0", 2 * H)
        e_pv0 = signal("e_pv0", NQUAD)
        e_o0 = signal("e_o0", 3)
        e_route0 = signal("e_route0", 3)
        e_pre0 = signal("e_pre0", 4)
        e_down0 = signal("e_down0", 2)
        e_z = signal("e_z", 2)
        e_v = signal("e_v", TK)
        e_klat = signal("e_klat", 4)
        e_q = signal("e_q", NPAIR)
        e_max1 = signal("e_max1", H)
        e_st1 = signal("e_st1", 3 * H)
        e_pv1 = signal("e_pv1", NPAIR)
        e_den1 = signal("e_den1", NPAIR)
        e_y1 = signal("e_y1", 2)
        e_route1 = signal("e_route1", 5)
        e_pre1 = signal("e_pre1", 2)
        e_out1 = signal("e_out1", 2)
        a_xT0 = signal("a_xT0", 1)
        a_xT = signal("a_xT", 2)
        a_ctxT = signal("a_ctxT", 1)
        a_cH = signal("a_cH", 1)
        a_kH = signal("a_kH", NPAIR)
        a_kq = signal("a_kq", H // 2)
        a_exp0 = signal("a_exp0", 2 * H)
        a_o0 = signal("a_o0", NQUAD)
        a_oT = signal("a_oT", 1)
        a_ratio = signal("a_ratio", 1)
        a_silu = signal("a_silu", 4)
        a_zT = signal("a_zT", 1)
        a_v = signal("a_v", TK)
        a_latH = signal("a_latH", 1)
        a_klat = signal("a_klat", 4)
        a_qH = signal("a_qH", NPAIR)
        a_exp1 = signal("a_exp1", 3 * H)
        a_yT = signal("a_yT", 1)
        a_sm = signal("a_sm", 1)
        a_maskT = signal("a_maskT", 1)
        a_gelu = signal("a_gelu", 2)
        d_xn0 = signal("d_xn0", 1)
        d_xn = signal("d_xn", 3)
        d_cn = signal("d_cn", 1)
        d_cL = signal("d_cL", 1)
        d_qkv0 = signal("d_qkv0", 1)
        d_stack = signal("d_stack", 1)
        d_kL = signal("d_kL", NPAIR)
        d_kq = signal("d_kq", H // 2)
        d_max0 = signal("d_max0", H)
        d_o0 = signal("d_o0", 1)
        d_x = signal("d_x", 4, before=1)
        d_gap = signal("d_gap", 1)
        d_exm = signal("d_exm", 1)
        d_um = signal("d_um", 2)
        d_hid0 = signal("d_hid0", 4)
        d_zm = signal("d_zm", 1)
        d_latT = signal("d_latT", 1)
        d_latL = signal("d_latL", 1)
        d_klat = signal("d_klat", 4)
        d_qL = signal("d_qL", NPAIR)
        d_max1 = signal("d_max1", H)
        d_diag1 = signal("d_diag1", H)
        d_o1 = signal("d_o1", NPAIR)
        d_smax = signal("d_smax", 1)
        d_prob = signal("d_prob", 1)
        d_mask = signal("d_mask", 1)
        d_xm = signal("d_xm", 2)
        g_cn = signal("g_cn", 1)
        g_diag0 = signal("g_diag0", H)
        g_pad = signal("g_pad", 1)
        g_sum = signal("g_sum", H - 2, before=1)
        DVE_STEPS, DVE_AHEAD_STEPS = 148, 67
        d_step = signal("d_step", DVE_STEPS)
        d_ahead = signal("d_ahead", DVE_AHEAD_STEPS)
        d_sel = signal("d_sel", 1, before=1)
        g_step = signal("g_step", 2 * (H - 2) + 1)
        g_ahead = signal("g_ahead", 1)

        x_v = x_d.rearrange("b (t p) d -> b p t d", p=P)
        ctx_v = ctx_d.rearrange("b (t p) d -> b p t d", p=P)
        out_v = out.rearrange("b (t p) d -> b p t d", p=P)

        def row(a, n):
            return a.rearrange("(o n) -> o n", o=1).to_broadcast([P, n])

        block = ctx.enter_context(nc.Block())

        @block.sync
        def _(sp):
            W = t_in
            first = [
                (raw[:, W_Q0, :], W["L0_xattn_Wq"]),
                (raw[:, W_K0:W_V0 + 1, :], W["L0_xattn_Wkv"].rearrange("(n p) d -> p n d", p=P)),
                (raw[:, W_PROJ, :], W["L0_xattn_Wproj"]),
            ]
            raw_loads = [
                (raw[:, W_GATE:W_GATE + FC, :], W["L0_ffn_w_gate"].rearrange("(n p) d -> p n d", p=P)),
                (raw[:, W_UP:W_UP + FC, :], W["L0_ffn_w_up"].rearrange("(n p) d -> p n d", p=P)),
                (raw[:, W_DOWN:W_DOWN + 2 * FC, :].rearrange("p (c a) d -> p c a d", a=2)[:, :, 0, :],
                 W["L0_ffn_w_down"].rearrange("d (c f) -> d c f", f=P)),
                (raw[:, W_DOWN:W_DOWN + 2 * FC, :].rearrange("p (c a) d -> p c a d", a=2)[:, :, 1, :],
                 W["L0_ffn_A2"].rearrange("e r (c f) -> (e r) c f", f=P)),
                (raw[:, W_A1, :], W["L0_ffn_A1"].rearrange("e r d -> (e r) d")),
                (raw[:, W_A3, :], W["L0_ffn_A3"].rearrange("e r d -> (e r) d")),
                (raw[:, W_B2, :].rearrange("p (e r) -> p e r", e=E), W["L0_ffn_B2"].rearrange("e d r -> d e r")),
                (gate0_raw, W["L0_ffn_gate_w"]),
            ]
            for c in range(FC):
                for to, name in ((W_B1, "L0_ffn_B1"), (W_B3, "L0_ffn_B3")):
                    raw_loads.append((raw[:, to + c, :].rearrange("p (e r) -> p e r", e=E),
                                      W[name][:, c * P:(c + 1) * P, :].rearrange("e f r -> f e r")))
            bias = [
                (bq0[:, :], row(W["L0_xattn_bq"], P)),
                (bkv0[:, :, :].rearrange("p a d -> p (a d)"), row(W["L0_xattn_bkv"], 2 * P)),
                (lnm_g[:, :], row(W["L1_xattn_ln_m_g"], P)), (lnm_b[:, :], row(W["L1_xattn_ln_m_b"], P)),
                (kg0[:, :], row(W["L0_xattn_k_gamma"], D0)), (kb0[:, :], row(W["L0_xattn_k_beta"], D0)),
                (qg0[:, :], row(W["L0_xattn_q_gamma"], D0)), (qb0[:, :], row(W["L0_xattn_q_beta"], D0)),
            ]
            small = [
                (bproj0[:, :], row(W["L0_xattn_bproj"], P)),
                (lnl_g[:, :], W["L1_xattn_ln_l_g"].rearrange("(p o) -> p o", o=1)),
                (lnl_b[:, :], W["L1_xattn_ln_l_b"].rearrange("(p o) -> p o", o=1)),
                (gates_raw[:, 0:2], row(W["g_xattn"], 2)), (gates_raw[:, 2:4], row(W["g_ffn"], 2)),
                (gate1[:, :], W["L1_ffn_gate_w"]),
                (gate1_b[:, :], W["L1_ffn_gate_b"].rearrange("(e o) -> e o", o=1)),
                (b1[0:E, :], W["L1_ffn_b1"]), (b2[0:E, :], W["L1_ffn_b2"]),
                (wout[:, :, :], W["L1_xattn_Wout"].rearrange("(n p) d -> p n d", p=P)),
                (w1[:, :, :], W["L1_ffn_W1"].rearrange("e d f -> d e f")),
            ]
            assert (len(first), len(bias), len(raw_loads), len(small)) == (
                FIRST_LOADS, BIAS_LOADS, RAW_LOADS, SMALL_LOADS)
            sp.dma_start(x_in[:, :, :], x_v[0]).then_inc(s_x.sem, 16)
            sp.dma_start(ctx_in[:, :, :], ctx_v[0]).then_inc(s_ctx.sem, 16)
            for to, of in first:
                sp.dma_start(to, of).then_inc(s_first.sem, 16)
            for to, of in bias:
                sp.dma_start(to, of).then_inc(s_bias.sem, 16)
            sp.dma_start(raw_kv[:, :, :, :],
                         W["L1_xattn_Wkv"].rearrange("d (a n m) -> d a n m", a=2, m=P)).then_inc(s_rawkv.sem, 16)
            sp.dma_start(raw_q[:, :, :],
                         W["L1_xattn_Wq"].rearrange("d (n m) -> d n m", m=P)).then_inc(s_rawkv.sem, 16)
            for to, of in raw_loads:
                sp.dma_start(to, of).then_inc(s_raw.sem, 16)
            sp.wait_ge(s_zero.sem, 1)
            for to, of in small:
                sp.dma_start(to, of).then_inc(s_small.sem, 16)

            def batch(b, last):
                if not last:
                    sp.wait_ge(d_x.sem, d_x.after(b, 1))
                    sp.dma_start(x_in[:, :, :], x_v[b + 1]).then_inc(s_x.sem, 16)
                    sp.dma_start(ctx_in[:, :, :], ctx_v[b + 1]).then_inc(s_ctx.sem, 16)
                sp.wait_ge(e_pv1.sem, e_pv1.after(b, NPAIR))
                for c in range(FC):
                    sp.dma_start(w2[:, c, :].rearrange("p (e d) -> p e d", e=E),
                                 t_in["L1_ffn_W2"][:, c * P:(c + 1) * P, :].rearrange("e f d -> f e d")
                                 ).then_inc(s_w2.sem, 16)
                sp.wait_ge(d_x.sem, d_x.after(b, 4))
                sp.dma_start(out_v[b], xr[:, :, :]).then_inc(s_out.sem, 16)

            with sp.Fori(0, B - 1) as b:
                batch(b, False)
            batch(B - 1, True)
            sp.wait_ge(s_out.sem, s_out.after(B, 0))

        @block.gpsimd
        def _(pool):
            pool.memset(ident[:, :], 0.0).then_inc(s_const.sem, 1)
            pool.wait_ge(s_const.sem, 1)
            pool.affine_select(out=ident[:, :], in_=ident[:, :], compare_op=ALU.not_equal, fill=1.0, base=0,
                               pattern=[[-1, P]], channel_multiplier=1).then_inc(s_const.sem, 1)
            pool.memset(v0[:, :, :], 1.0)
            pool.memset(b1[:, :], 0.0)
            pool.memset(b2[:, :], 0.0).then_inc(s_zero.sem, 1)
            pool.memset(onesb[:, :], 1.0)
            pool.memset(onesf[:, :], 1.0)
            pool.iota(iota_col[:, :], [[1, P]], base=0, channel_multiplier=0, allow_small_or_imprecise_dtypes=True)
            pool.iota(iota_er[:, :, :], [[1, E], [0, R]], base=0, channel_multiplier=0,
                      allow_small_or_imprecise_dtypes=True)
            pool.iota(iota_ed[:, :, :], [[1, E], [0, P]], base=0, channel_multiplier=0,
                      allow_small_or_imprecise_dtypes=True)
            pool.wait_ge(s_const.sem, 2)
            pool.tensor_copy(identb[:, :], ident[:, :])
            pool.tensor_scalar(negidentb[:, :], ident[:, :], -1.0, None, ALU.mult).then_inc(s_const.sem, 1)
            pool.memset(psum_1[:, 0, 0:1], 0.0).then_inc(g_sum.sem, 1)

            def context_ahead(n):
                pool.wait_ge(d_cn.sem, d_cn.after(n, 1))
                pool.tensor_tensor(cn[:, :, :], cn[:, :, :],
                                   lnm_g[:, :].rearrange("p (o d) -> p o d", o=1).to_broadcast([P, TC, P]),
                                   ALU.mult).then_inc(g_ahead.sem, 1)
                pool.wait_ge(g_ahead.sem, g_ahead.after(n, 1))
                pool.tensor_tensor(cn[:, :, :], cn[:, :, :],
                                   lnm_b[:, :].rearrange("p (o d) -> p o d", o=1).to_broadcast([P, TC, P]),
                                   ALU.add).then_inc(g_cn.sem, 1)

            def pad_ahead():
                pool.memset(stack[:, :, SR:SK], 0.0).then_inc(g_pad.sem, 1)

            pool.wait_ge(s_bias.sem, 16 * BIAS_LOADS)
            context_ahead(0)
            pool.wait_ge(s_whigh.sem, 1)
            pool.tensor_tensor(wkv_l[:, 0, :, :], raw_kv[:, 0, :, :], wkv_h[:, 0, :, :],
                               ALU.subtract).then_inc(s_wlow.sem, 1)
            pad_ahead()
            pool.tensor_tensor(wkv_l[:, 1, :, :], raw_kv[:, 1, :, :], wkv_h[:, 1, :, :],
                               ALU.subtract).then_inc(s_wlow.sem, 1)
            pool.tensor_tensor(wq_l[:, :, :], raw_q, wq_h[:, :, :], ALU.subtract).then_inc(s_wlow.sem, 1)

            def batch(b, last):
                for h in range(H):
                    pool.wait_ge(d_max0.sem, d_max0.after(b, h + 1))
                    if h >= DG0:
                        pool.wait_ge(e_st0.sem, e_st0.after(b, 2 * (h - DG0 + 1)))
                    pool.tensor_tensor(
                        diag[:, h % DG0, :, :],
                        negidentb[:, :].rearrange("p (o q) -> p o q", o=1).to_broadcast([P, TQ, P]),
                        rowmax[:, h % RM0, :].rearrange("p (t o) -> p t o", o=1).to_broadcast([P, TQ, P]),
                        ALU.mult).then_inc(g_diag0.sem, 1)
                for h in range(H - 2):
                    pool.wait_ge(a_exp1.sem, a_exp1.after(b, 3 * h + 3))
                    pool.wait_ge(g_sum.sem, g_sum.after(b, h))
                    e = p1[:, h % PR1, :]
                    pool.tensor_tensor(psum_a, e[:, 0:768], e[:, 768:1536], ALU.add).then_inc(g_step.sem, 1)
                    pool.wait_ge(g_step.sem, g_step.after(b, 1 + 2 * h))
                    if h >= 2:
                        pool.wait_ge(e_den1.sem, e_den1.after(b, h // 2))
                    pool.tensor_tensor(psum_a[:, 0:256], psum_a[:, 0:256], psum_a[:, 256:512],
                                       ALU.add).then_inc(g_step.sem, 1)
                    pool.wait_ge(g_step.sem, g_step.after(b, 2 + 2 * h))
                    pool.tensor_tensor(psum_1[:, h % 2, :], psum_a[:, 0:256], psum_a[:, 512:768],
                                       ALU.add).then_inc(g_sum.sem, 1)
                    if h == CN_HEAD and not last:
                        context_ahead(b + 1)
                if not last:
                    pool.wait_ge(a_exp1.sem, a_exp1.after(b, 3 * H))
                    pool.tensor_tensor(scratch_g[:, :], onesf[:, 0:1], onesf[:, 0:1], ALU.add).then_inc(g_step.sem, 1)
                    pad_ahead()

            with pool.Fori(0, B - 1) as b:
                batch(b, False)
            batch(B - 1, True)

        @block.scalar
        def _(act):
            def copy(to, of):
                return act.activation(to, of, ACT.Copy)

            def weights_out(n):
                act.wait_ge(s_wT.sem, n + 1)
                k = min(4, NT - 4 * n)
                copy(wt[:, 4 * n:4 * n + k, :].rearrange("p n d -> p (n d)"),
                     bank(6 + n % 2)[:, 0:k * P]).then_inc(s_wT_copied.sem, 1)

            weights_out(0)
            def operands_ahead(n):
                act.wait_ge(e_xT0.sem, e_xT0.after(n, 1))
                copy(xT0[:, :], bank(0)[:, 0:NQ]).then_inc(a_xT0.sem, 1)
                act.wait_ge(e_ctxT.sem, e_ctxT.after(n, 1))
                copy(ctxT[:, :], bank(1)).then_inc(a_ctxT.sem, 1)
                act.wait_ge(e_cnT.sem, e_cnT.after(n, 1))
                copy(kv_h[:, 0:NC_], bank(2)).then_inc(a_cH.sem, 1)

            operands_ahead(0)
            act.wait_ge(s_rawkv.sem, 32)
            copy(wkv_h[:, :, :, :], raw_kv)
            copy(wq_h[:, :, :], raw_q).then_inc(s_whigh.sem, 1)
            for n in range(1, 8):
                weights_out(n)
            act.wait_ge(s_wT.sem, 9)
            copy(gate0[:, :], bank(6)[:, 0:E]).then_inc(s_wT_copied.sem, 1)
            act.wait_ge(s_small.sem, 16 * SMALL_LOADS)
            act.activation(gates[:, :], gates_raw[:, :], ACT.Tanh).then_inc(s_tanh.sem, 1)

            def batch(b, last):
                def keys_high(p):
                    act.wait_ge(e_k.sem, e_k.after(b, p + 1))
                    src = bank(KEY_BANK[p])
                    copy(keys[0:D1, 2 * p, 0:NC_], src[0:D1, :])
                    copy(keys[D1:P, 2 * p + 1, 0:NC_], src[D1:P, :]).then_inc(a_kH.sem, 1)

                for kind, n in KEY_ORDER:
                    if kind == "stack" and n % 2 == 0:
                        act.wait_ge(e_kq.sem, e_kq.after(b, n + 1))
                        copy(kq[0:SK, n, :],
                             bank(STACK_BANK[n % 4])[0:SK, 0:384].bitcast(BF16)).then_inc(a_kq.sem, 1)
                    if kind == "keys":
                        keys_high(n)
                for h in range(H):
                    if h >= PR0:
                        act.wait_ge(e_pv0.sem, e_pv0.after(b, (h - PR0) // QUAD + 1))
                    for half in range(2):
                        act.wait_ge(e_st0.sem, e_st0.after(b, 2 * h + half + 1))
                        act.activation(p0[:, h % PR0, 2 * half:2 * half + 2, :].rearrange("p k q -> p (k q)"),
                                       bank(4 + half), ACT.Exp).then_inc(a_exp0.sem, 1)
                    if STACK_PAIR + h < NPAIR:
                        keys_high(STACK_PAIR + h)
                    if h % QUAD == 2 and h > QUAD:
                        g = h // QUAD - 1
                        act.wait_ge(e_pv0.sem, e_pv0.after(b, g + 1))
                        copy(o0[:, g, :], bank(6 + g % 2)[:, 0:NQ]).then_inc(a_o0.sem, 1)
                act.wait_ge(e_pv0.sem, e_pv0.after(b, NQUAD))
                copy(o0[:, NQUAD - 1, :], bank(6 + (NQUAD - 1) % 2)[:, 0:NQ]).then_inc(a_o0.sem, 1)

                def values_out(t):
                    act.wait_ge(e_v.sem, e_v.after(b, t + 1))
                    copy(v1[:, t, :], bank(V_BANK[t], 2)).then_inc(a_v.sem, 1)

                values_out(0)
                act.wait_ge(e_o0.sem, e_o0.after(b, 2))
                copy(o0_T, bank(2)[:, 0:NQ]).then_inc(a_oT.sem, 1)
                values_out(1)
                values_out(2)
                act.wait_ge(e_xT.sem, e_xT.after(b, 1))
                copy(xT[:, :], bank(4)[:, 0:NQ]).then_inc(a_xT.sem, 1)
                values_out(3)
                act.wait_ge(d_gap.sem, d_gap.after(b, 1))
                act.activation(wsel[:, 1, :], wsel[:, 0, :], ACT.Exp).then_inc(a_ratio.sem, 1)
                for s in range(4):
                    act.wait_ge(e_pre0.sem, e_pre0.after(b, s + 1))
                    if s >= 2:
                        act.wait_ge(d_hid0.sem, d_hid0.after(b, s - 1))
                    act.activation(sg[:, s % 2, :], bank(s % 2), ACT.Silu).then_inc(a_silu.sem, 1)
                act.wait_ge(e_z.sem, e_z.after(b, 1))
                copy(zT, bank(6)[:, 0:NQ]).then_inc(a_zT.sem, 1)
                act.wait_ge(d_latT.sem, d_latT.after(b, 1))
                copy(kv_h[:, NC_:NK], latT).then_inc(a_latH.sem, 1)

                def keys_of_latents(r):
                    act.wait_ge(e_klat.sem, e_klat.after(b, r + 1))
                    src = bank(KLAT_BANK[r]).rearrange("p (n q) -> p n q", n=2)
                    copy(keys[0:D1, 4 * r:4 * r + 4:2, NC_:NK], src[0:D1, :, :])
                    copy(keys[D1:P, 4 * r + 1:4 * r + 4:2, NC_:NK], src[D1:P, :, :]).then_inc(a_klat.sem, 1)

                def q_high(m):
                    act.wait_ge(e_q.sem, e_q.after(b, m + 1))
                    if m >= 2:
                        act.wait_ge(e_st1.sem, e_st1.after(b, 3 * (2 * m - 2)))
                    for n in range(2):
                        for half in range(2):
                            ins = copy(q_h[half * D1:(half + 1) * D1, m % 2, n, :],
                                       q_bank(m)[n * D1:(n + 1) * D1, :])
                    ins.then_inc(a_qH.sem, 1)

                keys_of_latents(0)
                q_high(0)
                keys_of_latents(1)
                keys_of_latents(2)
                values_out(TC)
                keys_of_latents(3)
                q_high(1)
                values_out(TC + 1)
                for i in range(1, H + 1):
                    h = i - 1
                    if h >= PR1:
                        act.wait_ge(e_pv1.sem, e_pv1.after(b, (h - PR1) // 2 + 1))
                        act.wait_ge(g_sum.sem, g_sum.after(b, h - PR1 + 1))
                    for n in range(3):
                        act.wait_ge(e_st1.sem, e_st1.after(b, 3 * h + n + 1))
                        act.activation(p1[:, h % PR1, n * BANK:(n + 1) * BANK], bank(3 + n), ACT.Exp,
                                       scale=SCALE1).then_inc(a_exp1.sem, 1)
                    if i % 2 == 0 and (i - 2) // 2 + 2 < NPAIR:
                        q_high((i - 2) // 2 + 2)
                if not last:
                    operands_ahead(b + 1)
                act.wait_ge(e_y1.sem, e_y1.after(b, 1))
                copy(yT, bank(0)[:, 0:NQ]).then_inc(a_yT.sem, 1)
                act.wait_ge(e_xT.sem, e_xT.after(b, 3))
                copy(xT[:, :], bank(2)[:, 0:NQ]).then_inc(a_xT.sem, 1)
                act.wait_ge(d_smax.sem, d_smax.after(b, 1))
                act.activation(probT[0:E, :], probT[0:E, :], ACT.Exp, bias=sm[:, 1:2],
                               accum_out=sm[:, 2:3]).then_inc(a_sm.sem, 1)
                act.wait_ge(e_route1.sem, e_route1.after(b, 3))
                copy(maskT, bank(5)[:, 0:NQ]).then_inc(a_maskT.sem, 1)
                for n in range(2):
                    act.wait_ge(e_pre1.sem, e_pre1.after(b, n + 1))
                    act.activation(hid1[:, 2 * n:2 * n + 2, :].rearrange("p c q -> p (c q)"), bank(2 + n),
                                   ACT.Gelu).then_inc(a_gelu.sem, 1)

            with act.Fori(0, B - 1) as b:
                batch(b, False)
            batch(B - 1, True)

        @block.vector
        def _(dve):
            dve.memset(scratch[:, 0:1], 0.0).then_inc(d_x.sem, 1)
            dve.memset(wsel[:, 0, 0:1], 0.0).then_inc(s_out.sem, 1)
            dve.memset(scratch[:, 1:2], 0.0).then_inc(d_sel.sem, 1)
            dve.wait_ge(d_x.sem, 1)
            dve.wait_ge(d_sel.sem, 1)

            count = {d_step: 0, d_ahead: 0}
            own_signal = [d_ahead, 0]

            def step(ins):
                count[own_signal[0]] += 1
                ins.then_inc(own_signal[0].sem, 1)

            def own():
                signal, n = own_signal
                dve.wait_ge(signal.sem, signal.after(n, count[signal]))

            def own_first():
                own()
                c = 0 if own_signal[0] is d_step else 1
                step(dve.memset(scratch[:, c:c + 1], 0.0))

            def then(ins):
                step(ins)
                own()

            def rsqrt(vh, y, t, columns=True):
                then(dve.tensor_scalar(t.bitcast(I32), vh.bitcast(I32), 1, None, ALU.arith_shift_right))
                then(dve.tensor_scalar(y.bitcast(I32), t.bitcast(I32), -1.0,
                                       float(RSQRT_MAGIC - (1 << 22) - (1 << 30)), ALU.mult, ALU.add))
                for _ in range(3):
                    if columns:
                        for c in range(y.shape[1]):
                            y_c = y[:, c:c + 1]
                            step(dve.scalar_tensor_tensor(out=t[:, c:c + 1], in0=y_c, scalar=y_c,
                                                          in1=vh[:, c:c + 1], op0=ALU.mult, op1=ALU.mult))
                        own()
                    else:
                        then(dve.tensor_tensor(t, y, y, ALU.mult))
                        then(dve.tensor_tensor(t, t, vh, ALU.mult))
                    then(dve.scalar_tensor_tensor(out=y, in0=t, scalar=1.5, in1=y, op0=ALU.add, op1=ALU.mult))

            def moments_of(of, tiles, st, mo):
                for t in range(tiles):
                    step(dve.bn_stats(st[:, t, :], of[:, t, :]))
                own_first()
                for t in range(tiles):
                    step(dve.bn_aggr(mo[:, t, :], st[:, t, :]))
                own()

            def normalise(to, of, tiles, mo, r):
                for t in range(tiles):
                    ins = dve.tensor_scalar(to[:, t, :], of[:, t, :], mo[:, t, 0:1], r[:, t:t + 1],
                                            ALU.subtract, ALU.mult)
                    if t < tiles - 1:
                        step(ins)
                return ins

            def layernorm(to, of, twice=False):
                moments_of(of, TQ, stats, moments)
                vh, y, tmp = (a[:, :] for a in rs_small)
                if twice:
                    then(dve.tensor_scalar(vh, moments[:, :, 1], -0.5 * (1.0 + EPS), -0.5 * EPS * EPS,
                                           ALU.mult, ALU.add))
                else:
                    then(dve.tensor_scalar(vh, moments[:, :, 1], EPS, -0.5, ALU.add, ALU.mult))
                rsqrt(vh, y, tmp)
                return normalise(to, of, TQ, moments, y)

            def wide(a, n, m):
                return a.rearrange("p (o d) -> p o d", o=1).to_broadcast([P, n, m])

            def groups(a):
                return a.rearrange("p (g o) -> p g o", o=1).to_broadcast([P, G0, D0])

            def tokens_ahead(n, part):
                held = list(own_signal)
                own_signal[:] = d_ahead, n
                vh, y, tmp = (a[:, :] for a in rs0)
                if part == 0:
                    count[d_ahead] = 0
                    dve.wait_ge(s_x.sem, s_x.after(n, 16))
                    dve.wait_ge(s_ctx.sem, s_ctx.after(n, 16))
                    for t in range(TQ):
                        step(dve.bn_stats(stats0[:, t, :], x_in[:, t, :]))
                    for t in range(TC):
                        step(dve.bn_stats(stats0[:, TQ + t, :], ctx_in[:, t, :]))
                elif part == 1:
                    own_first()
                    for t in range(TK):
                        step(dve.bn_aggr(moments0[:, t, :], stats0[:, t, :]))
                    own()
                    then(dve.tensor_scalar(vh, moments0[:, :, 1], EPS, -0.5, ALU.add, ALU.mult))
                    rsqrt(vh, y, tmp, columns=False)
                else:
                    normalise(xn0, x_in, TQ, moments0, y).then_inc(d_xn0.sem, 1)
                    normalise(cn, ctx_in, TC, moments0[:, TQ:TK, :], y[:, TQ:TK]).then_inc(d_cn.sem, 1)
                own_signal[:] = held

            def context_low_ahead(n):
                dve.wait_ge(a_cH.sem, a_cH.after(n, 1))
                dve.tensor_tensor(kv_l[:, 0:NC_], bank(2), kv_h[:, 0:NC_], ALU.subtract).then_inc(d_cL.sem, 1)

            def qkv_ahead(n):
                held = list(own_signal)
                own_signal[:] = d_ahead, n
                dve.wait_ge(e_qkv0.sem, e_qkv0.after(n, 1))
                k_tiles = qk[:, 0:TC * H, :].rearrange("p (t h) d -> p t (h d)", t=TC)
                q_tiles = qk[:, TC * H:G0, :].rearrange("p (t h) d -> p t (h d)", t=TQ)
                kv_ps = bank(4, 2).rearrange("p (t a d) -> p t a d", t=TC, a=2)
                step(dve.tensor_tensor(q_tiles, bank(3)[:, 0:NQ].rearrange("p (t d) -> p t d", t=TQ),
                                       wide(bq0[:, :], TQ, P), ALU.add))
                step(dve.tensor_tensor(k_tiles, kv_ps[:, :, 0, :], wide(bkv0[:, 0, :], TC, P), ALU.add))
                for t in range(TC):
                    ins = dve.tensor_tensor(
                        v0[:, t, 0:H * V0W].rearrange("p (h d) -> p h d", h=H)[:, :, 0:D0],
                        kv_ps[:, t, 1, :].rearrange("p (h d) -> p h d", h=H),
                        bkv0[:, 1, :].rearrange("p (h d) -> p h d", h=H), ALU.add)
                    if t < TC - 1:
                        step(ins)
                ins.then_inc(d_qkv0.sem, 1)
                own_signal[:] = held

            def stack_ahead(n):
                held = list(own_signal)
                own_signal[:] = d_ahead, n
                own()
                dve.wait_ge(d_qkv0.sem, d_qkv0.after(n, 1))
                then(dve.tensor_reduce(hsum, qk, AX, ALU.add))
                then(dve.tensor_scalar(hsum, hsum, 1.0 / D0, None, ALU.mult))
                then(dve.tensor_tensor(qk, qk, groups(hsum), ALU.subtract))
                then(dve.tensor_tensor(qk2, qk, qk, ALU.mult))
                then(dve.tensor_reduce(hsum, qk2, AX, ALU.add))
                then(dve.tensor_scalar(hsum, hsum, 1.0 / D0, EPS, ALU.mult, ALU.add))
                then(dve.tensor_scalar(rs_wide[0], hsum, -0.5, None, ALU.mult))
                rsqrt(*rs_wide, columns=False)
                then(dve.tensor_tensor(qk, qk, groups(rs_wide[1]), ALU.mult))
                for lo, hi, g, be in ((0, TC * H, kg0, kb0), (TC * H, G0, qg0, qb0)):
                    then(dve.tensor_tensor(qk[:, lo:hi, :], qk[:, lo:hi, :], wide(g[:, :], hi - lo, D0), ALU.mult))
                    then(dve.tensor_tensor(qk[:, lo:hi, :], qk[:, lo:hi, :], wide(be[:, :], hi - lo, D0), ALU.add))
                then(dve.tensor_copy(parts[:, :, 0, :], qk))
                then(dve.tensor_tensor(qk2, qk, parts[:, :, 0, :], ALU.subtract))
                then(dve.tensor_copy(parts[:, :, 1, :], qk2))
                then(dve.tensor_tensor(qk, qk2, parts[:, :, 1, :], ALU.subtract))
                then(dve.tensor_copy(parts[:, :, 2, :], qk))
                PW = NPART * D0
                for m in range(NPART):
                    step(dve.tensor_copy(stack[:, 0:TC * H, m * PW:(m + 1) * PW],
                                         parts[:, 0:TC * H, :, :].rearrange("p g s d -> p g (s d)")))
                for m in range(NPART):
                    ins = dve.tensor_copy(
                        stack[:, TC * H:G0, m * PW:(m + 1) * PW].rearrange("p g (s d) -> p g s d", s=NPART),
                        parts[:, TC * H:G0, m:m + 1, :].to_broadcast([P, TQ * H, NPART, D0]))
                    if m < NPART - 1:
                        step(ins)
                ins.then_inc(d_stack.sem, 1)
                assert count[d_ahead] == DVE_AHEAD_STEPS, count[d_ahead]
                own_signal[:] = held

            for part in range(3):
                tokens_ahead(0, part)
            context_low_ahead(0)
            dve.wait_ge(s_bias.sem, 16 * BIAS_LOADS)
            dve.tensor_scalar(qg0[:, :], qg0[:, :], SCALE0, None, ALU.mult).then_inc(s_scaled.sem, 1)
            dve.tensor_scalar(qb0[:, :], qb0[:, :], SCALE0, None, ALU.mult).then_inc(s_scaled.sem, 1)
            dve.wait_ge(s_scaled.sem, 2)
            qkv_ahead(0)
            stack_ahead(0)
            dve.wait_ge(s_small.sem, 16 * SMALL_LOADS)
            dve.wait_ge(s_tanh.sem, 1)

            def batch(b, last):
                own_signal[:] = d_step, b
                count[d_step] = 0
                def keys_low(p):
                    dve.wait_ge(a_kH.sem, a_kH.after(b, p + 1))
                    src = bank(KEY_BANK[p])
                    step(dve.tensor_tensor(keys[D1:P, 2 * p, 0:NC_], src[0:D1, :], keys[0:D1, 2 * p, 0:NC_],
                                           ALU.subtract))
                    dve.tensor_tensor(keys[0:D1, 2 * p + 1, 0:NC_], src[D1:P, :], keys[D1:P, 2 * p + 1, 0:NC_],
                                      ALU.subtract).then_inc(d_kL.sem, 1)

                for kind, n in KEY_ORDER:
                    if kind == "stack" and n % 2 == 1:
                        dve.wait_ge(e_kq.sem, e_kq.after(b, n + 1))
                        dve.tensor_copy(kq[0:SK, n, :],
                                        bank(STACK_BANK[n % 4])[0:SK, 0:384].bitcast(BF16)).then_inc(d_kq.sem, 1)
                    if kind == "keys":
                        keys_low(n)

                for h in range(H):
                    dve.wait_ge(e_max0.sem, e_max0.after(b, h + 1))
                    if h >= RM0:
                        dve.wait_ge(g_diag0.sem, g_diag0.after(b, h - RM0 + 1))
                    dve.tensor_reduce(rowmax[:, h % RM0, :],
                                      bank(2 * (h % 2), 2).rearrange("p (t k) -> p t k", t=TQ),
                                      AX, ALU.max).then_inc(d_max0.sem, 1)
                    if h >= 2 and STACK_PAIR + h - 2 < NPAIR:
                        keys_low(STACK_PAIR + h - 2)

                dve.wait_ge(e_o0.sem, e_o0.after(b, 1))
                o_ps = bank(0, 2).rearrange("p (t h c) -> p t h c", t=TQ, h=H)
                then(dve.reciprocal(rden0[:, :, :], o_ps[:, :, :, D0]))
                for t in range(TQ):
                    ins = dve.tensor_tensor(o0_tok[:, t, :].rearrange("p (h d) -> p h d", h=H), o_ps[:, t, :, 0:D0],
                                            rden0[:, t, :].rearrange("p (h o) -> p h o", o=1)
                                            .to_broadcast([P, H, D0]), ALU.mult)
                    if t < TQ - 1:
                        step(ins)
                ins.then_inc(d_o0.sem, 1)
                dve.wait_ge(s_out.sem, s_out.after(b, 0))
                then(dve.scalar_tensor_tensor(out=xr[:, :, :], in0=wide(bproj0[:, :], TQ, P), scalar=G_X0,
                                              in1=x_in[:, :, :], op0=ALU.mult, op1=ALU.add))
                dve.wait_ge(e_o0.sem, e_o0.after(b, 3))
                dve.scalar_tensor_tensor(out=xr[:, :, :], in0=bank(3)[:, 0:NQ].rearrange("p (t d) -> p t d", t=TQ),
                                         scalar=G_X0, in1=xr[:, :, :], op0=ALU.mult,
                                         op1=ALU.add).then_inc(d_x.sem, 1)

                dve.wait_ge(d_x.sem, d_x.after(b, 1))
                layernorm(xn, xr).then_inc(d_xn.sem, 1)
                dve.wait_ge(e_route0.sem, e_route0.after(b, 1))
                step(dve.tensor_copy(lg[:, :, :].rearrange("p t e -> p (t e)"), bank(5)[:, 0:TQ * E]))

                def top8(of):
                    own_first()
                    for t in range(TQ):
                        step(dve.max(top[:, t, :], of[:, t, :]))
                    own_first()
                    for t in range(TQ):
                        step(dve.max_index(topi[:, t, :], top[:, t, :], of[:, t, :]))
                    own()
                    then(dve.tensor_copy(topf[:, :, :], topi[:, :, :]))

                top8(lg)
                dve.tensor_tensor(wsel[:, 0, :], top[:, :, 1], top[:, :, 0], ALU.subtract).then_inc(d_gap.sem, 1)
                for j in range(2):
                    for t in range(TQ):
                        ins = dve.tensor_scalar(exm[:, j, t, :], iota_er[:, :, :].rearrange("p e r -> p (e r)"),
                                                topf[:, t, j:j + 1], None, ALU.is_equal)
                        if (j, t) != (1, TQ - 1):
                            step(ins)
                ins.then_inc(d_exm.sem, 1)
                dve.wait_ge(a_ratio.sem, a_ratio.after(b, 1))
                then(dve.tensor_scalar(wsel[:, 2, :], wsel[:, 1, :], 1.0, None, ALU.add))
                then(dve.reciprocal(wsel[:, 2, :], wsel[:, 2, :]))
                then(dve.tensor_tensor(wsel[:, 3, :], wsel[:, 2, :], wsel[:, 1, :], ALU.mult))
                dve.wait_ge(e_route0.sem, e_route0.after(b, 3))
                xa = bank(6).rearrange("p (u q) -> p u q", u=2)
                then(dve.tensor_scalar(exmT[:, 0, :], bank(7)[:, 0:NQ], LORA_SCALE, None, ALU.mult))
                dve.tensor_tensor(um[:, :, 0, :], xa, exmT[:, 0:1, :].to_broadcast([P, 2, NQ]),
                                  ALU.mult).then_inc(d_um.sem, 1)
                then(dve.tensor_scalar(exmT[:, 1, :], bank(7)[:, NQ:2 * NQ], LORA_SCALE, None, ALU.mult))
                dve.tensor_tensor(um[:, :, 1, :], xa, exmT[:, 1:2, :].to_broadcast([P, 2, NQ]),
                                  ALU.mult).then_inc(d_um.sem, 1)
                for s in range(4):
                    dve.wait_ge(a_silu.sem, a_silu.after(b, s + 1))
                    dve.tensor_tensor(hid0[:, s // 2, 2 * (s % 2):2 * (s % 2) + 2, :].rearrange("p c q -> p (c q)"),
                                      bank(2 + s % 2), sg[:, s % 2, :], ALU.mult).then_inc(d_hid0.sem, 1)
                for j in range(2):
                    for t in range(TQ):
                        step(dve.tensor_scalar(exm[:, j, t, :], exm[:, j, t, :], wsel[:, 2 + j, t:t + 1], LORA_SCALE,
                                               ALU.mult, ALU.mult))
                own()
                for j in range(2):
                    dve.wait_ge(e_down0.sem, e_down0.after(b, j + 1))
                    dn = bank(4 + j).rearrange("p (t a d) -> p t a d", t=TQ, a=2)
                    step(dve.tensor_tensor(zm[:, j, :, :], dn[:, :, 1, :], exm[:, j, :, :], ALU.mult))
                    for t in range(TQ):
                        if j == 0:
                            step(dve.tensor_scalar(dsum[:, t, :], dn[:, t, 0, :], wsel[:, 2, t:t + 1], None,
                                                   ALU.mult))
                        else:
                            step(dve.scalar_tensor_tensor(out=dsum[:, t, :], in0=dn[:, t, 0, :],
                                                          scalar=wsel[:, 3, t:t + 1], in1=dsum[:, t, :],
                                                          op0=ALU.mult, op1=ALU.add))
                    own()
                dve.tensor_tensor(zm[:, 0, :, :], zm[:, 0, :, :], zm[:, 1, :, :], ALU.add).then_inc(d_zm.sem, 1)
                then(dve.scalar_tensor_tensor(out=xr[:, :, :], in0=dsum, scalar=G_F0, in1=xr[:, :, :],
                                              op0=ALU.mult, op1=ALU.add))
                dve.wait_ge(e_z.sem, e_z.after(b, 2))
                dve.scalar_tensor_tensor(out=xr[:, :, :], in0=bank(7)[:, 0:NQ].rearrange("p (t d) -> p t d", t=TQ),
                                         scalar=G_F0, in1=xr[:, :, :], op0=ALU.mult,
                                         op1=ALU.add).then_inc(d_x.sem, 1)

                dve.wait_ge(d_x.sem, d_x.after(b, 2))
                layernorm(xn, xr, twice=True).then_inc(d_xn.sem, 1)
                dve.wait_ge(e_xT.sem, e_xT.after(b, 2))
                dve.tensor_scalar(latT, bank(0)[:, 0:NQ], lnl_g[:, :], lnl_b[:, :],
                                  ALU.mult, ALU.add).then_inc(d_latT.sem, 1)
                dve.wait_ge(d_latT.sem, d_latT.after(b, 1))
                dve.wait_ge(a_latH.sem, a_latH.after(b, 1))
                dve.tensor_tensor(kv_l[:, NC_:NK], latT, kv_h[:, NC_:NK], ALU.subtract).then_inc(d_latL.sem, 1)

                def keys_of_latents(r):
                    dve.wait_ge(a_klat.sem, a_klat.after(b, r + 1))
                    src = bank(KLAT_BANK[r]).rearrange("p (n q) -> p n q", n=2)
                    ev, od = slice(4 * r, 4 * r + 4, 2), slice(4 * r + 1, 4 * r + 4, 2)
                    step(dve.tensor_tensor(keys[D1:P, ev, NC_:NK], src[0:D1, :, :], keys[0:D1, ev, NC_:NK],
                                           ALU.subtract))
                    dve.tensor_tensor(keys[0:D1, od, NC_:NK], src[D1:P, :, :], keys[D1:P, od, NC_:NK],
                                      ALU.subtract).then_inc(d_klat.sem, 1)

                def q_low(m):
                    dve.wait_ge(a_qH.sem, a_qH.after(b, m + 1))
                    for n in range(2):
                        for half in range(2):
                            lo, hi = half * D1, (half + 1) * D1
                            ins = dve.tensor_tensor(q_l[lo:hi, m % 2, n, :],
                                                    q_bank(m)[n * D1:(n + 1) * D1, :],
                                                    q_h[n * D1:(n + 1) * D1, m % 2, n, :], ALU.subtract)
                            if (n, half) != (1, 1):
                                step(ins)
                    ins.then_inc(d_qL.sem, 1)

                def divide(p):
                    dve.wait_ge(e_den1.sem, e_den1.after(b, p + 1))
                    o = bank(6 + p % 2)
                    then(dve.reciprocal(o1[:, p, :], o[:, NQ:2 * NQ]))
                    dve.tensor_tensor(o1[:, p, :], o[:, 0:NQ], o1[:, p, :], ALU.mult).then_inc(d_o1.sem, 1)

                def row_max1(h):
                    dve.wait_ge(e_max1.sem, e_max1.after(b, h + 1))
                    dve.tensor_reduce(rowmax[:, h % 2, :], bank(0, 3).rearrange("p (t k) -> p t k", t=TQ),
                                      AX, ALU.max).then_inc(d_max1.sem, 1)
                    dve.wait_ge(d_max1.sem, d_max1.after(b, h + 1))
                    if h >= 2:
                        dve.wait_ge(e_st1.sem, e_st1.after(b, 3 * (h - 1)))
                    dve.tensor_tensor(
                        diag[:, h % 2, :, :],
                        negidentb[:, :].rearrange("p (o q) -> p o q", o=1).to_broadcast([P, TQ, P]),
                        rowmax[:, h % 2, :].rearrange("p (t o) -> p t o", o=1).to_broadcast([P, TQ, P]),
                        ALU.mult).then_inc(d_diag1.sem, 1)

                keys_of_latents(0)
                q_low(0)
                keys_of_latents(1)
                row_max1(0)
                keys_of_latents(2)
                keys_of_latents(3)
                q_low(1)
                for i in range(1, H + 1):
                    if i < H:
                        row_max1(i)
                    if i % 2 == 0 and i >= 6:
                        divide(i // 2 - 3)
                    if i % 2 == 0 and i // 2 + 1 < NPAIR:
                        q_low(i // 2 + 1)
                    if i in (7, 9, 11) and not last:
                        tokens_ahead(b + 1, (i - 7) // 2)
                if not last:
                    context_low_ahead(b + 1)
                divide(NPAIR - 2)
                divide(NPAIR - 1)
                if not last:
                    qkv_ahead(b + 1)
                dve.wait_ge(e_y1.sem, e_y1.after(b, 2))
                dve.scalar_tensor_tensor(out=xr[:, :, :], in0=bank(1)[:, 0:NQ].rearrange("p (t d) -> p t d", t=TQ),
                                         scalar=G_X1, in1=xr[:, :, :], op0=ALU.mult,
                                         op1=ALU.add).then_inc(d_x.sem, 1)

                dve.wait_ge(d_x.sem, d_x.after(b, 3))
                layernorm(xn, xr).then_inc(d_xn.sem, 1)
                then(dve.memset(probT, 0.0))
                dve.wait_ge(e_route1.sem, e_route1.after(b, 1))
                then(dve.tensor_scalar(probT[0:E, :], bank(2)[0:E, NQ:2 * NQ], gate1_b[:, :], None, ALU.add))
                then(dve.tensor_reduce(sm[:, 0:1], probT[0:E, :], AX, ALU.max))
                dve.tensor_scalar(sm[:, 1:2], sm[:, 0:1], -1.0, None, ALU.mult).then_inc(d_smax.sem, 1)
                dve.wait_ge(a_sm.sem, a_sm.after(b, 1))
                then(dve.reciprocal(sm[:, 3:4], sm[:, 2:3]))
                dve.tensor_scalar(probT[0:E, :], probT[0:E, :], sm[:, 3:4], None, ALU.mult).then_inc(d_prob.sem, 1)
                dve.wait_ge(e_route1.sem, e_route1.after(b, 2))
                step(dve.tensor_copy(lg[:, :, :], bank(4)[:, 0:NQ].rearrange("p (t n) -> p t n", t=TQ)[:, :, 0:E]))
                top8(lg)
                for t in range(TQ):
                    step(dve.tensor_scalar(maskb[:, t, :, :].rearrange("p e d -> p (e d)"),
                                           iota_ed[:, :, :].rearrange("p e d -> p (e d)"), topf[:, t, 0:1], None,
                                           ALU.is_equal))
                for t in range(TQ):
                    ins = dve.tensor_scalar(maskp[:, t, :], iota_col[:, :], topf[:, t, 0:1], None, ALU.is_equal)
                    if t < TQ - 1:
                        step(ins)
                ins.then_inc(d_mask.sem, 1)
                for n in range(2):
                    dve.wait_ge(e_route1.sem, e_route1.after(b, 4 + n))
                    dve.tensor_tensor(xm[:, 4 * n:4 * n + 4, :],
                                      bank((0, 6)[n], 2).rearrange("p (e q) -> p e q", e=4),
                                      xT[:, :].rearrange("p (o q) -> p o q", o=1).to_broadcast([P, 4, NQ]),
                                      ALU.mult).then_inc(d_xm.sem, 1)
                if not last:
                    stack_ahead(b + 1)
                for t in range(TQ):
                    dve.wait_ge(e_out1.sem, e_out1.after(b, t + 1))
                    then(dve.tensor_tensor(sel, bank((0, 6)[t], 2).rearrange("p (e d) -> p e d", e=E),
                                           maskp[:, t, 0:E].rearrange("p (e o) -> p e o", o=1)
                                           .to_broadcast([P, E, P]), ALU.mult))
                    then(dve.tensor_reduce(ysum[:, t, :], sel.rearrange("p e d -> p d e"), AX, ALU.add))
                    ins = dve.tensor_tensor(ysum[:, t, :], bank(4 + t)[:, 0:P], ysum[:, t, :], ALU.add)
                    if t == 0:
                        ins.then_inc(d_sel.sem, 1)
                    else:
                        then(ins)
                dve.wait_ge(d_sel.sem, d_sel.after(b, 1))
                dve.scalar_tensor_tensor(out=xr[:, :, :], in0=ysum, scalar=G_F1, in1=xr[:, :, :],
                                         op0=ALU.mult, op1=ALU.add).then_inc(d_x.sem, 1)
                assert count[d_step] == DVE_STEPS, count[d_step]

            with dve.Fori(0, B - 1) as b:
                batch(b, False)
            batch(B - 1, True)

        @block.tensor
        def _(pe):
            def mm(o, lhsT, rhs, start=True, stop=True):
                return pe.matmul(o, lhsT, rhs, start=start, stop=stop)

            def mm_split(o, lhs_hl, rhs_hl, start=True, stop=True):
                (lh, ll), (rh, rl) = lhs_hl, rhs_hl
                mm(o, lh, rh, start, False)
                mm(o, lh, rl, False, False)
                return mm(o, ll, rh, False, stop)

            def weights_in(n):
                if n >= 2:
                    pe.wait_ge(s_wT_copied.sem, n - 1)
                for m in range(4 * n, min(4 * n + 4, NT)):
                    ins = pe.transpose(bank(6 + n % 2)[:, (m % 4) * P:(m % 4 + 1) * P], raw[:, m, :], ident[:, :])
                ins.then_inc(s_wT.sem, 1)

            def tok(a, t):
                return a[:, t * P:(t + 1) * P]

            def transpose_tiles(o, of, tiles):
                for t in range(tiles):
                    ins = pe.transpose(tok(o, t), of[:, t, :], ident[:, :])
                return ins

            def transposes_ahead(n):
                pe.wait_ge(d_xn0.sem, d_xn0.after(n, 1))
                transpose_tiles(bank(0), xn0, TQ).then_inc(e_xT0.sem, 1)
                pe.wait_ge(s_ctx.sem, s_ctx.after(n, 16))
                transpose_tiles(bank(1), ctx_in, TC).then_inc(e_ctxT.sem, 1)
                pe.wait_ge(g_cn.sem, g_cn.after(n, 1))
                transpose_tiles(bank(2), cn, TC).then_inc(e_cnT.sem, 1)

            def qkv_ahead(n):
                pe.wait_ge(a_xT0.sem, a_xT0.after(n, 1))
                for t in range(TQ):
                    mm(tok(bank(3), t), tok(xT0, t), wt[:, W_Q0, :])
                pe.wait_ge(a_ctxT.sem, a_ctxT.after(n, 1))
                for t in range(TC):
                    ins = mm(bank(4, 2)[:, t * 2 * P:(t + 1) * 2 * P], tok(ctxT, t),
                             wt[:, W_K0:W_V0 + 1, :].rearrange("p n d -> p (n d)"))
                ins.then_inc(e_qkv0.sem, 1)

            pe.wait_ge(s_const.sem, 2)
            pe.wait_ge(s_first.sem, 16 * FIRST_LOADS)
            weights_in(0)
            transposes_ahead(0)
            pe.wait_ge(s_wT_copied.sem, 1)
            qkv_ahead(0)
            pe.wait_ge(s_raw.sem, 16 * RAW_LOADS)
            for n in range(1, 8):
                weights_in(n)
            pe.wait_ge(s_wT_copied.sem, 7)
            pe.transpose(bank(6)[:, 0:E], gate0_raw, ident[0:E, 0:E]).then_inc(s_wT.sem, 1)
            pe.wait_ge(s_wT_copied.sem, 9)
            pe.wait_ge(s_const.sem, 3)
            pe.wait_ge(s_wlow.sem, 3)
            pe.wait_ge(s_small.sem, 16 * SMALL_LOADS)

            def batch(b, last):
                pe.wait_ge(d_cL.sem, d_cL.after(b, 1))
                pe.wait_ge(d_stack.sem, d_stack.after(b, 1))
                pe.wait_ge(g_pad.sem, g_pad.after(b, 1))
                pe.wait_ge(d_qkv0.sem, d_qkv0.after(b, 1))
                pe.wait_ge(d_sel.sem, d_sel.after(b, 0))

                def project_keys(p):
                    mm_split(bank(KEY_BANK[p]), (wkv_h[:, 0, p, :], wkv_l[:, 0, p, :]),
                             (kv_h[:, 0:NC_], kv_l[:, 0:NC_])).then_inc(e_k.sem, 1)

                for kind, n in KEY_ORDER:
                    if kind == "stack":
                        if n == 2:
                            pe.wait_ge(d_x.sem, d_x.after(b, 0))
                        if n >= 4:
                            done = a_kq if n % 2 == 0 else d_kq
                            pe.wait_ge(done.sem, done.after(b, n // 2 - 1))
                        o = bank(STACK_BANK[n % 4])[:, 0:384].bitcast(BF16)
                        for t in range(TK):
                            ins = pe.transpose(o[0:SK, t * P:(t + 1) * P], stack[:, t * H + n, :], identb[:, :])
                        ins.then_inc(e_kq.sem, 1)
                    if kind == "keys":
                        if n >= 4:
                            pe.wait_ge(d_kL.sem, d_kL.after(b, n - 3))
                        project_keys(n)
                pe.wait_ge(a_kq.sem, a_kq.after(b, H // 2))
                pe.wait_ge(d_kq.sem, d_kq.after(b, H // 2))
                pe.wait_ge(d_kL.sem, d_kL.after(b, STACK_PAIR))

                def max0(h):
                    if h >= 2:
                        pe.wait_ge(d_max0.sem, d_max0.after(b, h - 1))
                    for t in range(TQ):
                        ins = mm(bank(2 * (h % 2) + t), kq[0:SK, h, NC_ + t * P:NC_ + (t + 1) * P],
                                 kq[0:SK, h, 0:NC_])
                    ins.then_inc(e_max0.sem, 1)

                def scores0(h):
                    pe.wait_ge(g_diag0.sem, g_diag0.after(b, h + 1))
                    for half in range(2):
                        if h >= 1:
                            pe.wait_ge(a_exp0.sem, a_exp0.after(b, 2 * h - 1 + half))
                        for k in (2 * half, 2 * half + 1):
                            o = bank(4 + half)[:, k % 2 * NQ:(k % 2 + 1) * NQ]
                            mm(o, kq[0:SK, h, k * P:(k + 1) * P], kq[0:SK, h, NC_:NK], True, False)
                            ins = mm(o, onesb[:, :], diag[:, h % DG0, :, :].rearrange("p t q -> p (t q)"), False, True)
                        ins.then_inc(e_st0.sem, 1)

                def values0(g, half):
                    pe.wait_ge(a_exp0.sem, a_exp0.after(b, 2 * QUAD * (g + 1)))
                    if g >= 2:
                        pe.wait_ge(a_o0.sem, a_o0.after(b, g - 1))
                    for k in (2 * half, 2 * half + 1):
                        for j in range(QUAD):
                            h = QUAD * g + j
                            ins = mm(bank(6 + g % 2)[32 * j:32 * j + 32, 0:NQ], v0[:, k, h * V0W:h * V0W + 32],
                                     p0[:, h % PR0, k, :], k == 0, k == TC - 1)
                    if half == 1:
                        ins.then_inc(e_pv0.sem, 1)

                def values_in(t, first):
                    for n in range(2):
                        ins = mm_split(bank(first + n), (tok(kv_h, t), tok(kv_l, t)),
                                       tuple(w[:, 1, 4 * n:4 * n + 4, :].rearrange("p n d -> p (n d)")
                                             for w in (wkv_h, wkv_l)))
                    ins.then_inc(e_v.sem, 1)

                max0(0)
                max0(1)
                for h in range(H):
                    scores0(h)
                    if h + 2 < H:
                        max0(h + 2)
                    if STACK_PAIR + h < NPAIR:
                        if STACK_PAIR + h == NPAIR - 1:
                            pe.wait_ge(d_kL.sem, d_kL.after(b, NPAIR - 2))
                        project_keys(STACK_PAIR + h)
                    if h == QUAD:
                        pe.wait_ge(d_kL.sem, d_kL.after(b, NPAIR))
                    if h % QUAD <= 1 and h >= QUAD:
                        values0(h // QUAD - 1, h % QUAD)
                values0(NQUAD - 1, 0)
                values0(NQUAD - 1, 1)
                pe.wait_ge(a_o0.sem, a_o0.after(b, NQUAD))
                pe.wait_ge(d_max0.sem, d_max0.after(b, H))
                for t in range(TQ):
                    for g in range(NQUAD):
                        ins = pe.transpose(bank(t)[:, g * P:(g + 1) * P], o0[:, g, t * P:(t + 1) * P], ident[:, :])
                ins.then_inc(e_o0.sem, 1)
                values_in(0, V_BANK[0])
                pe.wait_ge(d_o0.sem, d_o0.after(b, 1))
                transpose_tiles(bank(2), o0_tok, TQ).then_inc(e_o0.sem, 1)
                values_in(1, V_BANK[1])
                pe.wait_ge(a_oT.sem, a_oT.after(b, 1))
                for t in range(TQ):
                    ins = mm(tok(bank(3), t), tok(o0_T, t), wt[:, W_PROJ, :])
                ins.then_inc(e_o0.sem, 1)
                values_in(2, V_BANK[2])

                pe.wait_ge(d_xn.sem, d_xn.after(b, 1))
                pe.wait_ge(a_v.sem, a_v.after(b, 2))
                transpose_tiles(bank(4), xn, TQ).then_inc(e_xT.sem, 1)
                pe.wait_ge(a_xT.sem, a_xT.after(b, 1))
                for t in range(TQ):
                    ins = mm(bank(5)[:, t * E:(t + 1) * E], tok(xT, t), gate0[:, :])
                ins.then_inc(e_route0.sem, 1)
                for u, w in enumerate((W_A1, W_A3)):
                    ins = mm(bank(6)[:, u * NQ:(u + 1) * NQ], wt[:, w, :], xT[:, :])
                ins.then_inc(e_route0.sem, 1)
                values_in(3, V_BANK[3])
                pe.wait_ge(d_exm.sem, d_exm.after(b, 1))
                for j in range(2):
                    for t in range(TQ):
                        ins = pe.transpose(bank(7)[:, (j * TQ + t) * P:(j * TQ + t + 1) * P], exm[:, j, t, :],
                                           ident[:, :])
                ins.then_inc(e_route0.sem, 1)
                pe.wait_ge(d_um.sem, d_um.after(b, 1))
                pe.wait_ge(a_v.sem, a_v.after(b, TC))
                for s in range(4):
                    j = s // 2
                    if s >= 2:
                        pe.wait_ge(d_um.sem, d_um.after(b, 2))
                        pe.wait_ge(d_hid0.sem, d_hid0.after(b, s - 1))
                    for u, (wx, wb) in enumerate(((W_GATE, W_B1), (W_UP, W_B3))):
                        for c in (2 * (s % 2), 2 * (s % 2) + 1):
                            o = bank(2 * u + s % 2)[:, (c % 2) * NQ:(c % 2 + 1) * NQ]
                            mm(o, wt[:, wx + c, :], xT[:, :], True, False)
                            ins = mm(o, wt[:, wb + c, :], um[:, u, j, :], False, True)
                    ins.then_inc(e_pre0.sem, 1)
                for j in range(2):
                    pe.wait_ge(d_hid0.sem, d_hid0.after(b, 2 * j + 2))
                    for t in range(TQ):
                        for c in range(FC):
                            ins = mm(bank(4 + j)[:, t * 2 * P:(t + 1) * 2 * P], hid0[:, j, c, t * P:(t + 1) * P],
                                     wt[:, W_DOWN + 2 * c:W_DOWN + 2 * c + 2, :].rearrange("p n d -> p (n d)"),
                                     c == 0, c == FC - 1)
                    ins.then_inc(e_down0.sem, 1)
                pe.wait_ge(d_zm.sem, d_zm.after(b, 1))
                transpose_tiles(bank(6), zm[:, 0, :, :], TQ).then_inc(e_z.sem, 1)
                pe.wait_ge(a_zT.sem, a_zT.after(b, 1))
                for t in range(TQ):
                    ins = mm(tok(bank(7), t), tok(zT, t), wt[:, W_B2, :])
                ins.then_inc(e_z.sem, 1)

                pe.wait_ge(d_xn.sem, d_xn.after(b, 2))
                transpose_tiles(bank(0), xn, TQ).then_inc(e_xT.sem, 1)
                pe.wait_ge(d_latL.sem, d_latL.after(b, 1))
                lat = (kv_h[:, NC_:NK], kv_l[:, NC_:NK])

                def keys_of_latents(r):
                    for n in range(2):
                        ins = mm_split(bank(KLAT_BANK[r])[:, n * NQ:(n + 1) * NQ],
                                       (wkv_h[:, 0, 2 * r + n, :], wkv_l[:, 0, 2 * r + n, :]), lat)
                    ins.then_inc(e_klat.sem, 1)

                def project_q(m):
                    mm_split(q_bank(m), (wq_h[:, m, :], wq_l[:, m, :]), lat).then_inc(e_q.sem, 1)

                def max1(h):
                    pe.wait_ge(d_qL.sem, d_qL.after(b, h // 2 + 1))
                    if h >= 1:
                        pe.wait_ge(d_max1.sem, d_max1.after(b, h))
                    cuts = sorted({0, BANK, 2 * BANK, 3 * BANK, NK})
                    for lo, hi in zip(cuts, cuts[1:]):
                        t, k = lo // NK, lo % NK
                        ins = mm(bank(0, 3)[:, lo:hi], q_h[:, (h // 2) % 2, h % 2, t * P:(t + 1) * P],
                                 keys[:, h, k:k + hi - lo])
                    ins.then_inc(e_max1.sem, 1)

                keys_of_latents(0)
                project_q(0)
                keys_of_latents(1)
                keys_of_latents(2)
                pe.wait_ge(d_klat.sem, d_klat.after(b, 1))
                max1(0)
                pe.wait_ge(d_klat.sem, d_klat.after(b, 2))
                values_in(TC, V_BANK[TC])
                keys_of_latents(3)
                project_q(1)
                pe.wait_ge(d_klat.sem, d_klat.after(b, 3))
                pe.wait_ge(a_v.sem, a_v.after(b, TC + 1))
                values_in(TC + 1, V_BANK[TC + 1])
                pe.wait_ge(a_v.sem, a_v.after(b, TK))

                def scores1(h):
                    pe.wait_ge(d_diag1.sem, d_diag1.after(b, h + 1))
                    for n in range(3):
                        if h >= 1:
                            pe.wait_ge(a_exp1.sem, a_exp1.after(b, 3 * h - 2 + n))
                        for k in (2 * n, 2 * n + 1):
                            o = bank(3, 3)[:, k * NQ:(k + 1) * NQ]
                            mm(o, keys[:, h, k * P:(k + 1) * P], q_h[:, (h // 2) % 2, h % 2, :], True, False)
                            mm(o, keys[:, h, k * P:(k + 1) * P], q_l[:, (h // 2) % 2, h % 2, :], False, False)
                            ins = mm(o, onesb[:, :], diag[:, h % 2, :, :].rearrange("p t q -> p (t q)"), False, True)
                        ins.then_inc(e_st1.sem, 1)

                def values1(p):
                    pe.wait_ge(a_exp1.sem, a_exp1.after(b, 3 * (2 * p + 2)))
                    pe.wait_ge(d_qL.sem, d_qL.after(b, min(p + 2, NPAIR)))
                    if p >= 2:
                        pe.wait_ge(d_o1.sem, d_o1.after(b, p - 1))
                    for k in range(TK):
                        for j in range(2):
                            h = 2 * p + j
                            ins = mm(bank(6 + p % 2)[j * D1:(j + 1) * D1, 0:NQ], v1[:, k, h * D1:(h + 1) * D1],
                                     p1[:, h % PR1, k * NQ:(k + 1) * NQ], k == 0, k == TK - 1)
                    ins.then_inc(e_pv1.sem, 1)

                def sums1(p):
                    pe.wait_ge(d_qL.sem, d_qL.after(b, min(p + 4, NPAIR)))
                    if p < NPAIR - 1:
                        pe.wait_ge(g_sum.sem, g_sum.after(b, 2 * p + 2))
                        for j in range(2):
                            ins = mm(bank(6 + p % 2)[j * D1:(j + 1) * D1, NQ:2 * NQ], onesf[:, :], psum_1[:, j, :])
                    else:
                        for k in range(TK):
                            for j in range(2):
                                ins = mm(bank(6 + p % 2)[j * D1:(j + 1) * D1, NQ:2 * NQ], onesf[:, :],
                                         p1[:, (2 * p + j) % PR1, k * NQ:(k + 1) * NQ], k == 0, k == TK - 1)
                    ins.then_inc(e_den1.sem, 1)

                for i in range(H + 2):
                    if 1 <= i < H:
                        max1(i)
                    if 1 <= i <= H:
                        scores1(i - 1)
                    if i == H and not last:
                        pe.wait_ge(d_max1.sem, d_max1.after(b, H))
                        transposes_ahead(b + 1)
                    if i % 2 == 1 and i >= 3:
                        p = (i - 3) // 2
                        values1(p)
                        if p >= 1:
                            sums1(p - 1)
                        if p == NPAIR - 1:
                            sums1(p)
                    if i == 2:
                        pe.wait_ge(d_qL.sem, d_qL.after(b, 2))
                        project_q(2)
                    if i % 2 == 1 and 2 < (i + 3) // 2 < NPAIR:
                        project_q((i + 3) // 2)
                if not last:
                    qkv_ahead(b + 1)
                pe.wait_ge(d_max1.sem, d_max1.after(b, H))
                if not last:
                    pe.wait_ge(d_cL.sem, d_cL.after(b + 1, 1))
                for p in range(NPAIR):
                    pe.wait_ge(d_o1.sem, d_o1.after(b, p + 1))
                    ins = mm(bank(0)[:, 0:NQ], wout[:, p, :], o1[:, p, :], p == 0, p == NPAIR - 1)
                ins.then_inc(e_y1.sem, 1)
                pe.wait_ge(a_yT.sem, a_yT.after(b, 1))
                transpose_tiles(bank(1), yT.rearrange("p (t d) -> p t d", t=TQ), TQ).then_inc(e_y1.sem, 1)

                pe.wait_ge(d_xn.sem, d_xn.after(b, 3))
                transpose_tiles(bank(2), xn, TQ).then_inc(e_xT.sem, 1)
                pe.wait_ge(a_xT.sem, a_xT.after(b, 2))
                mm(bank(2)[0:E, NQ:2 * NQ], gate1[:, :], xT[:, :]).then_inc(e_route1.sem, 1)
                pe.wait_ge(d_prob.sem, d_prob.after(b, 1))
                if not last:
                    pe.wait_ge(d_qkv0.sem, d_qkv0.after(b + 1, 1))
                transpose_tiles(bank(4), probT.rearrange("p (t d) -> p t d", t=TQ), TQ).then_inc(e_route1.sem, 1)
                pe.wait_ge(d_mask.sem, d_mask.after(b, 1))
                transpose_tiles(bank(5), maskp, TQ).then_inc(e_route1.sem, 1)
                for n in range(2):
                    for e in range(4):
                        for t in range(TQ):
                            ins = mm(bank((0, 6)[n], 2)[:, e * NQ + t * P:e * NQ + (t + 1) * P],
                                     maskb[:, t, 4 * n + e, :], identb[:, :])
                    ins.then_inc(e_route1.sem, 1)
                pe.wait_ge(a_maskT.sem, a_maskT.after(b, 1))
                pe.wait_ge(d_xm.sem, d_xm.after(b, 2))
                for c in range(FC):
                    o = bank(2 + c // 2)[:, (c % 2) * NQ:(c % 2 + 1) * NQ]
                    for e in range(E):
                        mm(o, w1[:, e, c * P:(c + 1) * P], xm[:, e, :], e == 0, False)
                    ins = mm(o, b1[:, c * P:(c + 1) * P], maskT, False, True)
                    if c % 2 == 1:
                        ins.then_inc(e_pre1.sem, 1)
                for t in range(TQ):
                    mm(bank(4 + t)[:, 0:P], maskT[:, t * P:(t + 1) * P], b2[:, :])
                pe.wait_ge(s_w2.sem, s_w2.after(b, 16 * FC))
                pe.wait_ge(a_gelu.sem, a_gelu.after(b, 2))
                for t in range(TQ):
                    for n in range(2):
                        for c in range(FC):
                            ins = mm(bank((0, 6)[t] + n), hid1[:, c, t * P:(t + 1) * P],
                                     w2[:, c, n * BANK:(n + 1) * BANK], c == 0, c == FC - 1)
                    ins.then_inc(e_out1.sem, 1)

            with pe.Fori(0, B - 1) as b:
                batch(b, False)
            batch(B - 1, True)


FIRST_LOADS = 3
BIAS_LOADS = 8
RAW_LOADS = 16
SMALL_LOADS = 11

_INS = ['x', 'ctx_1024', 'g_xattn', 'g_ffn', 'L0_xattn_Wq', 'L0_xattn_bq', 'L0_xattn_Wkv', 'L0_xattn_bkv',
        'L0_xattn_q_gamma', 'L0_xattn_q_beta', 'L0_xattn_k_gamma', 'L0_xattn_k_beta', 'L0_xattn_Wproj',
        'L0_xattn_bproj', 'L0_ffn_gate_w', 'L0_ffn_w_gate', 'L0_ffn_w_up', 'L0_ffn_w_down', 'L0_ffn_A1',
        'L0_ffn_B1', 'L0_ffn_A3', 'L0_ffn_B3', 'L0_ffn_A2', 'L0_ffn_B2', 'L1_xattn_ln_m_g', 'L1_xattn_ln_m_b',
        'L1_xattn_ln_l_g', 'L1_xattn_ln_l_b', 'L1_xattn_Wq', 'L1_xattn_Wkv', 'L1_xattn_Wout', 'L1_ffn_gate_w',
        'L1_ffn_gate_b', 'L1_ffn_W1', 'L1_ffn_b1', 'L1_ffn_W2', 'L1_ffn_b2']
_OUT = ((4, 256, 128), 'float32')


def kernel(**inputs):
    import numpy as _np
    import concourse.bacc as _bacc
    from concourse import mybir as _mybir
    from concourse.bass_utils import run_bass_kernel_spmd as _run

    nc = _bacc.Bacc("TRN2", target_bir_lowering=False, num_devices=1)
    arrays, args = {}, {}
    for name in _INS:
        a = _np.ascontiguousarray(inputs[name])
        arrays[f"in_{name}_dram"] = a
        args[name] = nc.dram_tensor(f"in_{name}_dram", a.shape, _mybir.dt.from_np(a.dtype), kind="ExternalInput").ap()
    out = nc.dram_tensor("out_0_dram", _OUT[0], _mybir.dt.from_np(_np.dtype(_OUT[1])), kind="ExternalOutput").ap()
    flamingo(nc, args, out)
    r = _run(nc, [arrays], core_ids=[0])
    return r.results[0]["out_0_dram"]
```

```python
from contextlib import ExitStack

import concourse.bass as bass
from concourse import mybir

F32 = mybir.dt.float32
F32R = mybir.dt.float32r
BF16 = mybir.dt.bfloat16
I32 = mybir.dt.int32
U32 = mybir.dt.uint32
ALU = mybir.AluOpType
ACT = mybir.ActivationFunctionType
AX = mybir.AxisListType.X

P = 128
BANK = 512
SBUF_END = 229368
EPS = 1e-5
RSQRT_MAGIC = 0x5F3759DF


class Signal:

    def __init__(self, sem, per_batch, before=0):
        self.sem, self.per_batch, self.before = sem, per_batch, before

    def after(self, b, k):
        return b * self.per_batch + (self.before + k)


def flamingo(nc, t_in, out):
    x_d, ctx_d = t_in["x"], t_in["ctx_1024"]
    B, NQ, D = x_d.shape
    NC_ = ctx_d.shape[1]
    TQ, TC = NQ // P, NC_ // P
    TK = TC + TQ
    NK = NC_ + NQ
    H = 16
    D0 = D // H
    D1 = t_in["L1_xattn_Wq"].shape[1] // H
    E, R = t_in["L0_ffn_A1"].shape[:2]
    F = t_in["L0_ffn_w_gate"].shape[0]
    FC = F // P
    SCALE0 = float(D0) ** -0.5
    SCALE1 = float(D1) ** -0.5
    LORA_SCALE = 2.0
    NPART = 3
    SR = NPART * NPART * D0
    SK = 96
    G0 = (TC + TQ) * H
    NPAIR = H // 2
    QUAD = 4
    NQUAD = H // QUAD
    V0W = D0 + 1
    V0C = H * V0W + 32 - V0W
    PR0, PR1 = 6, 3
    RM0, DG0 = 4, 3
    V_COLS, O_COLS, P_COLS, K_COLS = TK * H * D1, NPAIR * NQ, 6144, H * NK
    V_AT = (SBUF_END - 4 * (V_COLS + O_COLS + P_COLS + K_COLS)) // 32 * 32
    O_AT = V_AT + 4 * V_COLS
    P_AT = O_AT + 4 * O_COLS
    KEYS_AT = P_AT + 4 * P_COLS
    assert D == P and E * R == P and NQ == 256 and NC_ == 512 and D1 == 64 and SR <= SK

    with ExitStack() as ctx:
        def sb(name, shape, dt=F32):
            return ctx.enter_context(nc.sbuf_tensor(name, shape, dt))

        signals = {}

        def signal(name, per_batch=0, before=0):
            s = Signal(ctx.enter_context(nc.semaphore(name)), per_batch, before)
            signals[name] = s
            return s

        ident = sb("ident", [P, P])
        identb = sb("identb", [P, P], BF16)
        negidentb = sb("negidentb", [P, P], BF16)
        onesb = sb("onesb", [P, P], BF16)
        onesf = sb("onesf", [P, D1])
        iota_er = sb("iota_er", [P, E, R])
        iota_col = sb("iota_col", [P, P])
        iota_ed = sb("iota_ed", [P, E, P], BF16)
        NT = 31
        wt = sb("wt", [P, NT, P])
        W_Q0, W_K0, W_V0, W_PROJ, W_GATE, W_UP, W_B1, W_B3, W_DOWN, W_A1, W_A3, W_B2 = (
            0, 1, 2, 3, 4, 8, 12, 16, 20, 28, 29, 30)
        gate0 = sb("gate0", [P, E])
        wkv_h = sb("wkv_h", [P, 2, NPAIR, P], F32R)
        wkv_l = sb("wkv_l", [P, 2, NPAIR, P], F32R)
        wq_h = sb("wq_h", [P, NPAIR, P], F32R)
        wq_l = sb("wq_l", [P, NPAIR, P], F32R)
        wout = sb("wout", [P, NPAIR, P])
        w1 = sb("w1", [P, E, F])
        b1 = sb("b1", [P, F])
        b2 = sb("b2", [P, P])
        gate1 = sb("gate1", [P, E])
        gate1_b = sb("gate1_b", [E, 1])
        bq0 = sb("bq0", [P, P])
        bkv0 = sb("bkv0", [P, 2, P])
        bproj0 = sb("bproj0", [P, P])
        qg0, qb0, kg0, kb0 = (sb(n, [P, D0]) for n in ("qg0", "qb0", "kg0", "kb0"))
        lnm_g, lnm_b = (sb(n, [P, P]) for n in ("lnm_g", "lnm_b"))
        lnl_g, lnl_b = (sb(n, [P, 1]) for n in ("lnl_g", "lnl_b"))
        gates_raw = sb("gates_raw", [P, 4])
        gates = sb("gates", [P, 4])
        G_X0, G_X1, G_F0, G_F1 = (gates[:, i:i + 1] for i in range(4))

        x_in = sb("x_in", [P, TQ, P])
        ctx_in = sb("ctx_in", [P, TC, P])
        xr = sb("xr", [P, TQ, P])
        xn = sb("xn", [P, TQ, P])
        xT = sb("xT", [P, NQ])
        xn0 = sb("xn0", [P, TQ, P])
        cn = sb("cn", [P, TC, P])
        xT0 = sb("xT0", [P, NQ])
        ctxT = sb("ctxT", [P, NC_])
        stats0 = sb("stats0", [P, TK, 6])
        moments0 = sb("moments0", [P, TK, 2])
        rs0 = tuple(sb(n, [P, TK]) for n in ("rs0_v", "rs0_y", "rs0_t"))
        kv_h = sb("kv_h", [P, NK], F32R)
        kv_l = sb("kv_l", [P, NK], F32R)
        v0 = sb("v0", [P, TC, V0C])
        area_k = nc.alloc_sbuf_tensor_at("area_k", [P, K_COLS], F32, offset=KEYS_AT)
        keys = nc.alloc_sbuf_tensor_at("keys", [P, H, NK], F32R, offset=KEYS_AT)
        q_h = sb("q_h", [P, 2, 2, NQ], F32R)
        q_l = sb("q_l", [P, 2, 2, NQ], F32R)
        area_v = nc.alloc_sbuf_tensor_at("area_v", [P, V_COLS], F32, offset=V_AT)
        area_o = nc.alloc_sbuf_tensor_at("area_o", [P, O_COLS], F32, offset=O_AT)
        area_p = nc.alloc_sbuf_tensor_at("area_p", [P, P_COLS], F32, offset=P_AT)
        w2_l = nc.alloc_sbuf_tensor_at("w2_l", [P, FC, E * P], F32R, offset=V_AT)
        w2_h = nc.alloc_sbuf_tensor_at("w2_h", [P, FC, E * P], F32R, offset=V_AT + 4 * FC * E * P)
        assert 2 * FC * E * P <= V_COLS + O_COLS
        hid1_l = nc.alloc_sbuf_tensor_at("hid1_l", [P, FC, NQ], F32R, offset=P_AT + 4 * 2048)
        hid1_h = nc.alloc_sbuf_tensor_at("hid1_h", [P, FC, NQ], F32R, offset=P_AT + 4 * 4096)
        stats = sb("stats", [P, TQ, 6])
        moments = sb("moments", [P, TQ, 2])
        rs_small = tuple(sb(n, [P, TQ]) for n in ("rs_v", "rs_y", "rs_t"))
        rowmax = sb("rowmax", [P, RM0, TQ])
        diag = sb("diag", [P, DG0, TQ, P], BF16)
        rden0 = sb("rden0", [P, TQ, H])
        lg = sb("lg", [P, TQ, E])
        top = sb("top", [P, TQ, 8])
        topi = sb("topi", [P, TQ, 8], U32)
        topf = sb("topf", [P, TQ, 8])
        wsel = sb("wsel", [P, 4, TQ])
        mask = sb("mask", [P, TQ, E])
        sm = sb("sm", [E, 4])
        scratch = sb("scratch", [P, 2])
        scratch_g = sb("scratch_g", [P, 1])
        assert nc.sbuf_base <= V_AT, nc.sbuf_base

        o0 = area_o[:, 0:NQUAD * NQ].rearrange("p (g q) -> p g q", g=NQUAD)
        o0_tok = area_o[:, 1024:1280].rearrange("p (t d) -> p t d", t=TQ)
        o0_T = area_o[:, 1280:1536]
        o1 = area_o[:, :].rearrange("p (h q) -> p h q", h=NPAIR)
        common = area_o[:, :].rearrange("p (u c q) -> p u c q", u=2, c=FC)
        qk = area_k[:, 4608:5376].rearrange("p (g d) -> p g d", d=D0)
        qk2 = area_k[:, 5376:6144].rearrange("p (g d) -> p g d", d=D0)
        parts = area_k[:, 6144:7296].bitcast(BF16).rearrange("p (g s d) -> p g s d", s=NPART, d=D0)
        rs_wide = tuple(area_k[:, n:n + G0] for n in range(7296, 7296 + 3 * G0, G0))
        hsum = area_k[:, 7296 + 3 * G0:7296 + 4 * G0]
        stack = area_k[:, 7680:7680 + G0 * SK // 2].bitcast(BF16).rearrange("p (g r) -> p g r", r=SK)
        kq = area_v[:, :].bitcast(BF16).rearrange("p (h n) -> p h n", h=H)
        v1 = area_v[:, :].rearrange("p (t n) -> p t n", t=TK)
        w2 = area_v[:, 0:FC * E * P].rearrange("p (c n) -> p c n", c=FC)
        p0 = area_p[:, 0:PR0 * TC * NQ].rearrange("p (s k q) -> p s k q", s=PR0, q=NQ)
        p1 = area_p[:, 0:PR1 * TK * NQ].rearrange("p (s n) -> p s n", s=PR1)
        psum_a = area_p[:, 4608:5376]
        psum_1 = area_p[:, 5376:5888].rearrange("p (s q) -> p s q", s=2)
        exm = area_p[:, 0:512].rearrange("p (j t n) -> p j t n", j=2, t=TQ)
        exmT = area_p[:, 512:1024].rearrange("p (j q) -> p j q", j=2)
        um = area_p[:, 1024:2048].rearrange("p (u j q) -> p u j q", u=2, j=2)
        hid0 = area_p[:, 2048:4096].rearrange("p (j c q) -> p j c q", j=2, c=FC)
        sg = area_p[:, 4096:5120].rearrange("p (s n) -> p s n", s=2)
        zm = area_p[:, 5120:5632].rearrange("p (j t n) -> p j t n", j=2, t=TQ)
        zT = area_p[:, 5632:5888]
        dsum = area_p[:, 5888:6144].rearrange("p (t n) -> p t n", t=TQ)
        xm = area_p[:, 0:2048].rearrange("p (e q) -> p e q", e=E)
        hid1 = area_p[:, 2048:3072].rearrange("p (c q) -> p c q", c=FC)
        maskb = area_p[:, 3072:4096].bitcast(BF16).rearrange("p (t e d) -> p t e d", t=TQ, e=E)
        sel = area_p[:, 0:(E + 1) * P].rearrange("p (e d) -> p e d", d=P)
        maskp = area_p[:, 5120:5376].rearrange("p (t n) -> p t n", t=TQ)
        maskT = area_p[:, 5376:5632]
        probT = area_p[:, 5632:5888]
        ysum = area_p[:, 5888:6144].rearrange("p (t n) -> p t n", t=TQ)
        yT = area_p[:, 0:256]
        latT = area_p[:, 5888:6144]
        late_copy = (area_p[:, 4096:4608], area_o[:, 0:512], area_o[:, 512:1024])
        klat_copy = area_p[:, 3072:4096].rearrange("p (r n) -> p r n", r=2)
        raw = area_v[:, 0:NT * P].rearrange("p (n d) -> p n d", n=NT)
        raw_kv = area_p[:, 0:2048].rearrange("p (a n d) -> p a n d", a=2, d=P)
        gate0_raw = area_p[0:E, 3072:3072 + P]
        raw_q = area_p[:, 2048:3072].rearrange("p (n d) -> p n d", d=P)

        ps = ctx.enter_context(nc.psum_tensor("ps", [P, 8 * BANK], F32))

        def bank(i, n=1):
            return ps[:, i * BANK:(i + n) * BANK]

        def q_bank(m):
            return bank(6 + m)[:, 0:NQ] if m < 2 else bank(6 + (m - 1) % 2)[:, NQ:2 * NQ]

        AHEAD_PAIRS = 2
        LOOP_KEYS = {0: 2, 1: 3, 2: 4}
        LATE_KEYS = (5, 6, 7)
        MAX_AHEAD = 3
        ACT_STACKS = (0, 1, 2, 3, 4, 6, 8, 10, 12, 14)
        TOKENS_HEAD = 3
        CN_HEAD = H - 8
        STACK_BANK = (2, 3, 0, 1, 2, 3, 0, 1, 4, 5, 6, 7, 4, 5, 6, 7)
        KEY_BANK = (6, 7, 6, 7, 6, 2, 1, 5)
        V_BANK = (4, 6, 0, 2, 3, 6)
        KLAT_BANK = (3, 4, 5, 6)
        KLAT_DVE = 2

        s_first = signal("s_first")
        s_bias = signal("s_bias")
        s_raw = signal("s_raw")
        s_rawkv = signal("s_rawkv")
        s_small = signal("s_small")
        s_zero = signal("s_zero")
        s_const = signal("s_const")
        s_v0 = signal("s_v0")
        s_wT = signal("s_wT")
        s_wT_copied = signal("s_wT_copied")
        s_whigh = signal("s_whigh")
        s_wlow = signal("s_wlow")
        s_scaled = signal("s_scaled")
        s_tanh = signal("s_tanh")
        s_x = signal("s_x", 16)
        s_ctx = signal("s_ctx", 16)
        s_w2 = signal("s_w2", 16 * FC)
        s_out = signal("s_out", 16, before=1)
        e_xT0 = signal("e_xT0", 1)
        e_xT = signal("e_xT", 3)
        e_ctxT = signal("e_ctxT", 1)
        e_cnT = signal("e_cnT", 1)
        e_qkv0 = signal("e_qkv0", 1)
        e_k = signal("e_k", NPAIR)
        e_kq = signal("e_kq", H)
        e_max0 = signal("e_max0", H)
        e_st0 = signal("e_st0", 2 * H)
        e_pv0 = signal("e_pv0", NQUAD)
        e_o0 = signal("e_o0", 3)
        e_route0 = signal("e_route0", 3)
        e_common = signal("e_common", 4)
        e_pre0 = signal("e_pre0", 4)
        e_down0 = signal("e_down0", 2)
        e_z = signal("e_z", 2)
        e_v = signal("e_v", TK)
        e_klat = signal("e_klat", 4)
        e_q = signal("e_q", NPAIR)
        e_max1 = signal("e_max1", H)
        e_st1 = signal("e_st1", 3 * H)
        e_pv1 = signal("e_pv1", NPAIR)
        e_den1 = signal("e_den1", NPAIR)
        e_y1 = signal("e_y1", 2)
        e_route1 = signal("e_route1", 5)
        e_pre1 = signal("e_pre1", 2)
        e_out1 = signal("e_out1", 4)
        a_xT0 = signal("a_xT0", 1)
        a_xT = signal("a_xT", 2)
        a_ctxT = signal("a_ctxT", 1)
        a_cH = signal("a_cH", 1)
        a_kH = signal("a_kH", NPAIR)
        a_kq = signal("a_kq", len(ACT_STACKS))
        a_exp0 = signal("a_exp0", 2 * H)
        a_o0 = signal("a_o0", NQUAD)
        a_oT = signal("a_oT", 1)
        a_ratio = signal("a_ratio", 1)
        a_common = signal("a_common", 4)
        a_silu = signal("a_silu", 4)
        a_zT = signal("a_zT", 1)
        a_v = signal("a_v", TK)
        a_latH = signal("a_latH", 1)
        a_klat = signal("a_klat", 4)
        a_qH = signal("a_qH", NPAIR)
        a_exp1 = signal("a_exp1", 3 * H)
        a_yT = signal("a_yT", 1)
        a_sm = signal("a_sm", 1)
        a_maskT = signal("a_maskT", 1)
        a_w2H = signal("a_w2H", FC)
        a_gelu = signal("a_gelu", 2)
        a_hidH = signal("a_hidH", 2)
        d_xn0 = signal("d_xn0", 1)
        d_xn = signal("d_xn", 3)
        d_cn = signal("d_cn", 1)
        d_cL = signal("d_cL", 1)
        d_qkv0 = signal("d_qkv0", 1)
        d_stack = signal("d_stack", 1)
        d_kL = signal("d_kL", NPAIR - len(LATE_KEYS))
        d_kLhalf = signal("d_kLhalf", NPAIR - len(LATE_KEYS))
        d_kq = signal("d_kq", H - len(ACT_STACKS))
        d_max0 = signal("d_max0", H)
        d_o0 = signal("d_o0", 1)
        d_x = signal("d_x", 4, before=1)
        d_gap = signal("d_gap", 1)
        d_exm = signal("d_exm", 1)
        d_um = signal("d_um", 2)
        d_gsum = signal("d_gsum", 4)
        d_usum = signal("d_usum", 4)
        d_hid0 = signal("d_hid0", 4)
        d_zm = signal("d_zm", 1)
        d_latT = signal("d_latT", 1)
        d_latL = signal("d_latL", 1)
        d_klat = signal("d_klat", KLAT_DVE)
        d_qL = signal("d_qL", NPAIR)
        d_max1 = signal("d_max1", H)
        d_diag1 = signal("d_diag1", H)
        d_o1 = signal("d_o1", NPAIR)
        d_smax = signal("d_smax", 1)
        d_prob = signal("d_prob", 1)
        d_mask = signal("d_mask", 2)
        d_xm = signal("d_xm", 2)
        g_cn = signal("g_cn", 1)
        g_w2L = signal("g_w2L", FC)
        g_hidL = signal("g_hidL", 2)
        g_kL = signal("g_kL", len(LATE_KEYS))
        g_kLhalf = signal("g_kLhalf", len(LATE_KEYS))
        g_klathalf = signal("g_klathalf", 4 - KLAT_DVE)
        g_klat = signal("g_klat", 4 - KLAT_DVE)
        g_diag0 = signal("g_diag0", H)
        g_pad = signal("g_pad", 1)
        g_sum = signal("g_sum", H - 2, before=1)
        DVE_STEPS, DVE_AHEAD_STEPS = 141, 67
        d_step = signal("d_step", DVE_STEPS)
        d_ahead = signal("d_ahead", DVE_AHEAD_STEPS)
        d_sel = signal("d_sel", 1, before=1)
        g_step = signal("g_step", 2 * (H - 2) + 1)
        g_ahead = signal("g_ahead", 1)

        x_v = x_d.rearrange("b (t p) d -> b p t d", p=P)
        ctx_v = ctx_d.rearrange("b (t p) d -> b p t d", p=P)
        out_v = out.rearrange("b (t p) d -> b p t d", p=P)

        def row(a, n):
            return a.rearrange("(o n) -> o n", o=1).to_broadcast([P, n])

        block = ctx.enter_context(nc.Block())

        @block.sync
        def _(sp):
            W = t_in
            first = [
                (raw[:, W_Q0, :], W["L0_xattn_Wq"]),
                (raw[:, W_K0:W_V0 + 1, :], W["L0_xattn_Wkv"].rearrange("(n p) d -> p n d", p=P)),
                (raw[:, W_PROJ, :], W["L0_xattn_Wproj"]),
            ]
            raw_loads = [
                (raw[:, W_GATE:W_GATE + FC, :], W["L0_ffn_w_gate"].rearrange("(n p) d -> p n d", p=P)),
                (raw[:, W_UP:W_UP + FC, :], W["L0_ffn_w_up"].rearrange("(n p) d -> p n d", p=P)),
                (raw[:, W_DOWN:W_DOWN + 2 * FC, :].rearrange("p (c a) d -> p c a d", a=2)[:, :, 0, :],
                 W["L0_ffn_w_down"].rearrange("d (c f) -> d c f", f=P)),
                (raw[:, W_DOWN:W_DOWN + 2 * FC, :].rearrange("p (c a) d -> p c a d", a=2)[:, :, 1, :],
                 W["L0_ffn_A2"].rearrange("e r (c f) -> (e r) c f", f=P)),
                (raw[:, W_A1, :], W["L0_ffn_A1"].rearrange("e r d -> (e r) d")),
                (raw[:, W_A3, :], W["L0_ffn_A3"].rearrange("e r d -> (e r) d")),
                (raw[:, W_B2, :].rearrange("p (e r) -> p e r", e=E), W["L0_ffn_B2"].rearrange("e d r -> d e r")),
                (gate0_raw, W["L0_ffn_gate_w"]),
            ]
            for c in range(FC):
                for to, name in ((W_B1, "L0_ffn_B1"), (W_B3, "L0_ffn_B3")):
                    raw_loads.append((raw[:, to + c, :].rearrange("p (e r) -> p e r", e=E),
                                      W[name][:, c * P:(c + 1) * P, :].rearrange("e f r -> f e r")))
            bias = [
                (bq0[:, :], row(W["L0_xattn_bq"], P)),
                (bkv0[:, :, :].rearrange("p a d -> p (a d)"), row(W["L0_xattn_bkv"], 2 * P)),
                (lnm_g[:, :], row(W["L1_xattn_ln_m_g"], P)), (lnm_b[:, :], row(W["L1_xattn_ln_m_b"], P)),
                (kg0[:, :], row(W["L0_xattn_k_gamma"], D0)), (kb0[:, :], row(W["L0_xattn_k_beta"], D0)),
                (qg0[:, :], row(W["L0_xattn_q_gamma"], D0)), (qb0[:, :], row(W["L0_xattn_q_beta"], D0)),
            ]
            small = [
                (bproj0[:, :], row(W["L0_xattn_bproj"], P)),
                (lnl_g[:, :], W["L1_xattn_ln_l_g"].rearrange("(p o) -> p o", o=1)),
                (lnl_b[:, :], W["L1_xattn_ln_l_b"].rearrange("(p o) -> p o", o=1)),
                (gates_raw[:, 0:2], row(W["g_xattn"], 2)), (gates_raw[:, 2:4], row(W["g_ffn"], 2)),
                (gate1[:, :], W["L1_ffn_gate_w"]),
                (gate1_b[:, :], W["L1_ffn_gate_b"].rearrange("(e o) -> e o", o=1)),
                (b1[0:E, :], W["L1_ffn_b1"]), (b2[0:E, :], W["L1_ffn_b2"]),
                (wout[:, :, :], W["L1_xattn_Wout"].rearrange("(n p) d -> p n d", p=P)),
                (w1[:, :, :], W["L1_ffn_W1"].rearrange("e d f -> d e f")),
            ]
            assert (len(first), len(bias), len(raw_loads), len(small)) == (
                FIRST_LOADS, BIAS_LOADS, RAW_LOADS, SMALL_LOADS)
            sp.dma_start(x_in[:, :, :], x_v[0]).then_inc(s_x.sem, 16)
            sp.dma_start(ctx_in[:, :, :], ctx_v[0]).then_inc(s_ctx.sem, 16)
            for to, of in first:
                sp.dma_start(to, of).then_inc(s_first.sem, 16)
            for to, of in bias:
                sp.dma_start(to, of).then_inc(s_bias.sem, 16)
            sp.dma_start(raw_kv[:, :, :, :],
                         W["L1_xattn_Wkv"].rearrange("d (a n m) -> d a n m", a=2, m=P)).then_inc(s_rawkv.sem, 16)
            sp.dma_start(raw_q[:, :, :],
                         W["L1_xattn_Wq"].rearrange("d (n m) -> d n m", m=P)).then_inc(s_rawkv.sem, 16)
            for to, of in raw_loads:
                sp.dma_start(to, of).then_inc(s_raw.sem, 16)
            sp.wait_ge(s_zero.sem, 1)
            for to, of in small:
                sp.dma_start(to, of).then_inc(s_small.sem, 16)

            def batch(b, last):
                if not last:
                    sp.wait_ge(d_x.sem, d_x.after(b, 1))
                    sp.dma_start(x_in[:, :, :], x_v[b + 1]).then_inc(s_x.sem, 16)
                    sp.dma_start(ctx_in[:, :, :], ctx_v[b + 1]).then_inc(s_ctx.sem, 16)
                sp.wait_ge(e_pv1.sem, e_pv1.after(b, NPAIR))
                for c in range(FC):
                    sp.dma_start(w2[:, c, :].rearrange("p (e d) -> p e d", e=E),
                                 t_in["L1_ffn_W2"][:, c * P:(c + 1) * P, :].rearrange("e f d -> f e d")
                                 ).then_inc(s_w2.sem, 16)
                sp.wait_ge(d_x.sem, d_x.after(b, 4))
                sp.dma_start(out_v[b], xr[:, :, :]).then_inc(s_out.sem, 16)

            with sp.Fori(0, B - 1) as b:
                batch(b, False)
            batch(B - 1, True)
            sp.wait_ge(s_out.sem, s_out.after(B, 0))

        @block.gpsimd
        def _(pool):
            pool.memset(ident[:, :], 0.0).then_inc(s_const.sem, 1)
            pool.wait_ge(s_const.sem, 1)
            pool.affine_select(out=ident[:, :], in_=ident[:, :], compare_op=ALU.not_equal, fill=1.0, base=0,
                               pattern=[[-1, P]], channel_multiplier=1).then_inc(s_const.sem, 1)
            pool.memset(v0[:, :, :], 1.0).then_inc(s_v0.sem, 1)
            pool.memset(b1[:, :], 0.0)
            pool.memset(b2[:, :], 0.0).then_inc(s_zero.sem, 1)
            pool.memset(onesb[:, :], 1.0)
            pool.memset(onesf[:, :], 1.0)
            pool.iota(iota_col[:, :], [[1, P]], base=0, channel_multiplier=0, allow_small_or_imprecise_dtypes=True)
            pool.iota(iota_er[:, :, :], [[1, E], [0, R]], base=0, channel_multiplier=0,
                      allow_small_or_imprecise_dtypes=True)
            pool.iota(iota_ed[:, :, :], [[1, E], [0, P]], base=0, channel_multiplier=0,
                      allow_small_or_imprecise_dtypes=True)
            pool.wait_ge(s_const.sem, 2)
            pool.tensor_copy(identb[:, :], ident[:, :])
            pool.tensor_scalar(negidentb[:, :], ident[:, :], -1.0, None, ALU.mult).then_inc(s_const.sem, 1)
            pool.memset(psum_1[:, 0, 0:1], 0.0).then_inc(g_sum.sem, 1)

            def context_ahead(n):
                pool.wait_ge(d_cn.sem, d_cn.after(n, 1))
                pool.tensor_tensor(cn[:, :, :], cn[:, :, :],
                                   lnm_g[:, :].rearrange("p (o d) -> p o d", o=1).to_broadcast([P, TC, P]),
                                   ALU.mult).then_inc(g_ahead.sem, 1)
                pool.wait_ge(g_ahead.sem, g_ahead.after(n, 1))
                pool.tensor_tensor(cn[:, :, :], cn[:, :, :],
                                   lnm_b[:, :].rearrange("p (o d) -> p o d", o=1).to_broadcast([P, TC, P]),
                                   ALU.add).then_inc(g_cn.sem, 1)

            def pad_ahead():
                pool.memset(stack[:, :, SR:SK], 0.0).then_inc(g_pad.sem, 1)

            pool.wait_ge(s_bias.sem, 16 * BIAS_LOADS)
            context_ahead(0)
            pool.wait_ge(s_whigh.sem, 1)
            pool.tensor_tensor(wkv_l[:, 0, :, :], raw_kv[:, 0, :, :], wkv_h[:, 0, :, :],
                               ALU.subtract).then_inc(s_wlow.sem, 1)
            pad_ahead()
            pool.tensor_tensor(wkv_l[:, 1, :, :], raw_kv[:, 1, :, :], wkv_h[:, 1, :, :],
                               ALU.subtract).then_inc(s_wlow.sem, 1)
            pool.tensor_tensor(wq_l[:, :, :], raw_q, wq_h[:, :, :], ALU.subtract).then_inc(s_wlow.sem, 1)

            def batch(b, last):
                for h in range(H):
                    pool.wait_ge(d_max0.sem, d_max0.after(b, h + 1))
                    if h >= DG0:
                        pool.wait_ge(e_st0.sem, e_st0.after(b, 2 * (h - DG0 + 1)))
                    pool.tensor_tensor(
                        diag[:, h % DG0, :, :],
                        negidentb[:, :].rearrange("p (o q) -> p o q", o=1).to_broadcast([P, TQ, P]),
                        rowmax[:, h % RM0, :].rearrange("p (t o) -> p t o", o=1).to_broadcast([P, TQ, P]),
                        ALU.mult).then_inc(g_diag0.sem, 1)
                pool.wait_ge(g_diag0.sem, g_diag0.after(b, H))
                for n, p in enumerate(LATE_KEYS):
                    pool.wait_ge(a_kH.sem, a_kH.after(b, p + 1))
                    pool.tensor_tensor(keys[D1:P, 2 * p, 0:NC_], late_copy[n][0:D1, :], keys[0:D1, 2 * p, 0:NC_],
                                       ALU.subtract).then_inc(g_kLhalf.sem, 1)
                    pool.wait_ge(g_kLhalf.sem, g_kLhalf.after(b, n + 1))
                    pool.tensor_tensor(keys[0:D1, 2 * p + 1, 0:NC_], late_copy[n][D1:P, :],
                                       keys[D1:P, 2 * p + 1, 0:NC_], ALU.subtract).then_inc(g_kL.sem, 1)
                    pool.wait_ge(g_kL.sem, g_kL.after(b, n + 1))
                for r in range(KLAT_DVE, 4):
                    pool.wait_ge(a_klat.sem, a_klat.after(b, r + 1))
                    src = klat_copy[:, r - KLAT_DVE, :].rearrange("p (n q) -> p n q", n=2)
                    ev, od = slice(4 * r, 4 * r + 4, 2), slice(4 * r + 1, 4 * r + 4, 2)
                    pool.tensor_tensor(keys[D1:P, ev, NC_:NK], src[0:D1, :, :], keys[0:D1, ev, NC_:NK],
                                       ALU.subtract).then_inc(g_klathalf.sem, 1)
                    pool.wait_ge(g_klathalf.sem, g_klathalf.after(b, r - KLAT_DVE + 1))
                    pool.tensor_tensor(keys[0:D1, od, NC_:NK], src[D1:P, :, :], keys[D1:P, od, NC_:NK],
                                       ALU.subtract).then_inc(g_klat.sem, 1)
                    pool.wait_ge(g_klat.sem, g_klat.after(b, r - KLAT_DVE + 1))
                for h in range(H - 2):
                    pool.wait_ge(a_exp1.sem, a_exp1.after(b, 3 * h + 3))
                    pool.wait_ge(g_sum.sem, g_sum.after(b, h))
                    e = p1[:, h % PR1, :]
                    pool.tensor_tensor(psum_a, e[:, 0:768], e[:, 768:1536], ALU.add).then_inc(g_step.sem, 1)
                    pool.wait_ge(g_step.sem, g_step.after(b, 1 + 2 * h))
                    if h >= 2:
                        pool.wait_ge(e_den1.sem, e_den1.after(b, h // 2))
                    pool.tensor_tensor(psum_a[:, 0:256], psum_a[:, 0:256], psum_a[:, 256:512],
                                       ALU.add).then_inc(g_step.sem, 1)
                    pool.wait_ge(g_step.sem, g_step.after(b, 2 + 2 * h))
                    pool.tensor_tensor(psum_1[:, h % 2, :], psum_a[:, 0:256], psum_a[:, 512:768],
                                       ALU.add).then_inc(g_sum.sem, 1)
                    if h == CN_HEAD and not last:
                        context_ahead(b + 1)
                if not last:
                    pool.wait_ge(a_exp1.sem, a_exp1.after(b, 3 * H))
                    pool.tensor_tensor(scratch_g[:, :], onesf[:, 0:1], onesf[:, 0:1], ALU.add).then_inc(g_step.sem, 1)
                    pad_ahead()
                for c in range(FC):
                    pool.wait_ge(a_w2H.sem, a_w2H.after(b, c + 1))
                    pool.tensor_tensor(w2_l[:, c, :], w2[:, c, :], w2_h[:, c, :],
                                       ALU.subtract).then_inc(g_w2L.sem, 1)
                for n in range(2):
                    part = slice(2 * n, 2 * n + 2)
                    pool.wait_ge(a_hidH.sem, a_hidH.after(b, n + 1))
                    pool.tensor_tensor(hid1_l[:, part, :], hid1[:, part, :], hid1_h[:, part, :],
                                       ALU.subtract).then_inc(g_hidL.sem, 1)

            with pool.Fori(0, B - 1) as b:
                batch(b, False)
            batch(B - 1, True)

        @block.scalar
        def _(act):
            def copy(to, of):
                return act.activation(to, of, ACT.Copy)

            def weights_out(n):
                act.wait_ge(s_wT.sem, n + 1)
                k = min(4, NT - 4 * n)
                copy(wt[:, 4 * n:4 * n + k, :].rearrange("p n d -> p (n d)"),
                     bank(6 + n % 2)[:, 0:k * P]).then_inc(s_wT_copied.sem, 1)

            def keys_high(n, p):
                act.wait_ge(e_k.sem, e_k.after(n, p + 1))
                src = bank(KEY_BANK[p])
                if p in LATE_KEYS:
                    copy(late_copy[LATE_KEYS.index(p)], src)
                copy(keys[0:D1, 2 * p, 0:NC_], src[0:D1, :])
                copy(keys[D1:P, 2 * p + 1, 0:NC_], src[D1:P, :]).then_inc(a_kH.sem, 1)

            weights_out(0)
            def operands_ahead(n):
                act.wait_ge(e_ctxT.sem, e_ctxT.after(n, 1))
                copy(ctxT[:, :], bank(1)).then_inc(a_ctxT.sem, 1)
                act.wait_ge(e_xT0.sem, e_xT0.after(n, 1))
                copy(xT0[:, :], bank(0)[:, 0:NQ]).then_inc(a_xT0.sem, 1)
                act.wait_ge(e_cnT.sem, e_cnT.after(n, 1))
                copy(kv_h[:, 0:NC_], bank(2)).then_inc(a_cH.sem, 1)

            operands_ahead(0)
            act.wait_ge(s_rawkv.sem, 32)
            copy(wkv_h[:, :, :, :], raw_kv)
            copy(wq_h[:, :, :], raw_q).then_inc(s_whigh.sem, 1)
            for n in range(1, 8):
                weights_out(n)
            act.wait_ge(s_wT.sem, 9)
            copy(gate0[:, :], bank(6)[:, 0:E]).then_inc(s_wT_copied.sem, 1)
            act.wait_ge(s_small.sem, 16 * SMALL_LOADS)
            act.activation(gates[:, :], gates_raw[:, :], ACT.Tanh).then_inc(s_tanh.sem, 1)
            for p in range(AHEAD_PAIRS):
                keys_high(0, p)

            def batch(b, last):
                for n in ACT_STACKS:
                    act.wait_ge(e_kq.sem, e_kq.after(b, n + 1))
                    copy(kq[0:SK, n, :], bank(STACK_BANK[n])[0:SK, 0:384].bitcast(BF16)).then_inc(a_kq.sem, 1)
                for h in range(H):
                    if h >= PR0:
                        act.wait_ge(e_pv0.sem, e_pv0.after(b, (h - PR0) // QUAD + 1))
                    for half in range(2):
                        act.wait_ge(e_st0.sem, e_st0.after(b, 2 * h + half + 1))
                        act.activation(p0[:, h % PR0, 2 * half:2 * half + 2, :].rearrange("p k q -> p (k q)"),
                                       bank(4 + half), ACT.Exp).then_inc(a_exp0.sem, 1)
                    if h in LOOP_KEYS:
                        keys_high(b, LOOP_KEYS[h])
                    if h % QUAD == 2 and h > QUAD:
                        g = h // QUAD - 1
                        act.wait_ge(e_pv0.sem, e_pv0.after(b, g + 1))
                        copy(o0[:, g, :], bank(6 + g % 2)[:, 0:NQ]).then_inc(a_o0.sem, 1)
                act.wait_ge(e_pv0.sem, e_pv0.after(b, NQUAD))
                copy(o0[:, NQUAD - 1, :], bank(6 + (NQUAD - 1) % 2)[:, 0:NQ]).then_inc(a_o0.sem, 1)

                def values_out(t):
                    act.wait_ge(e_v.sem, e_v.after(b, t + 1))
                    copy(v1[:, t, :], bank(V_BANK[t], 2)).then_inc(a_v.sem, 1)

                values_out(0)
                act.wait_ge(e_o0.sem, e_o0.after(b, 2))
                copy(o0_T, bank(2)[:, 0:NQ]).then_inc(a_oT.sem, 1)
                values_out(1)
                values_out(2)
                keys_high(b, LATE_KEYS[0])
                act.wait_ge(e_xT.sem, e_xT.after(b, 1))
                copy(xT[:, :], bank(4)[:, 0:NQ]).then_inc(a_xT.sem, 1)
                for n in range(4):
                    act.wait_ge(e_common.sem, e_common.after(b, n + 1))
                    if n == 2:
                        act.wait_ge(d_gap.sem, d_gap.after(b, 1))
                        act.activation(wsel[:, 1, :], wsel[:, 0, :], ACT.Exp).then_inc(a_ratio.sem, 1)
                    copy(common[:, n // 2, 2 * (n % 2):2 * (n % 2) + 2, :].rearrange("p c q -> p (c q)"),
                         bank(n)).then_inc(a_common.sem, 1)
                for s in range(4):
                    act.wait_ge(d_gsum.sem, d_gsum.after(b, s + 1))
                    act.activation(sg[:, s % 2, :], sg[:, s % 2, :], ACT.Silu).then_inc(a_silu.sem, 1)
                values_out(3)
                act.wait_ge(e_z.sem, e_z.after(b, 1))
                copy(zT, bank(6)[:, 0:NQ]).then_inc(a_zT.sem, 1)
                for p in LATE_KEYS[1:]:
                    keys_high(b, p)
                act.wait_ge(d_latT.sem, d_latT.after(b, 1))
                copy(kv_h[:, NC_:NK], latT).then_inc(a_latH.sem, 1)

                def keys_of_latents(r):
                    act.wait_ge(e_klat.sem, e_klat.after(b, r + 1))
                    src = bank(KLAT_BANK[r]).rearrange("p (n q) -> p n q", n=2)
                    if r >= KLAT_DVE:
                        copy(klat_copy[:, r - KLAT_DVE, :], bank(KLAT_BANK[r]))
                    copy(keys[0:D1, 4 * r:4 * r + 4:2, NC_:NK], src[0:D1, :, :])
                    copy(keys[D1:P, 4 * r + 1:4 * r + 4:2, NC_:NK], src[D1:P, :, :]).then_inc(a_klat.sem, 1)

                def q_high(m):
                    act.wait_ge(e_q.sem, e_q.after(b, m + 1))
                    if m >= 2:
                        act.wait_ge(e_st1.sem, e_st1.after(b, 3 * (2 * m - 2)))
                    for n in range(2):
                        for half in range(2):
                            ins = copy(q_h[half * D1:(half + 1) * D1, m % 2, n, :],
                                       q_bank(m)[n * D1:(n + 1) * D1, :])
                    ins.then_inc(a_qH.sem, 1)

                keys_of_latents(0)
                q_high(0)
                keys_of_latents(1)
                keys_of_latents(2)
                values_out(TC)
                q_high(1)
                keys_of_latents(3)
                for i in range(1, H + 1):
                    h = i - 1
                    if h >= PR1:
                        act.wait_ge(e_pv1.sem, e_pv1.after(b, (h - PR1) // 2 + 1))
                        act.wait_ge(g_sum.sem, g_sum.after(b, h - PR1 + 1))
                    if h == 2:
                        act.wait_ge(g_klat.sem, g_klat.after(b, 4 - KLAT_DVE))
                    for n in range(3):
                        act.wait_ge(e_st1.sem, e_st1.after(b, 3 * h + n + 1))
                        act.activation(p1[:, h % PR1, n * BANK:(n + 1) * BANK], bank(3 + n), ACT.Exp,
                                       scale=SCALE1).then_inc(a_exp1.sem, 1)
                    if h == 0:
                        values_out(TC + 1)
                    if i % 2 == 0 and (i - 2) // 2 + 2 < NPAIR:
                        q_high((i - 2) // 2 + 2)
                if not last:
                    operands_ahead(b + 1)
                act.wait_ge(e_y1.sem, e_y1.after(b, 1))
                copy(yT, bank(0)[:, 0:NQ]).then_inc(a_yT.sem, 1)
                act.wait_ge(e_xT.sem, e_xT.after(b, 3))
                copy(xT[:, :], bank(2)[:, 0:NQ]).then_inc(a_xT.sem, 1)
                act.wait_ge(d_smax.sem, d_smax.after(b, 1))
                act.activation(probT[0:E, :], probT[0:E, :], ACT.Exp, bias=sm[:, 1:2],
                               accum_out=sm[:, 2:3]).then_inc(a_sm.sem, 1)
                if not last:
                    for p in range(AHEAD_PAIRS):
                        keys_high(b + 1, p)
                act.wait_ge(e_route1.sem, e_route1.after(b, 5))
                copy(maskT, bank(3)[:, NQ:2 * NQ]).then_inc(a_maskT.sem, 1)
                act.wait_ge(s_w2.sem, s_w2.after(b, 16 * FC))
                for c in range(FC):
                    copy(w2_h[:, c, :], w2[:, c, :]).then_inc(a_w2H.sem, 1)
                for n in range(2):
                    act.wait_ge(e_pre1.sem, e_pre1.after(b, n + 1))
                    act.activation(hid1[:, 2 * n:2 * n + 2, :].rearrange("p c q -> p (c q)"), bank(2 + n),
                                   ACT.Gelu).then_inc(a_gelu.sem, 1)
                    act.wait_ge(a_gelu.sem, a_gelu.after(b, n + 1))
                    copy(hid1_h[:, 2 * n:2 * n + 2, :], hid1[:, 2 * n:2 * n + 2, :]).then_inc(a_hidH.sem, 1)

            with act.Fori(0, B - 1) as b:
                batch(b, False)
            batch(B - 1, True)

        @block.vector
        def _(dve):
            dve.memset(scratch[:, 0:1], 0.0).then_inc(d_x.sem, 1)
            dve.memset(wsel[:, 0, 0:1], 0.0).then_inc(s_out.sem, 1)
            dve.memset(scratch[:, 1:2], 0.0).then_inc(d_sel.sem, 1)
            dve.wait_ge(d_x.sem, 1)
            dve.wait_ge(d_sel.sem, 1)

            count = {d_step: 0, d_ahead: 0}
            own_signal = [d_ahead, 0]

            def step(ins):
                count[own_signal[0]] += 1
                ins.then_inc(own_signal[0].sem, 1)

            def own():
                signal, n = own_signal
                dve.wait_ge(signal.sem, signal.after(n, count[signal]))

            def own_first():
                own()
                c = 0 if own_signal[0] is d_step else 1
                step(dve.memset(scratch[:, c:c + 1], 0.0))

            def then(ins):
                step(ins)
                own()

            def rsqrt(vh, y, t, columns=True):
                then(dve.tensor_scalar(t.bitcast(I32), vh.bitcast(I32), 1, None, ALU.arith_shift_right))
                then(dve.tensor_scalar(y.bitcast(I32), t.bitcast(I32), -1.0,
                                       float(RSQRT_MAGIC - (1 << 22) - (1 << 30)), ALU.mult, ALU.add))
                for _ in range(3):
                    if columns:
                        for c in range(y.shape[1]):
                            y_c = y[:, c:c + 1]
                            step(dve.scalar_tensor_tensor(out=t[:, c:c + 1], in0=y_c, scalar=y_c,
                                                          in1=vh[:, c:c + 1], op0=ALU.mult, op1=ALU.mult))
                        own()
                    else:
                        then(dve.tensor_tensor(t, y, y, ALU.mult))
                        then(dve.tensor_tensor(t, t, vh, ALU.mult))
                    then(dve.scalar_tensor_tensor(out=y, in0=t, scalar=1.5, in1=y, op0=ALU.add, op1=ALU.mult))

            def moments_of(of, tiles, st, mo):
                for t in range(tiles):
                    step(dve.bn_stats(st[:, t, :], of[:, t, :]))
                own_first()
                for t in range(tiles):
                    step(dve.bn_aggr(mo[:, t, :], st[:, t, :]))
                own()

            def normalise(to, of, tiles, mo, r):
                for t in range(tiles):
                    ins = dve.tensor_scalar(to[:, t, :], of[:, t, :], mo[:, t, 0:1], r[:, t:t + 1],
                                            ALU.subtract, ALU.mult)
                    if t < tiles - 1:
                        step(ins)
                return ins

            def layernorm(to, of, twice=False):
                moments_of(of, TQ, stats, moments)
                vh, y, tmp = (a[:, :] for a in rs_small)
                if twice:
                    then(dve.tensor_scalar(vh, moments[:, :, 1], -0.5 * (1.0 + EPS), -0.5 * EPS * EPS,
                                           ALU.mult, ALU.add))
                else:
                    then(dve.tensor_scalar(vh, moments[:, :, 1], EPS, -0.5, ALU.add, ALU.mult))
                rsqrt(vh, y, tmp)
                return normalise(to, of, TQ, moments, y)

            def wide(a, n, m):
                return a.rearrange("p (o d) -> p o d", o=1).to_broadcast([P, n, m])

            def groups(a):
                return a.rearrange("p (g o) -> p g o", o=1).to_broadcast([P, G0, D0])

            def tokens_ahead(n, part):
                held = list(own_signal)
                own_signal[:] = d_ahead, n
                vh, y, tmp = (a[:, :] for a in rs0)
                if part == 0:
                    count[d_ahead] = 0
                    dve.wait_ge(s_x.sem, s_x.after(n, 16))
                    dve.wait_ge(s_ctx.sem, s_ctx.after(n, 16))
                    for t in range(TQ):
                        step(dve.bn_stats(stats0[:, t, :], x_in[:, t, :]))
                    for t in range(TC):
                        step(dve.bn_stats(stats0[:, TQ + t, :], ctx_in[:, t, :]))
                elif part == 1:
                    own_first()
                    for t in range(TK):
                        step(dve.bn_aggr(moments0[:, t, :], stats0[:, t, :]))
                    own()
                    then(dve.tensor_scalar(vh, moments0[:, :, 1], EPS, -0.5, ALU.add, ALU.mult))
                    rsqrt(vh, y, tmp, columns=False)
                else:
                    normalise(xn0, x_in, TQ, moments0, y).then_inc(d_xn0.sem, 1)
                    normalise(cn, ctx_in, TC, moments0[:, TQ:TK, :], y[:, TQ:TK]).then_inc(d_cn.sem, 1)
                own_signal[:] = held

            def context_low_ahead(n):
                dve.wait_ge(a_cH.sem, a_cH.after(n, 1))
                dve.tensor_tensor(kv_l[:, 0:NC_], bank(2), kv_h[:, 0:NC_], ALU.subtract).then_inc(d_cL.sem, 1)

            kv_ps = bank(4, 2).rearrange("p (t a d) -> p t a d", t=TC, a=2)

            def qk_ahead(n):
                held = list(own_signal)
                own_signal[:] = d_ahead, n
                dve.wait_ge(e_qkv0.sem, e_qkv0.after(n, 1))
                k_tiles = qk[:, 0:TC * H, :].rearrange("p (t h) d -> p t (h d)", t=TC)
                q_tiles = qk[:, TC * H:G0, :].rearrange("p (t h) d -> p t (h d)", t=TQ)
                step(dve.tensor_tensor(q_tiles, bank(3)[:, 0:NQ].rearrange("p (t d) -> p t d", t=TQ),
                                       wide(bq0[:, :], TQ, P), ALU.add))
                step(dve.tensor_tensor(k_tiles, kv_ps[:, :, 0, :], wide(bkv0[:, 0, :], TC, P), ALU.add))
                own_signal[:] = held

            def v_ahead(n):
                held = list(own_signal)
                own_signal[:] = d_ahead, n
                for t in range(TC):
                    ins = dve.tensor_tensor(
                        v0[:, t, 0:H * V0W].rearrange("p (h d) -> p h d", h=H)[:, :, 0:D0],
                        kv_ps[:, t, 1, :].rearrange("p (h d) -> p h d", h=H),
                        bkv0[:, 1, :].rearrange("p (h d) -> p h d", h=H), ALU.add)
                    if t < TC - 1:
                        step(ins)
                ins.then_inc(d_qkv0.sem, 1)
                own_signal[:] = held

            def stack_ahead(n):
                held = list(own_signal)
                own_signal[:] = d_ahead, n
                own()
                dve.wait_ge(d_qkv0.sem, d_qkv0.after(n, 1))
                then(dve.tensor_reduce(hsum, qk, AX, ALU.add))
                then(dve.tensor_scalar(hsum, hsum, 1.0 / D0, None, ALU.mult))
                then(dve.tensor_tensor(qk, qk, groups(hsum), ALU.subtract))
                then(dve.tensor_tensor(qk2, qk, qk, ALU.mult))
                then(dve.tensor_reduce(hsum, qk2, AX, ALU.add))
                then(dve.tensor_scalar(hsum, hsum, 1.0 / D0, EPS, ALU.mult, ALU.add))
                then(dve.tensor_scalar(rs_wide[0], hsum, -0.5, None, ALU.mult))
                rsqrt(*rs_wide, columns=False)
                then(dve.tensor_tensor(qk, qk, groups(rs_wide[1]), ALU.mult))
                for lo, hi, g, be in ((0, TC * H, kg0, kb0), (TC * H, G0, qg0, qb0)):
                    then(dve.tensor_tensor(qk[:, lo:hi, :], qk[:, lo:hi, :], wide(g[:, :], hi - lo, D0), ALU.mult))
                    then(dve.tensor_tensor(qk[:, lo:hi, :], qk[:, lo:hi, :], wide(be[:, :], hi - lo, D0), ALU.add))
                then(dve.tensor_copy(parts[:, :, 0, :], qk))
                then(dve.tensor_tensor(qk2, qk, parts[:, :, 0, :], ALU.subtract))
                then(dve.tensor_copy(parts[:, :, 1, :], qk2))
                then(dve.tensor_tensor(qk, qk2, parts[:, :, 1, :], ALU.subtract))
                then(dve.tensor_copy(parts[:, :, 2, :], qk))
                PW = NPART * D0
                for m in range(NPART):
                    step(dve.tensor_copy(stack[:, 0:TC * H, m * PW:(m + 1) * PW],
                                         parts[:, 0:TC * H, :, :].rearrange("p g s d -> p g (s d)")))
                for m in range(NPART):
                    ins = dve.tensor_copy(
                        stack[:, TC * H:G0, m * PW:(m + 1) * PW].rearrange("p g (s d) -> p g s d", s=NPART),
                        parts[:, TC * H:G0, m:m + 1, :].to_broadcast([P, TQ * H, NPART, D0]))
                    if m < NPART - 1:
                        step(ins)
                ins.then_inc(d_stack.sem, 1)
                assert count[d_ahead] == DVE_AHEAD_STEPS, count[d_ahead]
                own_signal[:] = held

            def keys_low(n, p):
                dve.wait_ge(a_kH.sem, a_kH.after(n, p + 1))
                src = bank(KEY_BANK[p])
                dve.tensor_tensor(keys[D1:P, 2 * p, 0:NC_], src[0:D1, :], keys[0:D1, 2 * p, 0:NC_],
                                       ALU.subtract).then_inc(d_kLhalf.sem, 1)
                dve.tensor_tensor(keys[0:D1, 2 * p + 1, 0:NC_], src[D1:P, :], keys[D1:P, 2 * p + 1, 0:NC_],
                                  ALU.subtract).then_inc(d_kL.sem, 1)

            for part in range(3):
                tokens_ahead(0, part)
            dve.wait_ge(s_bias.sem, 16 * BIAS_LOADS)
            dve.tensor_scalar(qg0[:, :], qg0[:, :], SCALE0, None, ALU.mult).then_inc(s_scaled.sem, 1)
            dve.tensor_scalar(qb0[:, :], qb0[:, :], SCALE0, None, ALU.mult).then_inc(s_scaled.sem, 1)
            dve.wait_ge(s_scaled.sem, 2)
            dve.wait_ge(s_v0.sem, 1)
            qk_ahead(0)
            v_ahead(0)
            context_low_ahead(0)
            stack_ahead(0)
            for p in range(AHEAD_PAIRS):
                keys_low(0, p)
            dve.wait_ge(s_small.sem, 16 * SMALL_LOADS)
            dve.wait_ge(s_tanh.sem, 1)

            def batch(b, last):
                own_signal[:] = d_step, b
                count[d_step] = 0
                for n in range(H):
                    if n not in ACT_STACKS:
                        dve.wait_ge(e_kq.sem, e_kq.after(b, n + 1))
                        dve.tensor_copy(kq[0:SK, n, :],
                                        bank(STACK_BANK[n])[0:SK, 0:384].bitcast(BF16)).then_inc(d_kq.sem, 1)

                for h in range(H):
                    dve.wait_ge(e_max0.sem, e_max0.after(b, h + 1))
                    if h >= RM0:
                        dve.wait_ge(g_diag0.sem, g_diag0.after(b, h - RM0 + 1))
                    dve.tensor_reduce(rowmax[:, h % RM0, :],
                                      bank(2 * (h % 2), 2).rearrange("p (t k) -> p t k", t=TQ),
                                      AX, ALU.max).then_inc(d_max0.sem, 1)
                    if h - MAX_AHEAD in LOOP_KEYS:
                        keys_low(b, LOOP_KEYS[h - MAX_AHEAD])

                dve.wait_ge(e_o0.sem, e_o0.after(b, 1))
                o_ps = bank(0, 2).rearrange("p (t h c) -> p t h c", t=TQ, h=H)
                then(dve.reciprocal(rden0[:, :, :], o_ps[:, :, :, D0]))
                for t in range(TQ):
                    ins = dve.tensor_tensor(o0_tok[:, t, :].rearrange("p (h d) -> p h d", h=H), o_ps[:, t, :, 0:D0],
                                            rden0[:, t, :].rearrange("p (h o) -> p h o", o=1)
                                            .to_broadcast([P, H, D0]), ALU.mult)
                    if t < TQ - 1:
                        step(ins)
                ins.then_inc(d_o0.sem, 1)
                dve.wait_ge(s_out.sem, s_out.after(b, 0))
                then(dve.scalar_tensor_tensor(out=xr[:, :, :], in0=wide(bproj0[:, :], TQ, P), scalar=G_X0,
                                              in1=x_in[:, :, :], op0=ALU.mult, op1=ALU.add))
                dve.wait_ge(e_o0.sem, e_o0.after(b, 3))
                dve.scalar_tensor_tensor(out=xr[:, :, :], in0=bank(3)[:, 0:NQ].rearrange("p (t d) -> p t d", t=TQ),
                                         scalar=G_X0, in1=xr[:, :, :], op0=ALU.mult,
                                         op1=ALU.add).then_inc(d_x.sem, 1)

                dve.wait_ge(d_x.sem, d_x.after(b, 1))
                layernorm(xn, xr).then_inc(d_xn.sem, 1)
                dve.wait_ge(e_route0.sem, e_route0.after(b, 1))
                step(dve.tensor_copy(lg[:, :, :].rearrange("p t e -> p (t e)"), bank(5)[:, 0:TQ * E]))

                def top8(of):
                    own_first()
                    for t in range(TQ):
                        step(dve.max(top[:, t, :], of[:, t, :]))
                    own_first()
                    for t in range(TQ):
                        step(dve.max_index(topi[:, t, :], top[:, t, :], of[:, t, :]))
                    own()
                    then(dve.tensor_copy(topf[:, :, :], topi[:, :, :]))

                top8(lg)
                dve.tensor_tensor(wsel[:, 0, :], top[:, :, 1], top[:, :, 0], ALU.subtract).then_inc(d_gap.sem, 1)
                for j in range(2):
                    for t in range(TQ):
                        ins = dve.tensor_scalar(exm[:, j, t, :], iota_er[:, :, :].rearrange("p e r -> p (e r)"),
                                                topf[:, t, j:j + 1], None, ALU.is_equal)
                        if (j, t) != (1, TQ - 1):
                            step(ins)
                ins.then_inc(d_exm.sem, 1)
                dve.wait_ge(a_ratio.sem, a_ratio.after(b, 1))
                then(dve.tensor_scalar(wsel[:, 2, :], wsel[:, 1, :], 1.0, None, ALU.add))
                then(dve.reciprocal(wsel[:, 2, :], wsel[:, 2, :]))
                then(dve.tensor_tensor(wsel[:, 3, :], wsel[:, 2, :], wsel[:, 1, :], ALU.mult))
                dve.wait_ge(e_route0.sem, e_route0.after(b, 3))
                xa = bank(6).rearrange("p (u q) -> p u q", u=2)
                then(dve.tensor_scalar(exmT[:, 0, :], bank(7)[:, 0:NQ], LORA_SCALE, None, ALU.mult))
                dve.tensor_tensor(um[:, :, 0, :], xa, exmT[:, 0:1, :].to_broadcast([P, 2, NQ]),
                                  ALU.mult).then_inc(d_um.sem, 1)
                then(dve.tensor_scalar(exmT[:, 1, :], bank(7)[:, NQ:2 * NQ], LORA_SCALE, None, ALU.mult))
                dve.tensor_tensor(um[:, :, 1, :], xa, exmT[:, 1:2, :].to_broadcast([P, 2, NQ]),
                                  ALU.mult).then_inc(d_um.sem, 1)

                def hidden(s):
                    dve.wait_ge(a_silu.sem, a_silu.after(b, s + 1))
                    dve.wait_ge(d_usum.sem, d_usum.after(b, s + 1))
                    dve.tensor_tensor(hid0_half(s), hid0_half(s), sg[:, s % 2, :], ALU.mult).then_inc(d_hid0.sem, 1)

                def hid0_half(s):
                    return hid0[:, s // 2, 2 * (s % 2):2 * (s % 2) + 2, :].rearrange("p c q -> p (c q)")

                dve.wait_ge(g_kL.sem, g_kL.after(b, 1))
                for s in range(4):
                    x_part = common[:, :, 2 * (s % 2):2 * (s % 2) + 2, :].rearrange("p u c q -> p u (c q)")
                    dve.wait_ge(e_pre0.sem, e_pre0.after(b, s + 1))
                    if s >= 2:
                        dve.wait_ge(d_hid0.sem, d_hid0.after(b, s - 1))
                    dve.tensor_tensor(sg[:, s % 2, :], bank(2 * (s % 2)), x_part[:, 0, :],
                                      ALU.add).then_inc(d_gsum.sem, 1)
                    dve.tensor_tensor(hid0_half(s), bank(2 * (s % 2) + 1), x_part[:, 1, :],
                                      ALU.add).then_inc(d_usum.sem, 1)
                    if s >= 1:
                        hidden(s - 1)
                hidden(3)
                for j in range(2):
                    for t in range(TQ):
                        step(dve.tensor_scalar(exm[:, j, t, :], exm[:, j, t, :], wsel[:, 2 + j, t:t + 1], LORA_SCALE,
                                               ALU.mult, ALU.mult))
                own()
                for j in range(2):
                    dve.wait_ge(e_down0.sem, e_down0.after(b, j + 1))
                    dn = bank(4 + j).rearrange("p (t a d) -> p t a d", t=TQ, a=2)
                    step(dve.tensor_tensor(zm[:, j, :, :], dn[:, :, 1, :], exm[:, j, :, :], ALU.mult))
                    for t in range(TQ):
                        if j == 0:
                            step(dve.tensor_scalar(dsum[:, t, :], dn[:, t, 0, :], wsel[:, 2, t:t + 1], None,
                                                   ALU.mult))
                        else:
                            step(dve.scalar_tensor_tensor(out=dsum[:, t, :], in0=dn[:, t, 0, :],
                                                          scalar=wsel[:, 3, t:t + 1], in1=dsum[:, t, :],
                                                          op0=ALU.mult, op1=ALU.add))
                    own()
                dve.tensor_tensor(zm[:, 0, :, :], zm[:, 0, :, :], zm[:, 1, :, :], ALU.add).then_inc(d_zm.sem, 1)
                then(dve.scalar_tensor_tensor(out=xr[:, :, :], in0=dsum, scalar=G_F0, in1=xr[:, :, :],
                                              op0=ALU.mult, op1=ALU.add))
                dve.wait_ge(e_z.sem, e_z.after(b, 2))
                dve.scalar_tensor_tensor(out=xr[:, :, :], in0=bank(7)[:, 0:NQ].rearrange("p (t d) -> p t d", t=TQ),
                                         scalar=G_F0, in1=xr[:, :, :], op0=ALU.mult,
                                         op1=ALU.add).then_inc(d_x.sem, 1)

                dve.wait_ge(d_x.sem, d_x.after(b, 2))
                layernorm(xn, xr, twice=True).then_inc(d_xn.sem, 1)
                dve.wait_ge(e_xT.sem, e_xT.after(b, 2))
                dve.tensor_scalar(latT, bank(0)[:, 0:NQ], lnl_g[:, :], lnl_b[:, :],
                                  ALU.mult, ALU.add).then_inc(d_latT.sem, 1)
                dve.wait_ge(d_latT.sem, d_latT.after(b, 1))
                dve.wait_ge(a_latH.sem, a_latH.after(b, 1))
                dve.tensor_tensor(kv_l[:, NC_:NK], latT, kv_h[:, NC_:NK], ALU.subtract).then_inc(d_latL.sem, 1)

                def keys_of_latents(r):
                    dve.wait_ge(a_klat.sem, a_klat.after(b, r + 1))
                    src = bank(KLAT_BANK[r]).rearrange("p (n q) -> p n q", n=2)
                    ev, od = slice(4 * r, 4 * r + 4, 2), slice(4 * r + 1, 4 * r + 4, 2)
                    step(dve.tensor_tensor(keys[D1:P, ev, NC_:NK], src[0:D1, :, :], keys[0:D1, ev, NC_:NK],
                                           ALU.subtract))
                    dve.tensor_tensor(keys[0:D1, od, NC_:NK], src[D1:P, :, :], keys[D1:P, od, NC_:NK],
                                      ALU.subtract).then_inc(d_klat.sem, 1)

                def q_low(m):
                    dve.wait_ge(a_qH.sem, a_qH.after(b, m + 1))
                    for n in range(2):
                        for half in range(2):
                            lo, hi = half * D1, (half + 1) * D1
                            ins = dve.tensor_tensor(q_l[lo:hi, m % 2, n, :],
                                                    q_bank(m)[n * D1:(n + 1) * D1, :],
                                                    q_h[n * D1:(n + 1) * D1, m % 2, n, :], ALU.subtract)
                            if (n, half) != (1, 1):
                                step(ins)
                    ins.then_inc(d_qL.sem, 1)

                def divide(p):
                    dve.wait_ge(e_den1.sem, e_den1.after(b, p + 1))
                    o = bank(6 + p % 2)
                    then(dve.reciprocal(o1[:, p, :], o[:, NQ:2 * NQ]))
                    dve.tensor_tensor(o1[:, p, :], o[:, 0:NQ], o1[:, p, :], ALU.mult).then_inc(d_o1.sem, 1)

                def row_max1(h):
                    dve.wait_ge(e_max1.sem, e_max1.after(b, h + 1))
                    dve.tensor_reduce(rowmax[:, h % 2, :], bank(0, 3).rearrange("p (t k) -> p t k", t=TQ),
                                      AX, ALU.max).then_inc(d_max1.sem, 1)
                    dve.wait_ge(d_max1.sem, d_max1.after(b, h + 1))
                    if h >= 2:
                        dve.wait_ge(e_st1.sem, e_st1.after(b, 3 * (h - 1)))
                    dve.tensor_tensor(
                        diag[:, h % 2, :, :],
                        negidentb[:, :].rearrange("p (o q) -> p o q", o=1).to_broadcast([P, TQ, P]),
                        rowmax[:, h % 2, :].rearrange("p (t o) -> p t o", o=1).to_broadcast([P, TQ, P]),
                        ALU.mult).then_inc(d_diag1.sem, 1)

                keys_of_latents(0)
                q_low(0)
                keys_of_latents(1)
                row_max1(0)
                q_low(1)
                for i in range(1, H + 1):
                    if i < H:
                        row_max1(i)
                    if i == 6:
                        dve.wait_ge(g_kL.sem, g_kL.after(b, len(LATE_KEYS)))
                    if i % 2 == 0 and i >= 6:
                        divide(i // 2 - 3)
                    if i % 2 == 0 and i // 2 + 1 < NPAIR:
                        q_low(i // 2 + 1)
                    if i in range(TOKENS_HEAD, TOKENS_HEAD + 6, 2) and not last:
                        tokens_ahead(b + 1, (i - TOKENS_HEAD) // 2)
                if not last:
                    context_low_ahead(b + 1)
                divide(NPAIR - 2)
                divide(NPAIR - 1)
                then(dve.memset(probT, 0.0))
                dve.wait_ge(e_y1.sem, e_y1.after(b, 2))
                dve.scalar_tensor_tensor(out=xr[:, :, :], in0=bank(1)[:, 0:NQ].rearrange("p (t d) -> p t d", t=TQ),
                                         scalar=G_X1, in1=xr[:, :, :], op0=ALU.mult,
                                         op1=ALU.add).then_inc(d_x.sem, 1)

                dve.wait_ge(d_x.sem, d_x.after(b, 3))
                layernorm(xn, xr).then_inc(d_xn.sem, 1)
                if not last:
                    qk_ahead(b + 1)
                dve.wait_ge(e_route1.sem, e_route1.after(b, 1))
                then(dve.tensor_scalar(probT[0:E, :], bank(2)[0:E, NQ:2 * NQ], gate1_b[:, :], None, ALU.add))
                then(dve.tensor_reduce(sm[:, 0:1], probT[0:E, :], AX, ALU.max))
                dve.tensor_scalar(sm[:, 1:2], sm[:, 0:1], -1.0, None, ALU.mult).then_inc(d_smax.sem, 1)
                if not last:
                    v_ahead(b + 1)
                dve.wait_ge(a_sm.sem, a_sm.after(b, 1))
                then(dve.reciprocal(sm[:, 3:4], sm[:, 2:3]))
                dve.tensor_scalar(probT[0:E, :], probT[0:E, :], sm[:, 3:4], None, ALU.mult).then_inc(d_prob.sem, 1)
                dve.wait_ge(e_route1.sem, e_route1.after(b, 2))
                step(dve.tensor_copy(lg[:, :, :], bank(3)[:, 0:NQ].rearrange("p (t n) -> p t n", t=TQ)[:, :, 0:E]))
                top8(lg)
                for t in range(TQ):
                    ins = dve.tensor_scalar(maskb[:, t, :, :].rearrange("p e d -> p (e d)"),
                                            iota_ed[:, :, :].rearrange("p e d -> p (e d)"), topf[:, t, 0:1], None,
                                            ALU.is_equal)
                    if t < TQ - 1:
                        step(ins)
                ins.then_inc(d_mask.sem, 1)
                for t in range(TQ):
                    ins = dve.tensor_scalar(maskp[:, t, :], iota_col[:, :], topf[:, t, 0:1], None, ALU.is_equal)
                    if t < TQ - 1:
                        step(ins)
                ins.then_inc(d_mask.sem, 1)
                for n in range(2):
                    dve.wait_ge(e_route1.sem, e_route1.after(b, 3 + n))
                    dve.tensor_tensor(xm[:, 4 * n:4 * n + 4, :],
                                      bank((0, 4)[n], 2).rearrange("p (e q) -> p e q", e=4),
                                      xT[:, :].rearrange("p (o q) -> p o q", o=1).to_broadcast([P, 4, NQ]),
                                      ALU.mult).then_inc(d_xm.sem, 1)
                if not last:
                    for p in range(AHEAD_PAIRS):
                        keys_low(b + 1, p)
                    stack_ahead(b + 1)
                dve.wait_ge(d_mask.sem, d_mask.after(b, 2))
                for t in range(TQ):
                    for n in range(2):
                        dve.wait_ge(e_out1.sem, e_out1.after(b, 2 * t + n + 1))
                        then(dve.tensor_tensor(
                            sel[:, 4 * n:4 * n + 4, :], bank((0, 6)[t] + n).rearrange("p (e d) -> p e d", d=P),
                            maskp[:, t, 4 * n:4 * n + 4].rearrange("p (e o) -> p e o", o=1).to_broadcast([P, 4, P]),
                            ALU.mult))
                        if n == 0:
                            then(dve.tensor_reduce(ysum[:, t, :], sel[:, 0:4, :].rearrange("p e d -> p d e"), AX,
                                                   ALU.add))
                            then(dve.tensor_tensor(sel[:, E, :], bank(4 + t)[:, 0:P], ysum[:, t, :], ALU.add))
                    ins = dve.tensor_reduce(ysum[:, t, :], sel[:, 4:E + 1, :].rearrange("p e d -> p d e"), AX, ALU.add)
                    if t == 0:
                        ins.then_inc(d_sel.sem, 1)
                        dve.wait_ge(d_sel.sem, d_sel.after(b, 1))
                    else:
                        then(ins)
                dve.scalar_tensor_tensor(out=xr[:, :, :], in0=ysum, scalar=G_F1, in1=xr[:, :, :],
                                         op0=ALU.mult, op1=ALU.add).then_inc(d_x.sem, 1)
                assert count[d_step] == DVE_STEPS, count[d_step]

            with dve.Fori(0, B - 1) as b:
                batch(b, False)
            batch(B - 1, True)

        @block.tensor
        def _(pe):
            def mm(o, lhsT, rhs, start=True, stop=True):
                return pe.matmul(o, lhsT, rhs, start=start, stop=stop)

            def mm_split(o, lhs_hl, rhs_hl, start=True, stop=True):
                (lh, ll), (rh, rl) = lhs_hl, rhs_hl
                mm(o, lh, rh, start, False)
                mm(o, lh, rl, False, False)
                return mm(o, ll, rh, False, stop)

            def weights_in(n):
                if n >= 2:
                    pe.wait_ge(s_wT_copied.sem, n - 1)
                for m in range(4 * n, min(4 * n + 4, NT)):
                    ins = pe.transpose(bank(6 + n % 2)[:, (m % 4) * P:(m % 4 + 1) * P], raw[:, m, :], ident[:, :])
                ins.then_inc(s_wT.sem, 1)

            def tok(a, t):
                return a[:, t * P:(t + 1) * P]

            def transpose_tiles(o, of, tiles):
                for t in range(tiles):
                    ins = pe.transpose(tok(o, t), of[:, t, :], ident[:, :])
                return ins

            def transposes_ahead(n):
                pe.wait_ge(s_ctx.sem, s_ctx.after(n, 16))
                transpose_tiles(bank(1), ctx_in, TC).then_inc(e_ctxT.sem, 1)
                pe.wait_ge(d_xn0.sem, d_xn0.after(n, 1))
                transpose_tiles(bank(0), xn0, TQ).then_inc(e_xT0.sem, 1)

            def context_ahead(n):
                pe.wait_ge(g_cn.sem, g_cn.after(n, 1))
                transpose_tiles(bank(2), cn, TC).then_inc(e_cnT.sem, 1)

            def project_keys(n, p):
                mm_split(bank(KEY_BANK[p]), (wkv_h[:, 0, p, :], wkv_l[:, 0, p, :]),
                         (kv_h[:, 0:NC_], kv_l[:, 0:NC_])).then_inc(e_k.sem, 1)

            def qkv_ahead(n):
                pe.wait_ge(a_ctxT.sem, a_ctxT.after(n, 1))
                for t in range(TC):
                    mm(bank(4, 2)[:, t * 2 * P:(t + 1) * 2 * P], tok(ctxT, t),
                       wt[:, W_K0:W_V0 + 1, :].rearrange("p n d -> p (n d)"))
                pe.wait_ge(a_xT0.sem, a_xT0.after(n, 1))
                for t in range(TQ):
                    ins = mm(tok(bank(3), t), tok(xT0, t), wt[:, W_Q0, :])
                ins.then_inc(e_qkv0.sem, 1)

            pe.wait_ge(s_const.sem, 2)
            pe.wait_ge(s_first.sem, 16 * FIRST_LOADS)
            weights_in(0)
            transposes_ahead(0)
            pe.wait_ge(s_wT_copied.sem, 1)
            qkv_ahead(0)
            context_ahead(0)
            pe.wait_ge(s_raw.sem, 16 * RAW_LOADS)
            for n in range(1, 8):
                weights_in(n)
            pe.wait_ge(s_wT_copied.sem, 7)
            pe.transpose(bank(6)[:, 0:E], gate0_raw, ident[0:E, 0:E]).then_inc(s_wT.sem, 1)
            pe.wait_ge(s_wT_copied.sem, 9)
            pe.wait_ge(s_const.sem, 3)
            pe.wait_ge(s_wlow.sem, 3)
            pe.wait_ge(s_small.sem, 16 * SMALL_LOADS)
            pe.wait_ge(d_cL.sem, d_cL.after(0, 1))
            for p in range(AHEAD_PAIRS):
                project_keys(0, p)

            def batch(b, last):
                pe.wait_ge(d_cL.sem, d_cL.after(b, 1))
                pe.wait_ge(d_stack.sem, d_stack.after(b, 1))
                pe.wait_ge(g_pad.sem, g_pad.after(b, 1))
                pe.wait_ge(d_qkv0.sem, d_qkv0.after(b, 1))
                pe.wait_ge(d_sel.sem, d_sel.after(b, 0))

                def stacked(n):
                    if n in ACT_STACKS:
                        pe.wait_ge(a_kq.sem, a_kq.after(b, sum(h <= n for h in ACT_STACKS)))
                    else:
                        pe.wait_ge(d_kq.sem, d_kq.after(b, sum(h not in ACT_STACKS for h in range(n + 1))))

                for n in range(H):
                    if n == 8:
                        pe.wait_ge(d_x.sem, d_x.after(b, 0))
                        pe.wait_ge(d_kL.sem, d_kL.after(b, AHEAD_PAIRS))
                    if n in (4, 5, 6, 7, 12, 13, 14, 15):
                        stacked(n - 4)
                    for t in range(TK):
                        ins = pe.transpose(bank(STACK_BANK[n])[0:SK, 0:384].bitcast(BF16)[:, t * P:(t + 1) * P],
                                           stack[:, t * H + n, :], identb[:, :])
                    ins.then_inc(e_kq.sem, 1)
                for n in (6, 7):
                    stacked(n)

                def max0(h):
                    if h >= 2:
                        pe.wait_ge(d_max0.sem, d_max0.after(b, h - 1))
                    for t in range(TQ):
                        ins = mm(bank(2 * (h % 2) + t), kq[0:SK, h, NC_ + t * P:NC_ + (t + 1) * P],
                                 kq[0:SK, h, 0:NC_])
                    ins.then_inc(e_max0.sem, 1)

                def scores0(h):
                    pe.wait_ge(g_diag0.sem, g_diag0.after(b, h + 1))
                    for half in range(2):
                        if h >= 1:
                            pe.wait_ge(a_exp0.sem, a_exp0.after(b, 2 * h - 1 + half))
                        for k in (2 * half, 2 * half + 1):
                            o = bank(4 + half)[:, k % 2 * NQ:(k % 2 + 1) * NQ]
                            mm(o, kq[0:SK, h, k * P:(k + 1) * P], kq[0:SK, h, NC_:NK], True, False)
                            ins = mm(o, onesb[:, :], diag[:, h % DG0, :, :].rearrange("p t q -> p (t q)"), False, True)
                        ins.then_inc(e_st0.sem, 1)

                def values0(g, half):
                    pe.wait_ge(a_exp0.sem, a_exp0.after(b, 2 * QUAD * (g + 1)))
                    if g >= 2:
                        pe.wait_ge(a_o0.sem, a_o0.after(b, g - 1))
                    for k in (2 * half, 2 * half + 1):
                        for j in range(QUAD):
                            h = QUAD * g + j
                            ins = mm(bank(6 + g % 2)[32 * j:32 * j + 32, 0:NQ], v0[:, k, h * V0W:h * V0W + 32],
                                     p0[:, h % PR0, k, :], k == 0, k == TC - 1)
                    if half == 1:
                        ins.then_inc(e_pv0.sem, 1)

                def values_in(t, first):
                    for n in range(2):
                        ins = mm_split(bank(first + n), (tok(kv_h, t), tok(kv_l, t)),
                                       tuple(w[:, 1, 4 * n:4 * n + 4, :].rearrange("p n d -> p (n d)")
                                             for w in (wkv_h, wkv_l)))
                    ins.then_inc(e_v.sem, 1)

                for h in range(MAX_AHEAD):
                    max0(h)
                for n in range(12, H):
                    stacked(n)
                for h in range(H):
                    scores0(h)
                    if h + MAX_AHEAD < H:
                        max0(h + MAX_AHEAD)
                    if h in LOOP_KEYS:
                        p = LOOP_KEYS[h]
                        before = max(q for q in range(p) if KEY_BANK[q] == KEY_BANK[p])
                        pe.wait_ge(d_kL.sem, d_kL.after(b, before + 1))
                        project_keys(b, p)
                    if h == QUAD:
                        pe.wait_ge(d_kL.sem, d_kL.after(b, 5))
                    if h == 2 * QUAD:
                        pe.wait_ge(d_kL.sem, d_kL.after(b, NPAIR - len(LATE_KEYS)))
                    if h % QUAD <= 1 and h >= QUAD:
                        values0(h // QUAD - 1, h % QUAD)

                def outputs0(g):
                    for t in range(TQ):
                        ins = pe.transpose(bank(t)[:, g * P:(g + 1) * P], o0[:, g, t * P:(t + 1) * P], ident[:, :])
                    return ins

                pe.wait_ge(a_o0.sem, a_o0.after(b, NQUAD - 1))
                pe.wait_ge(d_max0.sem, d_max0.after(b, H))
                for g in range(NQUAD - 1):
                    outputs0(g)
                values0(NQUAD - 1, 0)
                values0(NQUAD - 1, 1)
                pe.wait_ge(a_o0.sem, a_o0.after(b, NQUAD))
                outputs0(NQUAD - 1).then_inc(e_o0.sem, 1)
                values_in(0, V_BANK[0])
                pe.wait_ge(d_o0.sem, d_o0.after(b, 1))
                transpose_tiles(bank(2), o0_tok, TQ).then_inc(e_o0.sem, 1)
                values_in(1, V_BANK[1])
                pe.wait_ge(a_oT.sem, a_oT.after(b, 1))
                for t in range(TQ):
                    ins = mm(tok(bank(3), t), tok(o0_T, t), wt[:, W_PROJ, :])
                ins.then_inc(e_o0.sem, 1)
                values_in(2, V_BANK[2])
                project_keys(b, LATE_KEYS[0])

                pe.wait_ge(d_xn.sem, d_xn.after(b, 1))
                pe.wait_ge(a_v.sem, a_v.after(b, 2))
                transpose_tiles(bank(4), xn, TQ).then_inc(e_xT.sem, 1)
                pe.wait_ge(a_xT.sem, a_xT.after(b, 1))
                for t in range(TQ):
                    ins = mm(bank(5)[:, t * E:(t + 1) * E], tok(xT, t), gate0[:, :])
                ins.then_inc(e_route0.sem, 1)
                for u, w in enumerate((W_A1, W_A3)):
                    ins = mm(bank(6)[:, u * NQ:(u + 1) * NQ], wt[:, w, :], xT[:, :])
                ins.then_inc(e_route0.sem, 1)
                pe.wait_ge(a_kH.sem, a_kH.after(b, LATE_KEYS[0] + 1))
                pe.wait_ge(a_v.sem, a_v.after(b, 3))
                for n, w in enumerate((W_GATE, W_GATE + 2, W_UP, W_UP + 2)):
                    for c in range(2):
                        ins = mm(bank(n)[:, c * NQ:(c + 1) * NQ], wt[:, w + c, :], xT[:, :])
                    ins.then_inc(e_common.sem, 1)
                pe.wait_ge(d_exm.sem, d_exm.after(b, 1))
                for j in range(2):
                    for t in range(TQ):
                        ins = pe.transpose(bank(7)[:, (j * TQ + t) * P:(j * TQ + t + 1) * P], exm[:, j, t, :],
                                           ident[:, :])
                ins.then_inc(e_route0.sem, 1)
                pe.wait_ge(a_common.sem, a_common.after(b, 4))
                for s in range(4):
                    pe.wait_ge(d_um.sem, d_um.after(b, s // 2 + 1))
                    if s >= 2:
                        pe.wait_ge(d_usum.sem, d_usum.after(b, s - 1))
                    for u, wb in enumerate((W_B1, W_B3)):
                        for c in range(2):
                            ins = mm(bank(2 * (s % 2) + u)[:, c * NQ:(c + 1) * NQ], wt[:, wb + 2 * (s % 2) + c, :],
                                     um[:, u, s // 2, :])
                    ins.then_inc(e_pre0.sem, 1)
                for j in range(2):
                    pe.wait_ge(d_hid0.sem, d_hid0.after(b, 2 * j + 2))
                    for t in range(TQ):
                        for c in range(FC):
                            ins = mm(bank(4 + j)[:, t * 2 * P:(t + 1) * 2 * P], hid0[:, j, c, t * P:(t + 1) * P],
                                     wt[:, W_DOWN + 2 * c:W_DOWN + 2 * c + 2, :].rearrange("p n d -> p (n d)"),
                                     c == 0, c == FC - 1)
                    ins.then_inc(e_down0.sem, 1)
                values_in(3, V_BANK[3])
                pe.wait_ge(d_zm.sem, d_zm.after(b, 1))
                transpose_tiles(bank(6), zm[:, 0, :, :], TQ).then_inc(e_z.sem, 1)
                pe.wait_ge(a_zT.sem, a_zT.after(b, 1))
                for t in range(TQ):
                    ins = mm(tok(bank(7), t), tok(zT, t), wt[:, W_B2, :])
                ins.then_inc(e_z.sem, 1)

                for p in LATE_KEYS[1:]:
                    project_keys(b, p)
                pe.wait_ge(d_xn.sem, d_xn.after(b, 2))
                transpose_tiles(bank(0), xn, TQ).then_inc(e_xT.sem, 1)
                pe.wait_ge(a_latH.sem, a_latH.after(b, 1))
                lat = (kv_h[:, NC_:NK], kv_l[:, NC_:NK])

                def keys_of_latents(r):
                    for n in range(2):
                        o = bank(KLAT_BANK[r])[:, n * NQ:(n + 1) * NQ]
                        w = wkv_h[:, 0, 2 * r + n, :], wkv_l[:, 0, 2 * r + n, :]
                        mm(o, w[0], lat[0], True, False)
                        mm(o, w[1], lat[0], False, False)
                        if (r, n) == (0, 0):
                            pe.wait_ge(d_latL.sem, d_latL.after(b, 1))
                        ins = mm(o, w[0], lat[1], False, True)
                    ins.then_inc(e_klat.sem, 1)

                def project_q(m):
                    mm_split(q_bank(m), (wq_h[:, m, :], wq_l[:, m, :]), lat).then_inc(e_q.sem, 1)

                def max1(h):
                    pe.wait_ge(d_qL.sem, d_qL.after(b, h // 2 + 1))
                    if h == 0:
                        pe.wait_ge(a_kH.sem, a_kH.after(b, NPAIR))
                    if h // 2 in LATE_KEYS and h % 2 == 0:
                        pe.wait_ge(g_kL.sem, g_kL.after(b, LATE_KEYS.index(h // 2) + 1))
                    if h % 4 == 0 and h // 4 >= KLAT_DVE:
                        pe.wait_ge(g_klat.sem, g_klat.after(b, h // 4 - KLAT_DVE + 1))
                    if h >= 1:
                        pe.wait_ge(d_max1.sem, d_max1.after(b, h))
                    cuts = sorted({0, BANK, 2 * BANK, 3 * BANK, NK})
                    for lo, hi in zip(cuts, cuts[1:]):
                        t, k = lo // NK, lo % NK
                        ins = mm(bank(0, 3)[:, lo:hi], q_h[:, (h // 2) % 2, h % 2, t * P:(t + 1) * P],
                                 keys[:, h, k:k + hi - lo])
                    ins.then_inc(e_max1.sem, 1)

                keys_of_latents(0)
                project_q(0)
                keys_of_latents(1)
                pe.wait_ge(a_kH.sem, a_kH.after(b, NPAIR))
                keys_of_latents(2)
                pe.wait_ge(d_klat.sem, d_klat.after(b, 1))
                max1(0)
                pe.wait_ge(d_klat.sem, d_klat.after(b, 2))
                values_in(TC, V_BANK[TC])
                project_q(1)
                keys_of_latents(3)
                max1(1)

                def scores1(h):
                    pe.wait_ge(d_diag1.sem, d_diag1.after(b, h + 1))
                    for n in range(3):
                        if h == 0 and n == 0:
                            pe.wait_ge(a_v.sem, a_v.after(b, TC + 1))
                            pe.wait_ge(a_klat.sem, a_klat.after(b, 3))
                        if h >= 1:
                            pe.wait_ge(a_exp1.sem, a_exp1.after(b, 3 * h - 2 + n))
                        for k in (2 * n, 2 * n + 1):
                            o = bank(3, 3)[:, k * NQ:(k + 1) * NQ]
                            mm(o, keys[:, h, k * P:(k + 1) * P], q_h[:, (h // 2) % 2, h % 2, :], True, False)
                            mm(o, keys[:, h, k * P:(k + 1) * P], q_l[:, (h // 2) % 2, h % 2, :], False, False)
                            ins = mm(o, onesb[:, :], diag[:, h % 2, :, :].rearrange("p t q -> p (t q)"), False, True)
                        ins.then_inc(e_st1.sem, 1)

                def values1(p):
                    pe.wait_ge(a_exp1.sem, a_exp1.after(b, 3 * (2 * p + 2)))
                    pe.wait_ge(d_qL.sem, d_qL.after(b, min(p + 2, NPAIR)))
                    pe.wait_ge(a_v.sem, a_v.after(b, TK))
                    if p >= 2:
                        pe.wait_ge(d_o1.sem, d_o1.after(b, p - 1))
                    for k in range(TK):
                        for j in range(2):
                            h = 2 * p + j
                            ins = mm(bank(6 + p % 2)[j * D1:(j + 1) * D1, 0:NQ], v1[:, k, h * D1:(h + 1) * D1],
                                     p1[:, h % PR1, k * NQ:(k + 1) * NQ], k == 0, k == TK - 1)
                    ins.then_inc(e_pv1.sem, 1)

                def sums1(p):
                    pe.wait_ge(d_qL.sem, d_qL.after(b, min(p + 4, NPAIR)))
                    if p < NPAIR - 1:
                        pe.wait_ge(g_sum.sem, g_sum.after(b, 2 * p + 2))
                        for j in range(2):
                            ins = mm(bank(6 + p % 2)[j * D1:(j + 1) * D1, NQ:2 * NQ], onesf[:, :], psum_1[:, j, :])
                    else:
                        for k in range(TK):
                            for j in range(2):
                                ins = mm(bank(6 + p % 2)[j * D1:(j + 1) * D1, NQ:2 * NQ], onesf[:, :],
                                         p1[:, (2 * p + j) % PR1, k * NQ:(k + 1) * NQ], k == 0, k == TK - 1)
                    ins.then_inc(e_den1.sem, 1)

                for i in range(H + 2):
                    if 2 <= i < H:
                        max1(i)
                    if 1 <= i <= H:
                        scores1(i - 1)
                    if i == H and not last:
                        pe.wait_ge(d_max1.sem, d_max1.after(b, H))
                        transposes_ahead(b + 1)
                        context_ahead(b + 1)
                    if i % 2 == 1 and i >= 3:
                        p = (i - 3) // 2
                        values1(p)
                        if p >= 1:
                            sums1(p - 1)
                        if p == NPAIR - 1:
                            sums1(p)
                    if i == 1:
                        pe.wait_ge(d_qL.sem, d_qL.after(b, 2))
                        pe.wait_ge(a_klat.sem, a_klat.after(b, 4))
                        values_in(TC + 1, V_BANK[TC + 1])
                    if i == 2:
                        pe.wait_ge(a_v.sem, a_v.after(b, TK))
                        project_q(2)
                    if i % 2 == 1 and 2 < (i + 3) // 2 < NPAIR:
                        project_q((i + 3) // 2)
                pe.wait_ge(d_max1.sem, d_max1.after(b, H))
                if not last:
                    pe.wait_ge(d_cL.sem, d_cL.after(b + 1, 1))
                for p in range(NPAIR):
                    pe.wait_ge(d_o1.sem, d_o1.after(b, p + 1))
                    ins = mm(bank(0)[:, 0:NQ], wout[:, p, :], o1[:, p, :], p == 0, p == NPAIR - 1)
                ins.then_inc(e_y1.sem, 1)
                pe.wait_ge(a_yT.sem, a_yT.after(b, 1))
                transpose_tiles(bank(1), yT.rearrange("p (t d) -> p t d", t=TQ), TQ).then_inc(e_y1.sem, 1)

                if not last:
                    qkv_ahead(b + 1)
                    for p in range(AHEAD_PAIRS):
                        project_keys(b + 1, p)

                pe.wait_ge(d_xn.sem, d_xn.after(b, 3))
                transpose_tiles(bank(2), xn, TQ).then_inc(e_xT.sem, 1)
                pe.wait_ge(a_xT.sem, a_xT.after(b, 2))
                mm(bank(2)[0:E, NQ:2 * NQ], gate1[:, :], xT[:, :]).then_inc(e_route1.sem, 1)
                pe.wait_ge(d_prob.sem, d_prob.after(b, 1))
                transpose_tiles(bank(3), probT.rearrange("p (t d) -> p t d", t=TQ), TQ).then_inc(e_route1.sem, 1)
                pe.wait_ge(d_mask.sem, d_mask.after(b, 1))
                for n in range(2):
                    if n == 1 and not last:
                        pe.wait_ge(d_qkv0.sem, d_qkv0.after(b + 1, 1))
                    for e in range(4):
                        for t in range(TQ):
                            ins = mm(bank((0, 4)[n], 2)[:, e * NQ + t * P:e * NQ + (t + 1) * P],
                                     maskb[:, t, 4 * n + e, :], identb[:, :])
                    ins.then_inc(e_route1.sem, 1)
                pe.wait_ge(d_mask.sem, d_mask.after(b, 2))
                transpose_tiles(bank(3)[:, NQ:2 * NQ], maskp, TQ).then_inc(e_route1.sem, 1)
                for c in range(FC):
                    o = bank(2 + c // 2)[:, (c % 2) * NQ:(c % 2 + 1) * NQ]
                    for e in range(E):
                        if c == 0 and e % 4 == 0:
                            pe.wait_ge(d_xm.sem, d_xm.after(b, e // 4 + 1))
                        mm(o, w1[:, e, c * P:(c + 1) * P], xm[:, e, :], e == 0, False)
                    if c == 0:
                        pe.wait_ge(a_maskT.sem, a_maskT.after(b, 1))
                    ins = mm(o, b1[:, c * P:(c + 1) * P], maskT, False, True)
                    if c % 2 == 1:
                        ins.then_inc(e_pre1.sem, 1)
                for t in range(TQ):
                    mm(bank(4 + t)[:, 0:P], maskT[:, t * P:(t + 1) * P], b2[:, :])
                pe.wait_ge(a_gelu.sem, a_gelu.after(b, 2))
                if not last:
                    pe.wait_ge(d_kL.sem, d_kL.after(b + 1, AHEAD_PAIRS))
                pe.wait_ge(g_w2L.sem, g_w2L.after(b, FC))
                pe.wait_ge(g_hidL.sem, g_hidL.after(b, 1))
                for t in range(TQ):
                    for n in range(2):
                        o = bank((0, 6)[t] + n)
                        cols = slice(n * BANK, (n + 1) * BANK)
                        for c in range(2):
                            mm_split(o, (tok(hid1_h[:, c, :], t), tok(hid1_l[:, c, :], t)),
                                     (w2_h[:, c, cols], w2_l[:, c, cols]), c == 0, False)
                        pe.wait_ge(a_hidH.sem, a_hidH.after(b, 2))
                        for c in (2, 3):
                            mm(o, tok(hid1_h[:, c, :], t), w2_h[:, c, cols], False, False)
                            mm(o, tok(hid1_h[:, c, :], t), w2_l[:, c, cols], False, False)
                        pe.wait_ge(g_hidL.sem, g_hidL.after(b, 2))
                        for c in (2, 3):
                            ins = mm(o, tok(hid1_l[:, c, :], t), w2_h[:, c, cols], False, c == 3)
                        ins.then_inc(e_out1.sem, 1)

            with pe.Fori(0, B - 1) as b:
                batch(b, False)
            batch(B - 1, True)


FIRST_LOADS = 3
BIAS_LOADS = 8
RAW_LOADS = 16
SMALL_LOADS = 11

_INS = ['x', 'ctx_1024', 'g_xattn', 'g_ffn', 'L0_xattn_Wq', 'L0_xattn_bq', 'L0_xattn_Wkv', 'L0_xattn_bkv',
        'L0_xattn_q_gamma', 'L0_xattn_q_beta', 'L0_xattn_k_gamma', 'L0_xattn_k_beta', 'L0_xattn_Wproj',
        'L0_xattn_bproj', 'L0_ffn_gate_w', 'L0_ffn_w_gate', 'L0_ffn_w_up', 'L0_ffn_w_down', 'L0_ffn_A1',
        'L0_ffn_B1', 'L0_ffn_A3', 'L0_ffn_B3', 'L0_ffn_A2', 'L0_ffn_B2', 'L1_xattn_ln_m_g', 'L1_xattn_ln_m_b',
        'L1_xattn_ln_l_g', 'L1_xattn_ln_l_b', 'L1_xattn_Wq', 'L1_xattn_Wkv', 'L1_xattn_Wout', 'L1_ffn_gate_w',
        'L1_ffn_gate_b', 'L1_ffn_W1', 'L1_ffn_b1', 'L1_ffn_W2', 'L1_ffn_b2']
_OUT = ((4, 256, 128), 'float32')


def kernel(**inputs):
    import numpy as _np
    import concourse.bacc as _bacc
    from concourse import mybir as _mybir
    from concourse.bass_utils import run_bass_kernel_spmd as _run

    nc = _bacc.Bacc("TRN2", target_bir_lowering=False, num_devices=1)
    arrays, args = {}, {}
    for name in _INS:
        a = _np.ascontiguousarray(inputs[name])
        arrays[f"in_{name}_dram"] = a
        args[name] = nc.dram_tensor(f"in_{name}_dram", a.shape, _mybir.dt.from_np(a.dtype), kind="ExternalInput").ap()
    out = nc.dram_tensor("out_0_dram", _OUT[0], _mybir.dt.from_np(_np.dtype(_OUT[1])), kind="ExternalOutput").ap()
    flamingo(nc, args, out)
    r = _run(nc, [arrays], core_ids=[0])
    return r.results[0]["out_0_dram"]
```
